# Optimizing a Trainium2 kernel written in Bass

```python
import numpy as np
import jax
import jax.numpy as jnp

def _softmax(x, axis=-1):
    return jax.nn.softmax(x, axis=axis)

def _gelu(x):
    return jax.nn.gelu(x, approximate=True)

def _silu(x):
    return jax.nn.silu(x)

def _sigmoid(x):
    return jax.nn.sigmoid(x)

def _layernorm(x, axis=-1, eps=1e-05):
    m = jnp.mean(x, axis=axis, keepdims=True)
    v = jnp.var(x, axis=axis, keepdims=True)
    return (x - m) / jnp.sqrt(v + eps)

def _scatter_add(tgt, idx, src, axis=0):
    return tgt.at[idx].add(src)

def _segment_sum(src, seg, n):
    return jax.ops.segment_sum(src, seg, n)
kernel_name = 'mk_vit_tower_d1_tok_img512_r4_b00faf'

def setup_inputs(seed: int=0):
    np.random.seed(seed)
    _w = jnp.asarray

    def _rec_inputs():
        import jax
        import jax.numpy as jnp
        _rk = jax.random.key(seed)
        x = -0.000190493 + 0.999948 * jax.random.normal(jax.random.fold_in(_rk, 1), (128, 2, 104, 104), jnp.float32)
        return x
    x = _rec_inputs()

    def _L0_tok_setup():
        import jax, jax.numpy as jnp
        import numpy as np
        HP = 4
        PATCH = 8
        EPS = 1e-07

        def _shifts(x):
            h, w = (x.shape[2], x.shape[3])
            pad2 = ((0, 0), (0, 0))
            left_up = jnp.pad(x[:, :, HP:, :w - HP], pad2 + ((0, HP), (HP, 0)))
            right_up = jnp.pad(x[:, :, HP:, HP:], pad2 + ((0, HP), (0, HP)))
            left_down = jnp.pad(x[:, :, :h - HP, :w - HP], pad2 + ((HP, 0), (HP, 0)))
            right_down = jnp.pad(x[:, :, :h - HP, HP:], pad2 + ((HP, 0), (0, HP)))
            return (left_up, right_up, left_down, right_down)
        key = jax.random.key(seed)
        k1, k2, k3, k4 = jax.random.split(key, 4)
        B, C, S = (128, 2, 104)
        embed_dim = 128
        x = jax.random.normal(k1, (B, C, S, S), dtype=jnp.float32)
        gamma = 1.0 + 0.05 * jax.random.normal(k2, (10, S, S), dtype=jnp.float32)
        beta = 0.05 * jax.random.normal(k3, (10, S, S), dtype=jnp.float32)
        W = 0.02 * jax.random.normal(k4, (embed_dim, 10, PATCH, PATCH), dtype=jnp.float32)
        b = jnp.zeros((embed_dim,), dtype=jnp.float32)
        return {'x': x, 'gamma': gamma, 'beta': beta, 'W': W, 'b': b}
    _L0_tok_all = _L0_tok_setup()
    _L0_tok_in = {k: v for k, v in _L0_tok_all.items() if k in ('gamma', 'beta', 'W', 'b')}
    del _L0_tok_all

    def _L0_attn_setup():
        import jax, jax.numpy as jnp
        import numpy as np
        import math
        E = 128
        H = 8
        D = E // H
        C = 32
        NH = 5
        B, S = (4, 512)
        key = jax.random.key(seed)
        k0, k1, k2, k3 = jax.random.split(key, 4)
        x = jax.random.normal(k0, (B, S, E), jnp.float32)
        Wq = jax.random.normal(k1, (E, E), jnp.float32) * 0.02
        bq = jnp.zeros((E,), jnp.float32)
        Wv = jax.random.normal(k2, (E, E), jnp.float32) * 0.02
        bv = jnp.zeros((E,), jnp.float32)
        hyperplanes = jax.random.normal(k3, (D + 1, NH), jnp.float32)
        return {'x': x, 'Wq': Wq, 'bq': bq, 'Wv': Wv, 'bv': bv, 'hyperplanes': hyperplanes}
    _L0_attn_all = _L0_attn_setup()
    _L0_attn_in = {k: v for k, v in _L0_attn_all.items() if k in ('Wq', 'bq', 'Wv', 'bv', 'hyperplanes')}
    del _L0_attn_all

    def _L0_ffn_setup():
        import jax, jax.numpy as jnp
        import numpy as np
        B, S, D, H, E = (4, 512, 128, 8, 8)
        FF = 4 * D
        HD = D // H
        EPS = 1e-05

        def _layernorm(x, g, b):
            mu = jnp.mean(x, axis=-1, keepdims=True)
            var = jnp.mean((x - mu) ** 2, axis=-1, keepdims=True)
            return (x - mu) * jax.lax.rsqrt(var + EPS) * g + b
        key = jax.random.key(seed)
        ks = jax.random.split(key, 16)
        s = 0.02
        return {'x': jax.random.normal(ks[0], (B, S, D), dtype=jnp.float32), 'ln1_g': jnp.ones((D,), jnp.float32), 'ln1_b': jnp.zeros((D,), jnp.float32), 'Wq': jax.random.normal(ks[1], (D, D), jnp.float32) * s, 'bq': jnp.zeros((D,), jnp.float32), 'Wk': jax.random.normal(ks[2], (D, D), jnp.float32) * s, 'bk': jnp.zeros((D,), jnp.float32), 'Wv': jax.random.normal(ks[3], (D, D), jnp.float32) * s, 'bv': jnp.zeros((D,), jnp.float32), 'Wo': jax.random.normal(ks[4], (D, D), jnp.float32) * s, 'bo': jnp.zeros((D,), jnp.float32), 'gate_W': jax.random.normal(ks[5], (D, E), jnp.float32) * s, 'gate_b': jnp.zeros((E,), jnp.float32), 'W1': jax.random.normal(ks[6], (E, D, FF), jnp.float32) * s, 'b1': jnp.zeros((E, FF), jnp.float32), 'W2': jax.random.normal(ks[7], (E, FF, D), jnp.float32) * s, 'b2': jnp.zeros((E, D), jnp.float32)}
    _L0_ffn_all = _L0_ffn_setup()
    _L0_ffn_in = {k: v for k, v in _L0_ffn_all.items() if k in ('ln1_g', 'ln1_b', 'Wq', 'bq', 'Wk', 'bk', 'Wv', 'bv', 'Wo', 'bo', 'gate_W', 'gate_b', 'W1', 'b1', 'W2', 'b2')}
    del _L0_ffn_all
    return {'x': x, 'L0_tok_gamma': _L0_tok_in['gamma'], 'L0_tok_beta': _L0_tok_in['beta'], 'L0_tok_W': _L0_tok_in['W'], 'L0_tok_b': _L0_tok_in['b'], 'L0_attn_Wq': _L0_attn_in['Wq'], 'L0_attn_bq': _L0_attn_in['bq'], 'L0_attn_Wv': _L0_attn_in['Wv'], 'L0_attn_bv': _L0_attn_in['bv'], 'L0_attn_hyperplanes': _L0_attn_in['hyperplanes'], 'L0_ffn_ln1_g': _L0_ffn_in['ln1_g'], 'L0_ffn_ln1_b': _L0_ffn_in['ln1_b'], 'L0_ffn_Wq': _L0_ffn_in['Wq'], 'L0_ffn_bq': _L0_ffn_in['bq'], 'L0_ffn_Wk': _L0_ffn_in['Wk'], 'L0_ffn_bk': _L0_ffn_in['bk'], 'L0_ffn_Wv': _L0_ffn_in['Wv'], 'L0_ffn_bv': _L0_ffn_in['bv'], 'L0_ffn_Wo': _L0_ffn_in['Wo'], 'L0_ffn_bo': _L0_ffn_in['bo'], 'L0_ffn_gate_W': _L0_ffn_in['gate_W'], 'L0_ffn_gate_b': _L0_ffn_in['gate_b'], 'L0_ffn_W1': _L0_ffn_in['W1'], 'L0_ffn_b1': _L0_ffn_in['b1'], 'L0_ffn_W2': _L0_ffn_in['W2'], 'L0_ffn_b2': _L0_ffn_in['b2']}

def reference(x, L0_tok_gamma, L0_tok_beta, L0_tok_W, L0_tok_b, L0_attn_Wq, L0_attn_bq, L0_attn_Wv, L0_attn_bv, L0_attn_hyperplanes, L0_ffn_ln1_g, L0_ffn_ln1_b, L0_ffn_Wq, L0_ffn_bq, L0_ffn_Wk, L0_ffn_bk, L0_ffn_Wv, L0_ffn_bv, L0_ffn_Wo, L0_ffn_bo, L0_ffn_gate_W, L0_ffn_gate_b, L0_ffn_W1, L0_ffn_b1, L0_ffn_W2, L0_ffn_b2):
    import jax
    import jax.numpy as jnp

    def _L0_tok_ref(x, gamma, beta, W, b):
        import jax, jax.numpy as jnp
        import numpy as np
        HP = 4
        PATCH = 8
        EPS = 1e-07

        def _shifts(x):
            h, w = (x.shape[2], x.shape[3])
            pad2 = ((0, 0), (0, 0))
            left_up = jnp.pad(x[:, :, HP:, :w - HP], pad2 + ((0, HP), (HP, 0)))
            right_up = jnp.pad(x[:, :, HP:, HP:], pad2 + ((0, HP), (0, HP)))
            left_down = jnp.pad(x[:, :, :h - HP, :w - HP], pad2 + ((HP, 0), (HP, 0)))
            right_down = jnp.pad(x[:, :, :h - HP, HP:], pad2 + ((HP, 0), (0, HP)))
            return (left_up, right_up, left_down, right_down)
        lu, ru, ld, rd = _shifts(x)
        concat = jnp.concatenate((x, lu, ru, ld, rd), axis=1)
        mean = jnp.mean(concat, axis=(1, 2, 3), keepdims=True)
        var = jnp.var(concat, axis=(1, 2, 3), keepdims=True)
        normed = (concat - mean) * jax.lax.rsqrt(var + EPS)
        normed = normed * gamma[None] + beta[None]
        y = jax.lax.conv_general_dilated(normed, W, window_strides=(PATCH, PATCH), padding='VALID', dimension_numbers=('NCHW', 'OIHW', 'NCHW'))
        y = y + b[None, :, None, None]
        B, E = (y.shape[0], y.shape[1])
        y = y.reshape(B, E, -1).transpose(0, 2, 1)
        return y

    def _L0_attn_ref(x, Wq, bq, Wv, bv, hyperplanes):
        import jax, jax.numpy as jnp
        import numpy as np
        import math
        E = 128
        H = 8
        D = E // H
        C = 32
        NH = 5
        B, S = (4, 512)
        b_, s_, e_ = x.shape
        q = (x @ Wq + bq).reshape(b_, s_, H, D)
        v = (x @ Wv + bv).reshape(b_, s_, H, D)
        qa = jnp.concatenate([q, jnp.ones((b_, s_, H, 1), q.dtype)], axis=-1)
        proj = jnp.einsum('bshe,ey->bshy', qa, hyperplanes)
        bits = (proj >= 0).astype(jnp.int32)
        buckets = jnp.einsum('bshy,y->bsh', bits, 2 ** jnp.arange(NH, dtype=jnp.int32))
        bkt = jnp.transpose(buckets, (0, 2, 1))
        qh = jnp.transpose(q, (0, 2, 1, 3))
        vh = jnp.transpose(v, (0, 2, 1, 3))
        scores = jnp.einsum('bhid,bhjd->bhij', qh, qh) / math.sqrt(E)
        same = (bkt[:, :, :, None] == bkt[:, :, None, :]).astype(scores.dtype)
        att = jax.nn.softmax(scores * (C - 2.0 + same), axis=-1)
        out = jnp.einsum('bhij,bhjd->bhid', att, vh)
        return jnp.transpose(out, (0, 2, 1, 3)).reshape(b_, s_, e_)

    def _L0_ffn_ref(x, ln1_g, ln1_b, Wq, bq, Wk, bk, Wv, bv, Wo, bo, gate_W, gate_b, W1, b1, W2, b2):
        import jax, jax.numpy as jnp
        import numpy as np
        B, S, D, H, E = (4, 512, 128, 8, 8)
        FF = 4 * D
        HD = D // H
        EPS = 1e-05

        def _layernorm(x, g, b):
            mu = jnp.mean(x, axis=-1, keepdims=True)
            var = jnp.mean((x - mu) ** 2, axis=-1, keepdims=True)
            return (x - mu) * jax.lax.rsqrt(var + EPS) * g + b
        b, s, d = x.shape
        q = (x @ Wq + bq).reshape(b, s, H, HD)
        k = (x @ Wk + bk).reshape(b, s, H, HD)
        v = (x @ Wv + bv).reshape(b, s, H, HD)
        scores = jnp.einsum('bqhd,bkhd->bhqk', q, k) / jnp.sqrt(jnp.float32(HD))
        attn = jax.nn.softmax(scores, axis=-1)
        o = jnp.einsum('bhqk,bkhd->bqhd', attn, v).reshape(b, s, d) @ Wo + bo
        h = _layernorm(x + o, ln1_g, ln1_b)
        t = h.reshape(b * s, d)
        probs = jax.nn.softmax(t @ gate_W + gate_b, axis=-1)
        idx = jnp.argmax(probs, axis=-1)
        gw = jnp.max(probs, axis=-1)
        hid = jax.nn.gelu(jnp.einsum('nd,edf->enf', t, W1) + b1[:, None, :])
        out_all = jnp.einsum('enf,efd->end', hid, W2) + b2[:, None, :]
        onehot = jax.nn.one_hot(idx, E, dtype=t.dtype)
        out = jnp.einsum('ne,end->nd', onehot, out_all)
        out = out * gw[:, None]
        return out.reshape(b, s, d)
    h = _L0_tok_ref(x, L0_tok_gamma, L0_tok_beta, L0_tok_W, L0_tok_b)
    h = h + _L0_attn_ref(_layernorm(h, axis=-1), L0_attn_Wq, L0_attn_bq, L0_attn_Wv, L0_attn_bv, L0_attn_hyperplanes)
    h = h + _L0_ffn_ref(_layernorm(h, axis=-1), L0_ffn_ln1_g, L0_ffn_ln1_b, L0_ffn_Wq, L0_ffn_bq, L0_ffn_Wk, L0_ffn_bk, L0_ffn_Wv, L0_ffn_bv, L0_ffn_Wo, L0_ffn_bo, L0_ffn_gate_W, L0_ffn_gate_b, L0_ffn_W1, L0_ffn_b1, L0_ffn_W2, L0_ffn_b2)
    return h

_drawn_inputs = setup_inputs


def setup_inputs(seed=0):
    import zlib

    import numpy as np

    out = dict(_drawn_inputs(seed))
    spreads = {'L0_tok_b': (0.0, 0.1),
     'L0_attn_bq': (0.0, 0.585),
     'L0_attn_bv': (0.0, 0.1),
     'L0_ffn_ln1_g': (1.0, 0.6),
     'L0_ffn_ln1_b': (0.0, 0.648),
     'L0_ffn_bq': (0.0, 0.8),
     'L0_ffn_bk': (0.0, 0.8),
     'L0_ffn_bv': (0.0, 0.8),
     'L0_ffn_bo': (0.0, 0.785),
     'L0_ffn_gate_b': (0.0, 0.1),
     'L0_ffn_b1': (0.0, 0.8),
     'L0_ffn_b2': (0.0, 0.1)}
    factors = {'L0_attn_hyperplanes': 8.0,
     'L0_ffn_Wq': 8.0,
     'L0_ffn_Wk': 8.0,
     'L0_ffn_Wv': 8.0,
     'L0_ffn_Wo': 8.0,
     'L0_ffn_W1': 2.902,
     'L0_ffn_W2': 2.667}
    for name, (base, spread) in spreads.items():
        noise = np.random.default_rng([zlib.crc32(name.encode()), seed]).standard_normal(out[name].shape)
        drawn = base * np.exp(spread * noise) if base else spread * noise
        out[name] = jnp.asarray(drawn.astype(out[name].dtype))
    for name, factor in factors.items():
        out[name] = (out[name] * factor).astype(out[name].dtype)
    return out
```

```python
from contextlib import ExitStack

import concourse.bass as bass
import numpy as np
from concourse import mybir

F32 = mybir.dt.float32
BF16 = mybir.dt.bfloat16
I32 = mybir.dt.int32
U32 = mybir.dt.uint32
ALU = mybir.AluOpType
ACT = mybir.ActivationFunctionType
AX = mybir.AxisListType

IMG, CH, SIDE, HP, PATCH = 128, 2, 104, 4, 8
GRID = SIDE // PATCH
T = GRID * GRID
NBLK = GRID + 1
E = 128
H, D = 8, 16
SRC = 5
PAIRS = IMG // 2
N2 = 2 * T
TP = 192
REM = T - 128
NT = IMG * T
TILES = NT // 128
NE, FF = 8, 512
SLOTS = TILES + NE - 1
CT = 13
NC = TILES // CT
EPS_TOK, EPS_LN = 1e-7, 1e-5


def after(eng, sem, value):
    if isinstance(value, int) and value <= 0:
        return
    eng.wait_ge(sem, value)


def rsqrt(nc, eng, sem, before, v, y, t, bits):
    ops = nc.vector
    done = 0

    def link(ins):
        nonlocal done
        done += 1
        ins.then_inc(sem, 1)
        eng.wait_ge(sem, before + done)
    link(ops.tensor_scalar(bits, v.bitcast(I32), 1, None, ALU.arith_shift_right))
    link(ops.tensor_scalar(y.bitcast(I32), bits, -1.0, float(0x5F3759DF), ALU.mult, ALU.add))
    for _ in range(3):
        link(ops.tensor_tensor(t, y, y, ALU.mult))
        link(ops.scalar_tensor_tensor(t, t, -0.5, v, ALU.mult, ALU.mult))
        link(ops.scalar_tensor_tensor(y, t, 1.5, y, ALU.add, ALU.mult))
    assert done == RSQRT_OPS


RSQRT_OPS = 11


def hold(pool, passed):
    pool.sem_inc(passed, 1)


class Names:

    def __init__(self, nc, ctx, stage):
        self.nc, self.ctx, self.stage, self.sems = nc, ctx, stage, {}

    def sem(self, name):
        if name not in self.sems:
            self.sems[name] = self.ctx.enter_context(self.nc.semaphore(f"{self.stage}_{name}"))
        return self.sems[name]

    def clear(self):
        with self.nc.Block() as block:
            @block.gpsimd
            def _(pool):
                for s in self.sems.values():
                    pool.sem_clear(s)

    def sb(self, name, shape, dt=F32):
        return self.ctx.enter_context(self.nc.sbuf_tensor(f"{self.stage}_{name}", shape, dt))

    def ps(self, name, shape, dt=F32):
        return self.ctx.enter_context(self.nc.psum_tensor(f"{self.stage}_{name}", shape, dt))


def patch_tokens(nc, hT, ident, ximg, xblk, xpatch, gam, bet, wtok, btok, rows_dram):
    NCH = 8
    RC = CH * SIDE // NCH
    NALL = 2 * SRC * SIDE * SIDE
    INN = SIDE - 2 * HP
    WSUM = CH * (2 * SIDE * SIDE + 2 * INN * SIDE + INN * INN)
    with ExitStack() as ctx:
        n = Names(nc, ctx, "tok")
        sem = n.sem
        xi = n.sb("xi", [128, NCH, RC * SIDE])
        sq = n.sb("sq", [128, 2, RC * SIDE])
        gam_sb = n.sb("gam", [128, SRC, T])
        bet_sb = n.sb("bet", [128, SRC, T])
        w_sb = n.sb("w", [128, SRC, E])
        b_row = n.sb("b_row", [1, E])
        one_row = n.sb("one_row", [1, T])
        rall = n.sb("rall", [128, CH * SIDE])
        redge = n.sb("redge", [128, CH * SIDE])
        st = n.sb("st", [128, 12])
        bits = n.sb("bits", [128, 1], I32)
        ms = n.sb("ms", [128, 2])
        msT = n.sb("msT", [2, 128])
        rwide = n.sb("rwide", [128, 128])
        rb = n.sb("rb", [128, 128])
        gb_sb = n.sb("gb_sb", [128, 2, 2, E])
        psg = n.ps("psg", [128, 2, 2, 128])
        psm = n.ps("psm", [128, 512])

        with nc.Block() as block:
            @block.sync
            def _(sp):
                sp.dma_start(w_sb[:], wtok).then_inc(sem("w"), 16)
                sp.dma_start(gam_sb[:], gam).then_inc(sem("w"), 16)
                sp.dma_start(bet_sb[:], bet).then_inc(sem("w"), 16)
                sp.dma_start(b_row[:], btok).then_inc(sem("w"), 16)
                for c in range(NCH):
                    sp.dma_start(xi[:, c, :], ximg[:, c, :]).then_inc(sem(f"x{c}"), 16)
                sp.wait_ge(sem("gb"), 1)
                for r in range(2):
                    sp.dma_start(rows_dram[r, 0:128, :], gb_sb[:, 0, r, :]).then_inc(sem("rows"), 16)
                    sp.dma_start(rows_dram[r, 128:T, :], gb_sb[0:REM, 1, r, :]).then_inc(sem("rows"), 16)
                sp.wait_ge(sem("rows"), 64)

            @block.tensor
            def _(pe):
                pe.wait_ge(sem("w"), 64)
                pe.wait_ge(sem("ones"), 1)
                for tt, (t0, m) in enumerate(((0, 128), (128, REM))):
                    for s in range(SRC):
                        nc.tensor.matmul(psg[0:m, tt, 0, :], gam_sb[:, s, t0:t0 + m], w_sb[:, s, :],
                                         start=s == 0, stop=s == SRC - 1)
                    for s in range(SRC):
                        nc.tensor.matmul(psg[0:m, tt, 1, :], bet_sb[:, s, t0:t0 + m], w_sb[:, s, :],
                                         start=s == 0, stop=False)
                    last = nc.tensor.matmul(psg[0:m, tt, 1, :], one_row[:, t0:t0 + m], b_row[:],
                                            start=False, stop=True)
                last.then_inc(sem("g"), 1)
                pe.wait_ge(sem("ms"), 1)
                nc.tensor.matmul(psm[0:2, 0:128], ms[:], ident[:], start=True, stop=True)
                nc.tensor.matmul(psm[:, 128:256], rwide[:], ident[:], start=True, stop=True).then_inc(sem("mt"), 1)

            @block.scalar
            def _(act):
                act.wait_ge(sem("mean"), 1)
                for c in range(NCH):
                    if c >= 2:
                        act.wait_ge(sem("sqread"), c - 1)
                    nc.scalar.activation(sq[:, c % 2, :], xi[:, c, :], ACT.Square,
                                         bias=st[:, 4:5]).then_inc(sem("sq"), 1)

            @block.vector
            def _(dve):
                chain = [0]

                def link(ins):
                    chain[0] += 1
                    ins.then_inc(sem("chain"), 1)
                    dve.wait_ge(sem("chain"), chain[0])

                nc.vector.memset(one_row[:], 1.0).then_inc(sem("ones"), 1)

                def total(src, dst):
                    for c in range(CH):
                        base = c * SIDE
                        link(nc.vector.tensor_reduce(st[:, 0:1], rall[:, base:base + SIDE], AX.X, ALU.add))
                        link(nc.vector.tensor_reduce(st[:, 1:2], rall[:, base + HP:base + SIDE - HP], AX.X, ALU.add))
                        link(nc.vector.tensor_reduce(st[:, 2:3], redge[:, base:base + SIDE], AX.X, ALU.add))
                        link(nc.vector.tensor_reduce(st[:, 3:4], redge[:, base + HP:base + SIDE - HP], AX.X, ALU.add))
                        link(nc.vector.tensor_scalar(st[:, 0:1], st[:, 0:1], 3.0, None, ALU.mult))
                        link(nc.vector.scalar_tensor_tensor(st[:, 0:1], st[:, 1:2], 2.0, st[:, 0:1], ALU.mult, ALU.add))
                        link(nc.vector.tensor_tensor(st[:, 0:1], st[:, 0:1], st[:, 2:3], ALU.subtract))
                        link(nc.vector.tensor_tensor(st[:, 5 + c:6 + c], st[:, 0:1], st[:, 3:4], ALU.subtract))
                    link(nc.vector.tensor_tensor(dst, st[:, 5:6], st[:, 6:7], ALU.add))

                def rows(c, src):
                    v = src.rearrange("p (r c) -> p r c", c=SIDE)
                    nc.vector.tensor_reduce(rall[:, c * RC:(c + 1) * RC], v, AX.X, ALU.add)
                    edges = v.rearrange("p r (a b) -> p r a b", b=HP)[:, :, 0:SIDE // HP:SIDE // HP - 1, :]
                    return nc.vector.tensor_reduce(redge[:, c * RC:(c + 1) * RC], edges, AX.XY, ALU.add)

                for c in range(NCH):
                    dve.wait_ge(sem(f"x{c}"), 16)
                    last = rows(c, xi[:, c, :])
                link(last)
                total(None, st[:, 7:8])
                link(nc.vector.tensor_scalar(ms[:, 0:1], st[:, 7:8], 1.0 / NALL, None, ALU.mult))
                nc.vector.tensor_scalar(st[:, 4:5], ms[:, 0:1], -1.0, None, ALU.mult).then_inc(sem("mean"), 1)
                for c in range(NCH):
                    dve.wait_ge(sem("sq"), c + 1)
                    last = rows(c, sq[:, c % 2, :]).then_inc(sem("sqread"), 1)
                dve.wait_ge(sem("sqread"), NCH)
                total(None, st[:, 7:8])
                link(nc.vector.tensor_tensor(st[:, 10:11], ms[:, 0:1], ms[:, 0:1], ALU.mult))
                link(nc.vector.scalar_tensor_tensor(st[:, 8:9], st[:, 10:11], float(NALL - WSUM), st[:, 7:8],
                                                    ALU.mult, ALU.add))
                link(nc.vector.tensor_scalar(st[:, 8:9], st[:, 8:9], 1.0 / NALL, EPS_TOK, ALU.mult, ALU.add))
                rsqrt(nc, dve, sem("rsqrt"), 0, st[:, 8:9], st[:, 9:10], st[:, 11:12], bits[:])
                link(nc.vector.tensor_tensor(ms[:, 1:2], st[:, 8:9], st[:, 9:10], ALU.mult))
                dve.wait_ge(sem("g"), 1)
                for tt, m in enumerate((128, REM)):
                    nc.vector.tensor_scalar(gb_sb[0:m, tt, 0, :], psg[0:m, tt, 0, :], -1.0, None, ALU.mult)
                    last = nc.vector.tensor_copy(gb_sb[0:m, tt, 1, :], psg[0:m, tt, 1, :])
                last.then_inc(sem("gb"), 1)
                link(nc.vector.memset(rwide[:], 1.0))
                nc.vector.tensor_scalar(rwide[:], rwide[:], st[:, 9:10], None, ALU.mult).then_inc(sem("ms"), 1)
                dve.wait_ge(sem("mt"), 1)
                nc.vector.tensor_copy(msT[:], psm[0:2, 0:128])
                nc.vector.tensor_copy(rb[:], psm[:, 128:256])

        NW = 4
        ring = xi[:, :, :].rearrange("p a b -> p (a b)")
        XB = NBLK * IMG
        XP = GRID * IMG
        blk = [ring[:, r * XB:(r + 1) * XB].rearrange("p (j b) -> p j b", b=IMG) for r in range(4)]
        pat = [ring[:, 4 * XB + r * XP:4 * XB + (r + 1) * XP].rearrange("p (j b) -> p j b", b=IMG) for r in range(2)]
        off = 4 * XB + 2 * XP
        wg = [ring[:, off + r * SRC * E:off + (r + 1) * SRC * E].rearrange("p (s e) -> p s e", e=E) for r in range(NW)]
        off += NW * SRC * E
        gbr = [ring[0:2, off + r * GRID * E:off + (r + 1) * GRID * E] for r in range(2)]
        hv = hT[:, :].rearrange("p (b t) -> p b t", t=T)
        NB = 5
        pst = [n.ps(f"pst{k}", [128, 512]) for k in range(NB)]

        pools = [j for j in range(GRID) if j % 3 == 2]
        dves = [j for j in range(GRID) if j % 3 != 2]

        with nc.Block() as block:
            @block.sync
            def _(sp):
                sp.dma_start(blk[0], xblk[:, 0]).then_inc(sem("blk_first"), 16)

                def load(i, par):
                    after(sp, sem("done"), (i - 1) * GRID)
                    sp.dma_start(blk[(par + 1) % 4], xblk[:, bass.ds(i + 1, 1)]).then_inc(sem(f"blk{par % 2}"), 16)
                    sp.dma_start(pat[par % 2], xpatch[:, bass.ds(i, 1)]).then_inc(sem(f"blk{par % 2}"), 16)
                    sp.dma_start(gbr[par % 2], rows_dram[:, bass.ds(i * GRID, GRID), :].rearrange(
                        "r t e -> r (t e)")).then_inc(sem(f"blk{par % 2}"), 16)

                for i in range(5):
                    load(i, i)
                with sp.Fori(0, 2) as it:
                    for par in range(4):
                        load(it * 4 + (par + 5), par + 1)

            @block.gpsimd
            def _(pool):
                def row(i, par):
                    for j in pools:
                        after(pool, sem("done"), i * GRID + (j - NW + 1))
                        nc.gpsimd.tensor_tensor(wg[(par * GRID + j) % NW], w_sb[:, :, :],
                                                gam_sb[:, :, bass.ds(i * GRID + j, 1)].broadcast_to([128, SRC, E]),
                                                ALU.mult).then_inc(sem("wpool"), 1)
                row(0, 0)
                with pool.Fori(0, 3) as it:
                    for par in range(4):
                        row(it * 4 + par + 1, par + 1)

            @block.vector
            def _(dve):
                def evac(i, par, j):
                    dve.wait_ge(sem("done"), i * GRID + j + 1)
                    nc.vector.tensor_tensor(hv[:, :, bass.ds(i * GRID + j, 1)].rearrange("p b t -> p (b t)"),
                                            pst[j % NB][:, 0:IMG], rb[:], ALU.mult).then_inc(sem("out"), 1)

                def row(i, par):
                    for j in range(GRID):
                        if j in dves:
                            after(dve, sem("done"), i * GRID + (j - NW + 1))
                            nc.vector.tensor_tensor(wg[(par * GRID + j) % NW], w_sb[:, :, :],
                                                    gam_sb[:, :, bass.ds(i * GRID + j, 1)].broadcast_to([128, SRC, E]),
                                                    ALU.mult).then_inc(sem("wdve"), 1)
                        if j >= 2:
                            evac(i, par, j - 2)
                    evac(i, par, GRID - 2)
                    evac(i, par, GRID - 1)
                row(0, 0)
                with dve.Fori(0, 3) as it:
                    for par in range(4):
                        row(it * 4 + par + 1, par + 1)

            @block.tensor
            def _(pe):
                def row(i, par, half):
                    pe.wait_ge(sem(f"blk{par % 2}"), 48 * (half + 1))
                    for j in range(GRID):
                        if j in pools:
                            pe.wait_ge(sem("wpool"), i * len(pools) + pools.index(j) + 1)
                        else:
                            pe.wait_ge(sem("wdve"), i * len(dves) + dves.index(j) + 1)
                        after(pe, sem("out"), i * GRID + (j - NB + 1) if j >= NB else i * GRID)
                        w = wg[(par * GRID + j) % NW]
                        acc = pst[j % NB][:, 0:IMG]
                        top, low = blk[par % 4], blk[(par + 1) % 4]
                        for s, x in enumerate((pat[par % 2][:, j, :], low[:, j, :], low[:, j + 1, :],
                                               top[:, j, :], top[:, j + 1, :])):
                            nc.tensor.matmul(acc, w[:, s, :], x, start=s == 0, stop=False)
                        nc.tensor.matmul(acc, gbr[par % 2][:, j * E:(j + 1) * E], msT[:], start=False,
                                         stop=True).then_inc(sem("done"), 1)
                pe.wait_ge(sem("blk_first"), 16)
                row(0, 0, 0)
                with pe.Fori(0, 3) as it:
                    for par in range(4):
                        row(it * 4 + par + 1, par + 1, it * 2 + (par + 1) // 2)
        n.clear()


PARTS = 3
Q_OF = (0, 0, 1, 1, 0, 2)
K_OF = (0, 1, 0, 1, 2, 0)
KQ = len(Q_OF) * D
KB = KQ + D
UNITS = 8


def attention(nc, hT, ident, mats, weights, cols, scratch, lsh, tT_dram):
    stage = "lsh" if lsh else "att"
    scale = 1.0 / float(np.sqrt(E)) if lsh else 0.25
    NSIDE = 1 if lsh else 2
    NP = PARTS + 1 if lsh else 2 * PARTS
    LOADS = (2 * len(Q_OF) + 2) if lsh else 2 * len(Q_OF)
    with ExitStack() as ctx:
        n = Names(nc, ctx, stage)
        sem = n.sem
        wq = n.sb("wq", [128, E])
        wv = n.sb("wv", [128, E])
        wk = n.sb("wk", [128, E]) if not lsh else None
        wo = n.sb("wo", [128, E]) if not lsh else None
        hyp = n.sb("hyp", [128, E]) if lsh else None
        col = n.sb("col", [128, 8])
        sel_num = n.sb("sel_num", [128, 2, E])
        sel_den = n.sb("sel_den", [128, 2, E])
        mean_w = n.sb("mean_w", [128, 128])
        cent = n.sb("cent", [128, N2])
        sqr = n.sb("sqr", [128, N2])
        var, rstd, nwt = (n.sb(x, [128, 4]) for x in ("var", "rstd", "nwt"))
        nbits = n.sb("nbits", [128, 4], I32)
        NXH = 2 if lsh else 4
        xh = [n.sb(f"xh{p}", [128, N2]) for p in range(NXH)]
        qf = n.sb("qf", [128, N2])
        kf = n.sb("kf", [128, N2]) if not lsh else None
        rst = n.sb("rst", [128, N2])
        att = n.sb("att", [128, N2])
        prj = n.sb("prj", [128, N2]) if lsh else None
        parts = n.sb("parts", [128, NP, 2 * TP], BF16)
        qs = [n.sb(f"qs{p}", [KB, H, 2 * TP], BF16) for p in range(2)]
        ks = [n.sb(f"ks{p}", [KB, H, 2 * TP], BF16) for p in range(2)]
        kb = [n.sb(f"kb{p}", [KB, H, 2 * TP], BF16) for p in range(2)] if lsh else None
        vm = [n.sb(f"vm{p}", [128, 2, H, 32]) for p in range(2)]
        vr = [n.sb(f"vr{p}", [128, 2, H, 32]) for p in range(2)]
        fac = [n.sb(f"fac{p}", [128, 3 * T], BF16) for p in range(2)] if lsh else None
        scr = [n.sb(f"scr{p}", [128, 3 * T]) for p in range(2)] if lsh else None
        mx = [n.sb(f"mx{p}", [128, 3]) for p in range(2)]
        nm = [n.sb(f"nm{p}", [128, 3]) for p in range(2)]
        prob = [n.sb(f"prob{p}", [128, 3 * T]) for p in range(2)]
        ptm = [n.sb(f"ptm{p}", [128, 2 * TP]) for p in range(2)]
        ptr = [n.sb(f"ptr{p}", [128, 2 * TP]) for p in range(2)]
        osb = n.sb("osb", [128, 2, N2])
        rec = n.sb("rec", [128, N2])
        if not lsh:
            oh, yy, cent2, sqr2, nrm2, tt = (n.sb(x, [128, N2]) for x in ("oh", "yy", "cent2", "sqr2", "nrm2", "tt"))
            var2, rstd2 = (n.sb(x, [128, 4]) for x in ("var2", "rstd2"))
        g0, g1 = n.ps("g0", [128, 512]), n.ps("g1", [128, 512])
        ps_s = [n.ps("s0", [128, 512])]
        ps_f = n.ps("f", [128, 512]) if lsh else None
        if not lsh:
            ps_s.append(n.ps("s1", [128, 512]))
        NS = len(ps_s)
        ps_tm, ps_tr = n.ps("tm", [128, 512]), n.ps("tr", [128, 512])
        ps_o = [n.ps(f"o{g}", [128, 512]) for g in range(2)]

        CONST = len(weights) + 4

        def consts(eng):
            eng.wait_ge(sem("const"), 16 * CONST)
            eng.wait_ge(sem("zero"), 1)

        def parts_made(eng, pairs_done):
            if lsh:
                after(eng, sem("parts"), pairs_done)
            else:
                after(eng, sem("split"), 4 * NSIDE * pairs_done)

        def both(ap):
            return ap.rearrange("p (i t) -> p i t", t=TP)[:, :, 0:T]

        def two(ap):
            return ap.rearrange("p (i t) -> p i t", t=T)

        def h_of(i):
            return hT[:, bass.ds(i * N2, N2)]

        UNROLL = 2 if lsh else 4

        def pairs(eng, head, step):
            head()
            step(0, 0, 0)
            step(1, 1, 0)
            with eng.Fori(0, (PAIRS - 4) // UNROLL) as it:
                for k in range(UNROLL):
                    step(it * UNROLL + (2 + k), (2 + k) % 4, it * (UNROLL // 2) + (2 + k) // 2)
            step(PAIRS - 2, (PAIRS - 2) % 4, (PAIRS - 2) // 2)
            step(PAIRS - 1, (PAIRS - 1) % 4, (PAIRS - 1) // 2)

        def is_last(i, k):
            return isinstance(i, int) and i + k >= PAIRS

        def first(i):
            return isinstance(i, int) and i == 0

        with nc.Block() as block:
            @block.sync
            def _(sp):
                for dst, src in zip((wq, wv, hyp) if lsh else (wq, wv, wk, wo), weights):
                    sp.dma_start(dst[:], src).then_inc(sem("const"), 16)
                sp.dma_start(col[:], cols).then_inc(sem("const"), 16)
                sp.dma_start(sel_num[:], mats[0]).then_inc(sem("const"), 16)
                sp.dma_start(sel_den[:], mats[1]).then_inc(sem("const"), 16)
                sp.dma_start(mean_w[:], mats[2]).then_inc(sem("const"), 16)
                sp.wait_ge(sem("zero"), 1)

                def stack(i, par):
                    parts_made(sp, i + 1)
                    sp.dma_start(scratch[par, 0:NP].rearrange("s p t -> p s t"), parts[:]).then_inc(sem("store"), 16)
                    sp.wait_ge(sem("store"), 16 * (i + 1))
                    after(sp, sem("s"), UNITS * (i - 1))
                    if lsh:
                        after(sp, sem("f"), UNITS * (i - 1))

                    def load(dst, row, part):
                        sp.dma_start(dst[row:row + D], scratch[par, part].rearrange(
                            "(h d) t -> d h t", d=D)).then_inc(sem(f"load{par}"), 16)
                    for j, (a, b) in enumerate(zip(Q_OF, K_OF)):
                        load(qs[par], j * D, a)
                        load(ks[par], j * D, b if lsh else b + PARTS)
                    if lsh:
                        load(qs[par], KQ, PARTS)
                        load(kb[par], KQ, PARTS)

                def head():
                    stack(0, 0)
                    stack(1, 1)

                def step(i, m, half):
                    if not is_last(i, 2):
                        stack(i + 2, m % 2)
                    if not lsh and not first(i) and not first(i - 1):
                        sp.wait_ge(sem("tt"), i - 1)
                        sp.dma_start(tT_dram[:, bass.ds((i - 2) * N2, N2)], tt[:]).then_inc(sem("out"), 16)
                pairs(sp, head, step)
                if not lsh:
                    for i in (PAIRS - 2, PAIRS - 1):
                        sp.wait_ge(sem("tt"), i + 1)
                        sp.dma_start(tT_dram[:, i * N2:(i + 1) * N2], tt[:]).then_inc(sem("out"), 16)
                    sp.wait_ge(sem("out"), 16 * PAIRS)

            @block.tensor
            def _(pe):
                mm = nc.tensor.matmul
                reader = [None, None]

                def bank(b, i, name, m, c):
                    if reader[b]:
                        pe.wait_ge(sem(reader[b][0]), i * reader[b][1] + reader[b][2])
                    reader[b] = (name, m, c)
                    return (g0, g1)[b]

                def next_step():
                    for b in range(2):
                        if reader[b]:
                            name, m, c = reader[b]
                            reader[b] = (name, m, c - m)

                def mean(i, b):
                    g = bank(b, i, "cent", 1, 3)
                    mm(g[:, 0:N2], mean_w[:], h_of(i + 2), start=True, stop=True).then_inc(sem("mean"), 1)

                def token_means(g, x):
                    for im in range(2):
                        for k, t0 in enumerate((im * T, im * T + REM)):
                            last = mm(g[:, 2 * im + k:2 * im + k + 1], x[:, t0:t0 + 128], mean_w[:, 0:1],
                                      start=True, stop=True)
                    return last

                def spread(g, x):
                    for im in range(2):
                        c = 2 * im
                        mm(g[:, im * T:im * T + 128], x[:, c:c + 1].broadcast_to([128, 128]), ident[:],
                           start=True, stop=True)
                        last = mm(g[:, im * T + 128:(im + 1) * T], x[:, c + 1:c + 2].broadcast_to([128, 128]),
                                  ident[:, 128 - REM:128], start=True, stop=True)
                    return last

                def variance(i, b):
                    g = bank(b, i, "vcp", 1, 3)
                    pe.wait_ge(sem("sq"), i + 3)
                    token_means(g, sqr).then_inc(sem("var"), 1)

                def deviation(i, b):
                    g = bank(b, i, "xh", 1, 3)
                    pe.wait_ge(sem("rs"), RSQRT_OPS * (i + 3))
                    spread(g, rstd).then_inc(sem("rbc"), 1)

                def project(w, i, m, b, name, name_read):
                    g = bank(b, i, name_read, 1, 3)
                    pe.wait_ge(sem("xh"), i + 3)
                    mm(g[:, 0:N2], w[:], xh[(m + 2) % NXH][:], start=True, stop=True).then_inc(sem(name), 1)

                def hyperplanes(i, b):
                    g = bank(b, i, "prc", 1, 3)
                    pe.wait_ge(sem("qf"), i + 3)
                    mm(g[:, 0:N2], hyp[:], qf[:], start=True, stop=True).then_inc(sem("pr"), 1)

                def values(i, m, im, b):
                    g = bank(b, i, "v_copied", 2, 3 + im)
                    pe.wait_ge(sem("xh"), i + 2)
                    x = xh[(m + 1) % NXH][:, im * T:(im + 1) * T]
                    mm(g[:, 0:E], x[:, 0:128], wv[:], start=True, stop=True)
                    mm(g[0:REM, E:2 * E], x[:, 128:T], wv[:], start=True, stop=True).then_inc(sem("v"), 1)

                def scores(i, par, half, u):
                    im, a = u // 4, 2 * (u % 4)
                    n_u = i * UNITS + u
                    if u == 0:
                        pe.wait_ge(sem(f"load{par}"), 16 * LOADS * (half + 1))
                    after(pe, sem("scr" if lsh else "exp"), n_u - (NS - 1))

                    def products(dst, rows, k):
                        q0 = im * TP
                        for x in range(2):
                            mm(dst[:, x * T:(x + 1) * T], qs[par][0:rows, a + x, q0:q0 + 128],
                               k[par][0:rows, a + x, q0:q0 + T], start=True, stop=True)
                            last = mm(dst[64 * x:64 * x + 64, 2 * T:3 * T], qs[par][0:rows, a + x, q0 + 128:q0 + TP],
                                      k[par][0:rows, a + x, q0:q0 + T], start=True, stop=True)
                        return last
                    products(ps_s[u % NS], KQ, ks).then_inc(sem("s"), 1)
                    if lsh:
                        after(pe, sem("f_read"), n_u)
                        products(ps_f, KB, kb).then_inc(sem("f"), 1)

                def transposes(i, u):
                    n_u = i * UNITS + u
                    pe.wait_ge(sem("exp"), n_u + 1)
                    after(pe, sem("tm_read"), n_u)
                    after(pe, sem("tr_read"), n_u)
                    p = prob[u % 2]
                    for x in range(2):
                        nc.tensor.transpose(ps_tm[:, x * TP:x * TP + 128], p[:, x * T:x * T + 128], ident[:])
                        nc.tensor.transpose(ps_tr[0:REM, x * TP:x * TP + 128], p[:, x * T + 128:(x + 1) * T], ident[:])
                    rest_m = ps_tm[:, 0:2 * TP].rearrange("p (x t) -> p x t", t=TP)[:, :, 128:TP]
                    rest_r = ps_tr[0:REM, 0:2 * TP].rearrange("p (x t) -> p x t", t=TP)[:, :, 128:TP]
                    nc.tensor.transpose(rest_m, p[:, 2 * T:2 * T + 128], ident[:])
                    nc.tensor.transpose(rest_r, p[:, 2 * T + 128:3 * T], ident[:]).then_inc(sem("t"), 1)

                def weighted(i, par, u):
                    im, a = u // 4, 2 * (u % 4)
                    n_u = i * UNITS + u
                    pe.wait_ge(sem("tm_read"), n_u + 1)
                    pe.wait_ge(sem("tr_read"), n_u + 1)
                    if u == 0:
                        pe.wait_ge(sem("v_copied"), 2 * (i + 1))
                        after(pe, sem("o0"), i)
                        after(pe, sem("o1"), i)
                    for x in range(2):
                        hd = a + x
                        out = ps_o[hd // 4][32 * (hd % 4):32 * (hd % 4) + 32, im * T:(im + 1) * T]
                        mm(out, vm[par][:, im, hd, :], ptm[u % 2][:, x * TP:x * TP + T], start=True, stop=False)
                        last = mm(out, vr[par][:, im, hd, :], ptr[u % 2][:, x * TP:x * TP + T], start=False, stop=True)
                    last.then_inc(sem("pv"), 1)

                def finish(i):
                    pe.wait_ge(sem("o0"), i)
                    pe.wait_ge(sem("o1"), i)
                    for b, (sel, name, read) in enumerate(((sel_num, "num", "tn"), (sel_den, "den", "rec"))):
                        g = bank(b, i, read, 1, 0)
                        mm(g[:, 0:N2], sel[:, 0, :], osb[:, 0, :], start=True, stop=False)
                        mm(g[:, 0:N2], sel[:, 1, :], osb[:, 1, :], start=False, stop=True).then_inc(sem(name), 1)

                def output(i, k):
                    ready, done, read = (("oh", "wo", "yy"), ("yy", "mean2", "cent2"), ("sq2", "var2", "vcp2"),
                                         ("rs2", "rbc2", "tn2"))[k]
                    g = bank(0, i, read, 1, 0)
                    pe.wait_ge(sem(ready), i * (RSQRT_OPS if k == 3 else 1))
                    if k == 2:
                        last = token_means(g, sqr2)
                    elif k == 3:
                        last = spread(g, rstd2)
                    else:
                        w, x = ((wo, oh), (mean_w, yy))[k]
                        last = mm(g[:, 0:N2], w[:], x[:], start=True, stop=True)
                    last.then_inc(sem(done), 1)

                def head():
                    consts(pe)
                    for a in (-2, -1):
                        mean(a, 0)
                        variance(a, 1)
                        deviation(a, 0)
                        project(wq, a, a, 1, "q", "qf")
                        if lsh:
                            hyperplanes(a, 0)
                        else:
                            project(wk, a, a, 0, "k", "kf")
                        if a == -2:
                            next_step()
                    values(-1, -1, 0, 1)
                    values(-1, -1, 1, 0)
                    scores(0, 0, 0, 0)
                    scores(0, 0, 0, 1)

                def step(i, m, half):
                    par = m % 2
                    next_step()
                    have_a, have_v = not is_last(i, 2), not is_last(i, 1)
                    for u in range(UNITS):
                        if u < 6:
                            scores(i, par, half, u + 2)
                        elif have_v:
                            scores(i + 1, 1 - par, half + par, u - 6)
                        if u > 0:
                            weighted(i, par, u - 1)
                        elif not first(i):
                            weighted(i - 1, 1 - par, UNITS - 1)
                        transposes(i, u)
                        later = not lsh and not first(i)
                        if u == 0 and have_a:
                            mean(i, 0 if lsh else 1)
                        if u == 1 and not first(i):
                            finish(i)
                        if u == 2 and have_a:
                            variance(i, 1)
                        if u == 3 and have_a:
                            deviation(i, 0 if lsh else 1)
                        if u == 3 and later:
                            output(i, 0)
                        if u == 4 and have_a:
                            project(wq, i, m, 1, "q", "qf")
                        if u == 4 and later:
                            output(i, 1)
                        if u == 5 and have_v:
                            values(i, m, 0, 0)
                        if u == 5 and have_a:
                            if lsh:
                                hyperplanes(i, 1)
                            else:
                                project(wk, i, m, 1, "k", "kf")
                        if u == 6 and later:
                            output(i, 2)
                        if u == 6 and have_v:
                            values(i, m, 1, 0 if lsh else 1)
                        if u == 7 and later:
                            output(i, 3)
                pairs(pe, head, step)
                weighted(PAIRS - 1, 1, UNITS - 1)
                next_step()
                finish(PAIRS)
                if not lsh:
                    for k in range(4):
                        output(PAIRS, k)

            @block.scalar
            def _(act):
                fn = nc.scalar.activation

                def factors(i, u):
                    n_u = i * UNITS + u
                    act.wait_ge(sem("f"), n_u + 1)
                    after(act, sem("scr"), n_u - 1)
                    fn(fac[u % 2][:], ps_f[:, 0:3 * T], ACT.Copy, bias=-1.0, scale=8.0).then_inc(sem("f_read"), 1)

                def exponentials(i, u):
                    n_u = i * UNITS + u
                    act.wait_ge(sem("nm"), n_u + 1)
                    after(act, sem("t"), n_u - 1)
                    src = scr[u % 2] if lsh else ps_s[u % NS]
                    for x in range(3):
                        last = fn(prob[u % 2][:, x * T:(x + 1) * T], src[:, x * T:(x + 1) * T], ACT.Exp,
                                  bias=nm[u % 2][:, x:x + 1], scale=scale)
                    last.then_inc(sem("exp"), 1)

                def rest_keys(i, u):
                    n_u = i * UNITS + u
                    act.wait_ge(sem("t"), n_u + 1)
                    after(act, sem("pv"), n_u - 1)
                    fn(ptr[u % 2][0:REM, :], ps_tr[0:REM, 0:2 * TP], ACT.Copy).then_inc(sem("tr_read"), 1)

                def square(i):
                    act.wait_ge(sem("cent"), i + 3)
                    after(act, sem("var"), i + 2)
                    fn(sqr[:], cent[:], ACT.Square).then_inc(sem("sq"), 1)

                def with_bias(i, dst, g, bias, name, done):
                    act.wait_ge(sem(name), i + 3)
                    parts_made(act, i + 2)
                    fn(dst[:], g[:, 0:N2], ACT.Identity, bias=col[:, bias:bias + 1]).then_inc(sem(done), 1)

                def v_copy(i, par, im, g):
                    act.wait_ge(sem("v"), 2 * i + 3 + im)
                    if im == 0:
                        after(act, sem("pv"), UNITS * i)
                    fn(vm[par][:, im, :, 0:D], g[:, 0:E].rearrange("p (h d) -> p h d", d=D), ACT.Copy)
                    fn(vr[par][0:REM, im, :, 0:D], g[0:REM, E:2 * E].rearrange("p (h d) -> p h d", d=D),
                       ACT.Copy).then_inc(sem("v_copied"), 1)

                def head():
                    consts(act)
                    for a in (-2, -1):
                        square(a)
                        with_bias(a, qf, g1, 0, "q", "qf")
                        if lsh:
                            with_bias(a, prj, g0, 1, "pr", "prc")
                        else:
                            with_bias(a, kf, g0, 1, "k", "kf")
                    v_copy(-1, 0, 0, g1)
                    v_copy(-1, 0, 1, g0)
                    if lsh:
                        factors(0, 0)
                        factors(0, 1)

                def step(i, m, half):
                    have_a, have_v = not is_last(i, 2), not is_last(i, 1)
                    for u in range(UNITS):
                        exponentials(i, u)
                        if lsh and u < 6:
                            factors(i, u + 2)
                        elif lsh and have_v:
                            factors(i + 1, u - 6)
                        if u == 0 and not first(i):
                            outputs(i)
                        if u == 2 and have_a:
                            square(i)
                        if u == 5 and have_a:
                            with_bias(i, qf, g1, 0, "q", "qf")
                        if u == 6 and have_v:
                            v_copy(i, (m + 1) % 2, 0, g0)
                        if u == 6 and have_a:
                            if lsh:
                                with_bias(i, prj, g1, 1, "pr", "prc")
                            else:
                                with_bias(i, kf, g1, 1, "k", "kf")
                        if u == 6 and not lsh and not first(i):
                            square2(i)
                        if u == 7 and have_v:
                            v_copy(i, (m + 1) % 2, 1, g0 if lsh else g1)
                        rest_keys(i, u)

                def outputs(i):
                    act.wait_ge(sem("pv"), UNITS * i)
                    after(act, sem("den"), i - 1)
                    fn(osb[:, 1, :], ps_o[1][:, 0:N2], ACT.Copy).then_inc(sem("o1"), 1)

                def square2(i):
                    act.wait_ge(sem("cent2"), i)
                    after(act, sem("var2"), i - 1)
                    fn(sqr2[:], cent2[:], ACT.Square).then_inc(sem("sq2"), 1)

                pairs(act, head, step)
                outputs(PAIRS)
                if not lsh:
                    square2(PAIRS)

            @block.vector
            def _(dve):
                def row_max(i, u):
                    n_u = i * UNITS + u
                    dve.wait_ge(sem("s"), n_u + 1)
                    if lsh:
                        dve.wait_ge(sem("f_read"), n_u + 1)
                        after(dve, sem("exp"), n_u - 1)
                        nc.vector.scalar_tensor_tensor(scr[u % 2][:], fac[u % 2][:], 30.0, ps_s[0][:, 0:3 * T],
                                                       ALU.max, ALU.mult).then_inc(sem("scr"), 1)
                        dve.wait_ge(sem("scr"), n_u + 1)
                    src = scr[u % 2] if lsh else ps_s[u % NS]
                    nc.vector.tensor_reduce(mx[u % 2][:], src[:, 0:3 * T].rearrange("p (x t) -> p x t", t=T),
                                            AX.X, ALU.max).then_inc(sem("mx"), 1)
                    dve.wait_ge(sem("mx"), n_u + 1)
                    after(dve, sem("exp"), n_u - 1)
                    nc.vector.tensor_scalar(nm[u % 2][:], mx[u % 2][:], -scale, None, ALU.mult).then_inc(sem("nm"), 1)

                def main_keys(i, u):
                    n_u = i * UNITS + u
                    dve.wait_ge(sem("t"), n_u + 1)
                    after(dve, sem("pv"), n_u - 1)
                    nc.vector.tensor_copy(ptm[u % 2][:], ps_tm[:, 0:2 * TP]).then_inc(sem("tm_read"), 1)

                def center(i, g):
                    dve.wait_ge(sem("mean"), i + 3)
                    after(dve, sem("sq"), i + 2)
                    after(dve, sem("xh"), i + 2)
                    nc.vector.tensor_tensor(cent[:], h_of(i + 2), g[:, 0:N2], ALU.subtract).then_inc(sem("cent"), 1)

                def deviation(i, g, v, y, ready, copied, spread_done, done, nth):
                    dve.wait_ge(sem(ready), nth + 1)
                    nc.vector.tensor_scalar(v[:], g[:, 0:4], EPS_LN, None, ALU.add).then_inc(sem(copied), 1)
                    dve.wait_ge(sem(copied), nth + 1)
                    after(dve, sem(spread_done), nth)
                    rsqrt(nc, dve, sem(done), nth * RSQRT_OPS, v[:], y[:], nwt[:], nbits[:])

                def normal(i, m, g):
                    dve.wait_ge(sem("rbc"), i + 3)
                    dve.wait_ge(sem("cent"), i + 3)
                    if not first(i + 2):
                        after(dve, sem("v"), 2 * (i + 3 - NXH))
                        if not lsh:
                            after(dve, sem("yy"), i + 3 - NXH)
                            after(dve, sem("k"), i + 3 - NXH)
                        after(dve, sem("q"), i + 3 - NXH)
                    nc.vector.tensor_tensor(xh[(m + 2) % NXH][:], cent[:], g[:, 0:N2], ALU.mult).then_inc(sem("xh"), 1)

                def outputs(i):
                    dve.wait_ge(sem("pv"), UNITS * i)
                    after(dve, sem("den"), i - 1)
                    nc.vector.tensor_copy(osb[:, 0, :], ps_o[0][:, 0:N2]).then_inc(sem("o0"), 1)

                def divide(i):
                    dve.wait_ge(sem("den"), i)
                    after(dve, sem("tn"), i - 1)
                    nc.vector.reciprocal(rec[:], g1[:, 0:N2]).then_inc(sem("rec"), 1)
                    dve.wait_ge(sem("rec"), i)
                    dve.wait_ge(sem("num"), i)
                    if not lsh:
                        after(dve, sem("oh"), i - 1)
                    nc.vector.tensor_tensor(att[:], g0[:, 0:N2], rec[:], ALU.mult).then_inc(sem("tn"), 1)
                    if lsh:
                        dve.wait_ge(sem("tn"), i)
                        nc.vector.scalar_tensor_tensor(h_of(i - 1), att[:], col[:, 2:3], h_of(i - 1),
                                                       ALU.add, ALU.add).then_inc(sem("hnew"), 1)

                def residual(i, m):
                    dve.wait_ge(sem("wo"), i)
                    after(dve, sem("mean2"), i - 1)
                    after(dve, sem("cent2"), i - 1)
                    nc.vector.scalar_tensor_tensor(yy[:], g0[:, 0:N2], col[:, 3:4], xh[(m + 3) % 4][:],
                                                   ALU.add, ALU.add).then_inc(sem("yy"), 1)

                def center2(i):
                    dve.wait_ge(sem("mean2"), i)
                    dve.wait_ge(sem("yy"), i)
                    after(dve, sem("sq2"), i - 1)
                    after(dve, sem("tn2"), i - 1)
                    nc.vector.tensor_tensor(cent2[:], yy[:], g0[:, 0:N2], ALU.subtract).then_inc(sem("cent2"), 1)

                def normal2(i):
                    dve.wait_ge(sem("rbc2"), i)
                    dve.wait_ge(sem("cent2"), i)
                    after(dve, sem("tt"), i - 1)
                    nc.vector.tensor_tensor(nrm2[:], cent2[:], g0[:, 0:N2], ALU.mult).then_inc(sem("tn2"), 1)

                gm = g0 if lsh else g1

                def head():
                    for b in [parts, *vm, *vr, *ptr]:
                        nc.vector.memset(b[:], 0.0)
                    nc.vector.memset(ptm[0][:], 0.0)
                    if lsh:
                        for b in kb:
                            nc.vector.memset(b[:], 0.0)
                    last = nc.vector.memset(ptm[1][:], 0.0).then_inc(sem("zdone"), 1)
                    dve.wait_ge(sem("zdone"), 1)
                    for b in (*vm, *vr):
                        last = nc.vector.memset(b[:, :, :, D:D + 1], 1.0)
                    last.then_inc(sem("zero"), 1)
                    consts(dve)
                    for a in (-2, -1):
                        center(a, g0)
                        deviation(a, g1, var, rstd, "var", "vcp", "rbc", "rs", a + 2)
                        normal(a, a, g0)
                    row_max(0, 0)

                def step(i, m, half):
                    have_a, have_v = not is_last(i, 2), not is_last(i, 1)
                    for u in range(UNITS):
                        if u < 7:
                            row_max(i, u + 1)
                        elif have_v:
                            row_max(i + 1, 0)
                        later = not lsh and not first(i)
                        if u == 0 and not first(i):
                            outputs(i)
                        if u == 0 and later and not first(i - 1):
                            normal2(i - 1)
                        if u == 1 and have_a:
                            center(i, gm)
                        if u == 2 and not first(i):
                            divide(i)
                        if u == 3 and have_a:
                            deviation(i, g1, var, rstd, "var", "vcp", "rbc", "rs", i + 2)
                        if u == 4 and have_a:
                            normal(i, m, gm)
                        if u == 4 and later:
                            residual(i, m)
                        if u == 5 and later:
                            center2(i)
                        if u == 7 and later:
                            deviation(i, g0, var2, rstd2, "var2", "vcp2", "rbc2", "rs2", i - 1)
                        main_keys(i, u)
                pairs(dve, head, step)
                outputs(PAIRS)
                if not lsh:
                    normal2(PAIRS - 1)
                divide(PAIRS)
                if lsh:
                    dve.wait_ge(sem("hnew"), PAIRS)
                else:
                    residual(PAIRS, PAIRS % 4)
                    center2(PAIRS)
                    deviation(PAIRS, g0, var2, rstd2, "var2", "vcp2", "rbc2", "rs2", PAIRS - 1)
                    normal2(PAIRS)

            @block.gpsimd
            def _(pool):
                def split(i, src, ready, base, k):
                    pool.wait_ge(sem(ready), i + 3)
                    after(pool, sem("store"), 16 * (i + 2))
                    hold(pool, sem("pass"))
                    hi, mid, low = (both(parts[:, base + p, :]) for p in range(3))
                    n_s = (i + 2) * NSIDE * 4 + 4 * k
                    nc.gpsimd.tensor_copy(hi, two(src[:])).then_inc(sem("split"), 1)
                    pool.wait_ge(sem("split"), n_s + 1)
                    nc.gpsimd.tensor_tensor(two(rst[:]), two(src[:]), hi, ALU.subtract).then_inc(sem("split"), 1)
                    pool.wait_ge(sem("split"), n_s + 2)
                    hold(pool, sem("pass"))
                    nc.gpsimd.tensor_copy(mid, two(rst[:])).then_inc(sem("split"), 1)
                    pool.wait_ge(sem("split"), n_s + 3)
                    last = nc.gpsimd.tensor_tensor(low, two(rst[:]), mid, ALU.subtract)
                    last.then_inc(sem("split"), 1)
                    pool.wait_ge(sem("split"), n_s + 4)

                def make_parts(i):
                    split(i, qf, "qf", 0, 0)
                    if lsh:
                        pool.wait_ge(sem("prc"), i + 3)
                        hold(pool, sem("pass"))
                        nc.gpsimd.tensor_scalar(both(parts[:, PARTS, :]), two(prj[:]), 0.0, 0.5,
                                                ALU.is_ge, ALU.subtract).then_inc(sem("parts"), 1)
                    else:
                        split(i, kf, "kf", PARTS, 1)

                def head():
                    consts(pool)
                    for a in (-2, -1):
                        make_parts(a)

                def step(i, m, half):
                    if not lsh and not first(i):
                        if not first(i - 1):
                            affine(i - 1)
                        v_bias(i)
                    if not is_last(i, 2):
                        make_parts(i)

                def v_bias(i):
                    pool.wait_ge(sem("tn"), i)
                    after(pool, sem("wo"), i - 1)
                    hold(pool, sem("pass"))
                    nc.gpsimd.tensor_scalar(oh[:], att[:], col[:, 2:3], None, ALU.add).then_inc(sem("oh"), 1)

                def affine(i):
                    pool.wait_ge(sem("tn2"), i)
                    after(pool, sem("out"), 16 * (i - 1))
                    hold(pool, sem("pass"))
                    nc.gpsimd.tensor_scalar(tt[:], nrm2[:], col[:, 4:5], col[:, 5:6], ALU.mult,
                                            ALU.add).then_inc(sem("tt"), 1)

                pairs(pool, head, step)
                if not lsh:
                    affine(PAIRS - 1)
                    v_bias(PAIRS)
                    affine(PAIRS)
        n.clear()


def chunks(eng, step):
    for k in range(3):
        step(k, k % 2, k // 2)
    with eng.Fori(0, (NC - 3) // 2) as it:
        for p in range(2):
            step(it * 2 + (p + 3), 1 - p, it + (p + 1))


def route(nc, hT, ident, tT_dram, t_dram, sorted_dram, gate_w, gate_b, prefix_w, logit, dest, best, tile_expert):
    with ExitStack() as ctx:
        n = Names(nc, ctx, "route")
        sem = n.sem
        gw = n.sb("gw", [128, NE])
        gb = n.sb("gb", [128, NE])
        upper = n.sb("upper", [128, 128])
        ones = n.sb("ones", [128, 128])
        tc = [n.sb(f"tc{p}", [128, CT * 128]) for p in range(2)]
        tok = [n.sb(f"tok{p}", [128, CT, 128]) for p in range(2)]
        zeros = n.sb("zeros", [128, 8 * 128])
        ps_l = [n.ps(f"l{p}", [128, 512]) for p in range(2)]
        ps_t = [n.ps(f"t{p}", [128, 512]) for p in range(2)]
        hot = n.sb("hot", [128, TILES, NE])
        rank = n.sb("rank", [128, TILES, NE])
        count = n.sb("count", [128, TILES, NE])
        cum = n.sb("cum", [128, NE, TILES])
        top = n.sb("top", [128, TILES])
        work = n.sb("work", [128, TILES, NE])
        pick = n.sb("pick", [128, TILES])
        idx_e = n.sb("idx_e", [128, NE])
        tot = n.sb("tot", [128, NE])
        tot_i = n.sb("tot_i", [128, NE], I32)
        tiles = n.sb("tiles", [128, NE])
        ends = n.sb("ends", [128, NE])
        starts = n.sb("starts", [128, NE])
        slot_no = n.sb("slot_no", [1, SLOTS])
        acc = [n.sb(f"acc{p}", [1, SLOTS]) for p in range(2)]

        with nc.Block() as block:
            @block.sync
            def _(sp):
                for dst, src in ((gw, gate_w), (gb, gate_b), (upper, prefix_w)):
                    sp.dma_start(dst[:], src).then_inc(sem("const"), 16)
                sp.wait_ge(sem("zeros"), 1)
                for k in range(SLOTS // 8):
                    sp.dma_start(sorted_dram[k * 1024:(k + 1) * 1024, :].rearrange("(p r) e -> p (r e)", r=8),
                                 zeros[:]).then_inc(sem("cleared"), 16)

                def load(k, p):
                    after(sp, sem("turned"), (k - 1) * CT)
                    sp.dma_start(tc[p][:], tT_dram[:, bass.ds(k * (CT * 128), CT * 128)]).then_inc(sem(f"load{p}"), 16)

                def store(k, p):
                    sp.wait_ge(sem("tok"), (k + 1) * CT)
                    sp.dma_start(t_dram[bass.ds(k * (CT * 128), CT * 128), :].rearrange("(c p) e -> p c e", p=128),
                                 tok[p][:]).then_inc(sem(f"store{p}"), 16)

                load(0, 0)
                for k in range(2):
                    load(k + 1, 1 - k)
                    store(k, k)
                with sp.Fori(0, (NC - 3) // 2) as it:
                    for p in range(2):
                        load(it * 2 + (p + 3), 1 - p)
                        store(it * 2 + (p + 2), p)
                store(NC - 1, 0)
                sp.wait_ge(sem("store0"), 16 * ((NC + 1) // 2))
                sp.wait_ge(sem("store1"), 16 * (NC // 2))
                sp.wait_ge(sem("cleared"), 16 * (SLOTS // 8))

            @block.tensor
            def _(pe):
                pe.wait_ge(sem("const"), 48)

                def chunk(k, p, half):
                    pe.wait_ge(sem(f"load{p}"), 16 * (half + 1))
                    after(pe, sem("logit"), k - 1)
                    for c in range(CT):
                        x = tc[p][:, c * 128:(c + 1) * 128]
                        nc.tensor.matmul(ps_l[p][:, c * NE:(c + 1) * NE], x, gw[:], start=True,
                                         stop=True).then_inc(sem("gate"), 1)
                        after(pe, sem("tok"), k * CT + (c - 1))
                        nc.tensor.transpose(ps_t[(p * CT + c) % 2][:, 0:128], x, ident[:]).then_inc(sem("turned"), 1)
                chunks(pe, chunk)

            @block.vector
            def _(dve):
                nc.vector.memset(ones[:], 1.0)
                nc.vector.memset(zeros[:], 0.0).then_inc(sem("zeros"), 1)
                dve.wait_ge(sem("const"), 48)

                def chunk(k, p, half):
                    after(dve, sem(f"store{p}"), 16 * half)
                    for c in range(CT):
                        dve.wait_ge(sem("turned"), k * CT + (c + 1))
                        nc.vector.tensor_copy(tok[p][:, c, :], ps_t[(p * CT + c) % 2][:, 0:128]).then_inc(sem("tok"), 1)
                    dve.wait_ge(sem("gate"), (k + 1) * CT)
                    nc.vector.tensor_tensor(logit[:, bass.ds(k * CT, CT), :],
                                            ps_l[p][:, 0:CT * NE].rearrange("p (c e) -> p c e", e=NE),
                                            gb[:, :].rearrange("p (o e) -> p o e", o=1).broadcast_to([128, CT, NE]),
                                            ALU.add).then_inc(sem("logit"), 1)
                chunks(dve, chunk)

        def per_token(x):
            return x.rearrange("p (c o) -> p c o", o=1).broadcast_to([128, TILES, NE])

        def per_expert(x):
            return x.rearrange("p (o e) -> p o e", o=1).broadcast_to([128, TILES, NE])

        with nc.Block() as block:
            @block.gpsimd
            def _(pool):
                nc.gpsimd.iota(idx_e[:], pattern=[[1, NE]], base=-NE, channel_multiplier=0,
                               allow_small_or_imprecise_dtypes=True)
                nc.gpsimd.iota(slot_no[:], pattern=[[1, SLOTS]], base=0, channel_multiplier=0,
                               allow_small_or_imprecise_dtypes=True).then_inc(sem("iota"), 1)

            @block.scalar
            def _(act):
                act.wait_ge(sem("shifted"), 1)
                nc.scalar.activation(work[:], work[:], ACT.Exp).then_inc(sem("gate_exp"), 1)

            @block.tensor
            def _(pe):
                pe.wait_ge(sem("hot"), 1)
                flat = hot[:, :, :].rearrange("p c e -> p (c e)")
                W = TILES * NE
                for k in range(0, W, 512):
                    w = min(512, W - k)
                    b = k // 512
                    if b:
                        pe.wait_ge(sem("cnt"), b)
                    nc.tensor.matmul(ps_l[0][:, 0:w], upper[:], flat[:, k:k + w], start=True, stop=True)
                    nc.tensor.matmul(ps_l[1][:, 0:w], ones[:], flat[:, k:k + w], start=True,
                                     stop=True).then_inc(sem("ranked"), 1)

            @block.vector
            def _(dve):
                chain = [0]

                def link(ins):
                    chain[0] += 1
                    ins.then_inc(sem("chain"), 1)
                    dve.wait_ge(sem("chain"), chain[0])

                tt_, ts_ = nc.vector.tensor_tensor, nc.vector.tensor_scalar
                link(nc.vector.tensor_reduce(top[:], logit[:], AX.X, ALU.max))
                link(tt_(work[:], logit[:], per_token(top[:]), ALU.subtract))
                dve.wait_ge(sem("iota"), 1)
                link(ts_(hot[:], work[:], 0.0, None, ALU.is_equal))
                link(tt_(hot[:], hot[:], per_expert(idx_e[:]), ALU.mult))
                link(nc.vector.tensor_reduce(pick[:], hot[:], AX.X, ALU.min))
                nc.vector.tensor_copy(rank[:], per_expert(idx_e[:])).then_inc(sem("shifted"), 1)
                dve.wait_ge(sem("shifted"), 1)
                tt_(hot[:], rank[:], per_token(pick[:]), ALU.is_equal).then_inc(sem("hot"), 1)
                dve.wait_ge(sem("gate_exp"), 1)
                link(nc.vector.tensor_reduce(top[:], work[:], AX.X, ALU.add))
                link(nc.vector.reciprocal(best[:], top[:]))
                dve.wait_ge(sem("hot"), 1)
                W = TILES * NE
                rf, cf = (x[:, :, :].rearrange("p c e -> p (c e)") for x in (rank, count))
                for k in range(0, W, 512):
                    w = min(512, W - k)
                    dve.wait_ge(sem("ranked"), k // 512 + 1)
                    nc.vector.tensor_copy(rf[:, k:k + w], ps_l[0][:, 0:w])
                    last = nc.vector.tensor_copy(cf[:, k:k + w], ps_l[1][:, 0:w]).then_inc(sem("cnt"), 1)
                dve.wait_ge(sem("cnt"), (W + 511) // 512)
                for e in range(NE):
                    c = count[:, :, e]
                    last = nc.vector.tensor_tensor_scan(cum[:, e, :], c, c, 0.0, ALU.add, ALU.bypass)
                link(last)
                cv = cum[:, :, :].rearrange("p e c -> p c e")
                link(tt_(work[:], cv, count[:], ALU.subtract))
                link(tt_(rank[:], rank[:], work[:], ALU.add))
                link(ts_(tot_i[:], cum[:, :, TILES - 1], 127.0, None, ALU.add))
                link(ts_(tot_i[:], tot_i[:], 7, None, ALU.arith_shift_right))
                link(nc.vector.tensor_copy(tiles[:], tot_i[:]))
                link(nc.vector.tensor_tensor_scan(ends[:], tiles[:], tiles[:], 0.0, ALU.add, ALU.bypass))
                link(tt_(starts[:], ends[:], tiles[:], ALU.subtract))
                link(ts_(starts[:], starts[:], 128.0, None, ALU.mult))
                link(tt_(rank[:], rank[:], per_expert(starts[:]), ALU.add))
                link(tt_(rank[:], rank[:], hot[:], ALU.mult))
                link(nc.vector.tensor_reduce(pick[:], rank[:], AX.X, ALU.add))
                link(nc.vector.tensor_copy(dest[:], pick[:]))
                link(ts_(acc[0][:], slot_no[:], ends[0:1, 0:1], None, ALU.is_ge))
                for e in range(1, NE - 1):
                    link(nc.vector.scalar_tensor_tensor(acc[e % 2][:], slot_no[:], ends[0:1, e:e + 1],
                                                        acc[(e + 1) % 2][:], ALU.is_ge, ALU.add))
                link(nc.vector.tensor_copy(tile_expert[:], acc[(NE - 2) % 2][:]))

        with nc.Block() as block:
            @block.sync
            def _(sp):
                def load(k, p, half):
                    after(sp, sem(f"scattered{p}"), 16 * CT * half)
                    sp.dma_start(tok[p][:], t_dram[bass.ds(k * (CT * 128), CT * 128), :].rearrange(
                        "(c p) e -> p c e", p=128)).then_inc(sem(f"back{p}"), 16)
                chunks(sp, load)

            @block.gpsimd
            def _(pool):
                ids = [n.sb(f"ids{p}", [128, CT], U32) for p in range(2)]

                def chunk(k, p, half):
                    after(pool, sem(f"scattered{p}"), 16 * CT * half)
                    hold(pool, sem("pass"))
                    nc.gpsimd.tensor_copy(ids[p][:], dest[:, bass.ds(k * CT, CT)]).then_inc(sem("ids"), 1)
                    pool.wait_ge(sem("ids"), k + 1)
                    pool.wait_ge(sem(f"back{p}"), 16 * (half + 1))
                    hold(pool, sem("pass"))
                    for c in range(CT):
                        nc.gpsimd.indirect_dma_start(
                            sorted_dram[:, :], bass.IndirectOffsetOnAxis(ap=ids[p][:, c:c + 1], axis=0),
                            tok[p][:, c, :], None).then_inc(sem(f"scattered{p}"), 16)
                chunks(pool, chunk)
                pool.wait_ge(sem("scattered0"), 16 * CT * ((NC + 1) // 2))
                pool.wait_ge(sem("scattered1"), 16 * CT * (NC // 2))


def experts(nc, ident, sorted_dram, y_dram, w1, b1, w2, b2, tile_expert):
    FC = FF // 128
    with ExitStack() as ctx:
        n = Names(nc, ctx, "moe")
        sem = n.sem
        w1_sb = n.sb("w1", [128, NE * FF])
        b1_sb = n.sb("b1", [128, NE * FF])
        w2_sb = n.sb("w2", [128, NE * FC * E])
        b2_sb = n.sb("b2", [128, NE * E])
        xs = [n.sb(f"xs{p}", [128, E]) for p in range(2)]
        xt = [n.sb(f"xt{p}", [128, E]) for p in range(2)]
        pre = [n.sb(f"pre{p}", [128, FF]) for p in range(2)]
        hid = [n.sb(f"hid{p}", [128, FF]) for p in range(2)]
        hidT = [n.sb(f"hidT{p}", [128, FF]) for p in range(2)]
        ys = [n.sb(f"ys{p}", [128, E]) for p in range(2)]
        ps_x, ps_y = n.ps("x", [128, 512]), n.ps("y", [128, 512])
        ps_h = [n.ps(f"h{p}", [128, 512]) for p in range(2)]
        ps_t = [n.ps(f"t{p}", [128, 512]) for p in range(2)]
        with nc.Block() as block:
            @block.sync
            def _(sp):
                for dst, src in ((w1_sb, w1), (b1_sb, b1), (w2_sb, w2), (b2_sb, b2)):
                    sp.dma_start(dst[:], src).then_inc(sem("w"), 16)

                def load(s, p):
                    after(sp, sem("xT"), s - 1)
                    sp.dma_start(xs[p][:], sorted_dram[bass.ds(s * 128, 128), :]).then_inc(sem(f"load{p}"), 16)

                def store(s, p):
                    sp.wait_ge(sem("ys"), s + 1)
                    sp.dma_start(y_dram[bass.ds(s * 128, 128), :], ys[p][:]).then_inc(sem(f"store{p}"), 16)
                load(0, 0)
                load(1, 1)
                load(2, 0)
                store(0, 0)
                load(3, 1)
                store(1, 1)
                with sp.Fori(0, SLOTS // 2 - 2) as it:
                    for p in range(2):
                        load(it * 2 + (p + 4), p)
                        store(it * 2 + (p + 2), p)
                store(SLOTS - 2, 0)
                store(SLOTS - 1, 1)
                for p in range(2):
                    sp.wait_ge(sem(f"store{p}"), 16 * (SLOTS // 2))

            def expert_of(eng, s):
                return eng.value_load(tile_expert[0:1, bass.ds(s, 1)], min_val=0, max_val=NE - 1)

            @block.tensor
            def _(pe):
                pe.wait_ge(sem("w"), 64)

                def front(s, p, half):
                    pe.wait_ge(sem(f"load{p}"), 16 * (half + 1))
                    after(pe, sem("xt"), s)
                    nc.tensor.transpose(ps_x[:, 0:128], xs[p][:], ident[:]).then_inc(sem("xT"), 1)
                    e = expert_of(pe, s)
                    pe.wait_ge(sem("xt"), s + 1)
                    after(pe, sem("pre"), s - 1)
                    nc.tensor.matmul(ps_h[p][:], xt[p][:], w1_sb[:, bass.ds(e * FF, FF)], start=True,
                                     stop=True).then_inc(sem("h"), 1)

                def back(s, p):
                    pe.wait_ge(sem("gelu"), s + 1)
                    after(pe, sem("hT"), s - 1)
                    for f in range(FC):
                        last = nc.tensor.transpose(ps_t[p][:, f * 128:(f + 1) * 128], hid[p][:, f * 128:(f + 1) * 128],
                                                   ident[:])
                    last.then_inc(sem("ht"), 1)
                    e = expert_of(pe, s)
                    pe.wait_ge(sem("hT"), s + 1)
                    after(pe, sem("ys"), s)
                    for f in range(FC):
                        last = nc.tensor.matmul(ps_y[:, 0:E], hidT[p][:, f * 128:(f + 1) * 128],
                                                w2_sb[:, bass.ds(e * (FC * E) + f * E, E)], start=f == 0,
                                                stop=f == FC - 1)
                    last.then_inc(sem("y"), 1)
                front(0, 0, 0)
                front(1, 1, 0)
                back(0, 0)
                for p in range(2):
                    front(p + 2, p, 1)
                    back(p + 1, 1 - p)
                with pe.Fori(0, SLOTS // 2 - 2) as it:
                    for p in range(2):
                        front(it * 2 + (p + 4), p, it + 2)
                        back(it * 2 + (p + 3), 1 - p)
                back(SLOTS - 1, 1)

            @block.scalar
            def _(act):
                def step(s, p):
                    act.wait_ge(sem("pre"), s + 1)
                    after(act, sem("ht"), s - 1)
                    nc.scalar.activation(hid[p][:], pre[p][:], ACT.Gelu_apprx_tanh).then_inc(sem("gelu"), 1)
                for s in range(3):
                    step(s, s % 2)
                with act.Fori(0, SLOTS // 2 - 2) as it:
                    for p in range(2):
                        step(it * 2 + (p + 3), 1 - p)
                step(SLOTS - 1, 1)

            @block.vector
            def _(dve):
                dve.wait_ge(sem("w"), 64)

                def front(s, p):
                    dve.wait_ge(sem("xT"), s + 1)
                    after(dve, sem("h"), s - 1)
                    nc.vector.tensor_copy(xt[p][:], ps_x[:, 0:128]).then_inc(sem("xt"), 1)
                    e = expert_of(dve, s)
                    dve.wait_ge(sem("h"), s + 1)
                    after(dve, sem("gelu"), s - 1)
                    nc.vector.tensor_tensor(pre[p][:], ps_h[p][:], b1_sb[:, bass.ds(e * FF, FF)],
                                            ALU.add).then_inc(sem("pre"), 1)

                def back(s, p, half):
                    dve.wait_ge(sem("ht"), s + 1)
                    after(dve, sem("y"), s - 1)
                    nc.vector.tensor_copy(hidT[p][:], ps_t[p][:]).then_inc(sem("hT"), 1)
                    e = expert_of(dve, s)
                    dve.wait_ge(sem("y"), s + 1)
                    after(dve, sem(f"store{p}"), 16 * half)
                    nc.vector.tensor_tensor(ys[p][:], ps_y[:, 0:E], b2_sb[:, bass.ds(e * E, E)],
                                            ALU.add).then_inc(sem("ys"), 1)
                front(0, 0)
                front(1, 1)
                back(0, 0, 0)
                for p in range(2):
                    front(p + 2, p)
                    back(p + 1, 1 - p, p)
                with dve.Fori(0, SLOTS // 2 - 2) as it:
                    for p in range(2):
                        front(it * 2 + (p + 4), p)
                        back(it * 2 + (p + 3), 1 - p, it + (p + 1))
                back(SLOTS - 1, 1, SLOTS // 2 - 1)


def combine(nc, hT, ident, y_dram, dest, best, out):
    with ExitStack() as ctx:
        n = Names(nc, ctx, "comb")
        sem = n.sem
        ids = [n.sb(f"ids{p}", [128, CT], U32) for p in range(2)]
        rows = [n.sb(f"rows{p}", [128, CT, E]) for p in range(2)]
        hc = [n.sb(f"hc{p}", [128, CT * 128]) for p in range(2)]
        fin = [n.sb(f"fin{p}", [128, CT, E]) for p in range(2)]
        pr = [n.sb(f"pr{p}", [128, CT]) for p in range(2)]
        ps = [n.ps(f"ps{p}", [128, 512]) for p in range(2)]
        with nc.Block() as block:
            @block.gpsimd
            def _(pool):
                def chunk(k, p, half):
                    after(pool, sem("fin"), CT * (k - 1))
                    hold(pool, sem("pass"))
                    nc.gpsimd.tensor_copy(ids[p][:], dest[:, bass.ds(k * CT, CT)]).then_inc(sem("ids"), 1)
                    pool.wait_ge(sem("ids"), k + 1)
                    hold(pool, sem("pass"))
                    for c in range(CT):
                        nc.gpsimd.indirect_dma_start(
                            rows[p][:, c, :], None, y_dram[:, :],
                            bass.IndirectOffsetOnAxis(ap=ids[p][:, c:c + 1], axis=0)).then_inc(sem(f"rows{p}"), 16)
                chunks(pool, chunk)

            @block.scalar
            def _(act):
                def chunk(k, p, half):
                    after(act, sem("turned"), CT * (k - 1))
                    nc.scalar.activation(hc[p][:], hT[:, bass.ds(k * (CT * 128), CT * 128)], ACT.Copy
                                         ).then_inc(sem("hc"), 1)
                chunks(act, chunk)

            @block.tensor
            def _(pe):
                def chunk(k, p, half):
                    pe.wait_ge(sem("hc"), k + 1)
                    for c in range(CT):
                        after(pe, sem("fin"), k * CT + (c - 1))
                        nc.tensor.transpose(ps[(p * CT + c) % 2][:, 0:128], hc[p][:, c * 128:(c + 1) * 128],
                                            ident[:]).then_inc(sem("turned"), 1)
                chunks(pe, chunk)

            @block.vector
            def _(dve):
                def chunk(k, p, half):
                    after(dve, sem(f"store{p}"), 16 * half)
                    dve.wait_ge(sem(f"rows{p}"), 16 * CT * (half + 1))
                    nc.vector.tensor_copy(pr[p][:], best[:, bass.ds(k * CT, CT)]).then_inc(sem("pr"), 1)
                    dve.wait_ge(sem("pr"), k + 1)
                    for c in range(CT):
                        dve.wait_ge(sem("turned"), k * CT + (c + 1))
                        nc.vector.scalar_tensor_tensor(fin[p][:, c, :], rows[p][:, c, :], pr[p][:, c:c + 1],
                                                       ps[(p * CT + c) % 2][:, 0:128], ALU.mult,
                                                       ALU.add).then_inc(sem("fin"), 1)
                chunks(dve, chunk)

            @block.sync
            def _(sp):
                def chunk(k, p, half):
                    sp.wait_ge(sem("fin"), CT * (k + 1))
                    sp.dma_start(out[bass.ds(k * (CT * 128), CT * 128), :].rearrange("(c p) e -> p c e", p=128),
                                 fin[p][:]).then_inc(sem(f"store{p}"), 16)
                chunks(sp, chunk)
                sp.wait_ge(sem("store0"), 16 * ((NC + 1) // 2))
                sp.wait_ge(sem("store1"), 16 * (NC // 2))


def tower(nc, a, out):
    scratch = nc.dram_tensor("qk_parts", [2, 2 * PARTS, 128, 2 * TP], BF16).ap()
    rows_dram = nc.dram_tensor("tok_rows", [2, T, E], F32).ap()
    tT_dram = nc.dram_tensor("t_features", [E, NT], F32).ap()
    t_dram = nc.dram_tensor("t_tokens", [NT, E], F32).ap()
    sorted_dram = nc.dram_tensor("t_sorted", [SLOTS * 128, E], F32).ap()
    y_dram = nc.dram_tensor("y_sorted", [SLOTS * 128, E], F32).ap()
    with ExitStack() as ctx:
        hT = ctx.enter_context(nc.sbuf_tensor("hT", [128, NT], F32))
        ident = ctx.enter_context(nc.sbuf_tensor("ident", [128, 128], F32))
        ld = ctx.enter_context(nc.semaphore("ident_loaded"))
        with nc.Block() as block:
            @block.sync
            def _(sp):
                sp.dma_start(ident[:], a["ident"]).then_inc(ld, 16)
                sp.wait_ge(ld, 16)
        patch_tokens(nc, hT, ident, a["ximg"], a["xblk"], a["xpatch"], a["gam"], a["bet"], a["wtok"], a["btok"],
                     rows_dram)
        mats = (a["sel_num"], a["sel_den"], a["mean_w"])
        attention(nc, hT, ident, mats, (a["lsh_wq"], a["lsh_wv"], a["lsh_hyp"]), a["lsh_cols"], scratch, True, None)
        attention(nc, hT, ident, mats, (a["att_wq"], a["att_wv"], a["att_wk"], a["att_wo"]), a["att_cols"], scratch,
                  False, tT_dram)
        with ExitStack() as tail:
            dest = tail.enter_context(nc.sbuf_tensor("dest", [128, TILES], U32))
            best = tail.enter_context(nc.sbuf_tensor("best", [128, TILES], F32))
            tile_expert = tail.enter_context(nc.sbuf_tensor("tile_expert", [1, SLOTS], I32))
            logit = tail.enter_context(nc.sbuf_tensor("logit", [128, TILES, NE], F32))
            route(nc, hT, ident, tT_dram, t_dram, sorted_dram, a["gate_w"], a["gate_b"], a["prefix_w"], logit, dest,
                  best, tile_expert)
            experts(nc, ident, sorted_dram, y_dram, a["w1"], a["b1"], a["w2"], a["b2"], tile_expert)
            combine(nc, hT, ident, y_dram, dest, best, out)


def constants():
    num, den = np.zeros((128, 2, E), np.float32), np.zeros((128, 2, E), np.float32)
    for h in range(H):
        g, s = h // 4, h % 4
        for d in range(D):
            num[32 * s + d, g, h * D + d] = 1.0
            den[32 * s + D, g, h * D + d] = 1.0
    return {"sel_num": num, "sel_den": den, "mean_w": np.full((128, 128), 1.0 / E, np.float32),
            "ident": np.eye(128, dtype=np.float32), "prefix_w": np.triu(np.ones((128, 128), np.float32), 1)}


def layout(v):
    x = v["x"]
    wide = np.pad(x, ((0, 0), (0, 0), (HP, HP), (HP, HP)))

    def blocks(z, k):
        return z.reshape(IMG, CH, k, PATCH, k, PATCH).transpose(1, 3, 5, 2, 4, 0).reshape(E, k, k, IMG)

    def patches(z):
        return z.reshape(SRC, CH, GRID, PATCH, GRID, PATCH).transpose(1, 3, 5, 0, 2, 4).reshape(E, SRC, T)

    def columns(*arrays):
        c = np.zeros((E, 8), np.float32)
        for k, z in enumerate(arrays):
            c[:, k] = z
        return c
    hp = v["L0_attn_hyperplanes"]
    hyp, hyp_b = np.zeros((E, E), np.float32), np.zeros(E, np.float32)
    for h in range(H):
        hyp[h * D:(h + 1) * D, h * D:h * D + hp.shape[1]] = hp[:D]
        hyp_b[h * D:h * D + hp.shape[1]] = hp[D]
    W1, W2 = v["L0_ffn_W1"], v["L0_ffn_W2"]
    return {
        "ximg": x.reshape(IMG, 8, -1), "xblk": blocks(wide, NBLK), "xpatch": blocks(x, GRID),
        "gam": patches(v["L0_tok_gamma"]), "bet": patches(v["L0_tok_beta"]),
        "wtok": v["L0_tok_W"].reshape(E, SRC, CH, PATCH, PATCH).transpose(2, 3, 4, 1, 0).reshape(E, SRC, E),
        "btok": v["L0_tok_b"].reshape(1, E),
        "lsh_wq": v["L0_attn_Wq"], "lsh_wv": v["L0_attn_Wv"], "lsh_hyp": hyp,
        "lsh_cols": columns(v["L0_attn_bq"], hyp_b, v["L0_attn_bv"]),
        "att_wq": v["L0_ffn_Wq"], "att_wv": v["L0_ffn_Wv"], "att_wk": v["L0_ffn_Wk"], "att_wo": v["L0_ffn_Wo"],
        "att_cols": columns(*(v["L0_ffn_" + k] for k in ("bq", "bk", "bv", "bo", "ln1_g", "ln1_b"))),
        "gate_w": v["L0_ffn_gate_W"], "gate_b": np.broadcast_to(v["L0_ffn_gate_b"], (128, NE)),
        "w1": W1.transpose(1, 0, 2).reshape(E, NE * FF),
        "b1": np.broadcast_to(v["L0_ffn_b1"].reshape(1, -1), (128, NE * FF)),
        "w2": W2.reshape(NE, FF // 128, 128, E).transpose(2, 0, 1, 3).reshape(128, -1),
        "b2": np.broadcast_to(v["L0_ffn_b2"].reshape(1, -1), (128, NE * E)),
        **constants(),
    }


def kernel(**inputs):
    from concourse import bacc
    from concourse.bass_utils import run_bass_kernel_spmd

    nc = bacc.Bacc("TRN2", target_bir_lowering=False, num_devices=1)
    arrays = {k: np.ascontiguousarray(z) for k, z in layout({k: np.asarray(z) for k, z in inputs.items()}).items()}
    args = {k: nc.dram_tensor("in_" + k, z.shape, mybir.dt.from_np(z.dtype), kind="ExternalInput").ap()
            for k, z in arrays.items()}
    out = nc.dram_tensor("out", (NT, E), F32, kind="ExternalOutput").ap()
    tower(nc, args, out)
    result = run_bass_kernel_spmd(nc, [{"in_" + k: z for k, z in arrays.items()}], core_ids=[0])
    return result.results[0]["out"].reshape(IMG, T, E)
```

```python
from contextlib import ExitStack

import concourse.bass as bass
import numpy as np
from concourse import mybir

F32 = mybir.dt.float32
BF16 = mybir.dt.bfloat16
I32 = mybir.dt.int32
U32 = mybir.dt.uint32
ALU = mybir.AluOpType
ACT = mybir.ActivationFunctionType
AX = mybir.AxisListType

IMG, CH, SIDE, HP, PATCH = 128, 2, 104, 4, 8
GRID = SIDE // PATCH
T = GRID * GRID
NBLK = GRID + 1
E = 128
H, D = 8, 16
SRC = 5
PAIRS = IMG // 2
N2 = 2 * T
TP = 192
REM = T - 128
NT = IMG * T
TILES = NT // 128
NE, FF = 8, 512
SLOTS = TILES + NE - 1
CT = 13
NC = TILES // CT
EPS_TOK, EPS_LN = 1e-7, 1e-5


def after(eng, sem, value):
    if isinstance(value, int) and value <= 0:
        return
    eng.wait_ge(sem, value)


RSQRT_MAGIC = float(0x5F3759DF)
RSQRT_OPS = 11
NEWTON_OPS = 12


def rsqrt(nc, eng, sem, before, v, y, t, bits):
    ops = nc.vector
    done = 0

    def link(ins):
        nonlocal done
        done += 1
        ins.then_inc(sem, 1)
        eng.wait_ge(sem, before + done)
    link(ops.tensor_scalar(bits, v.bitcast(I32), 1, None, ALU.arith_shift_right))
    link(ops.tensor_scalar(y.bitcast(I32), bits, -1.0, RSQRT_MAGIC, ALU.mult, ALU.add))
    for _ in range(3):
        link(ops.tensor_tensor(t, y, y, ALU.mult))
        link(ops.scalar_tensor_tensor(t, t, -0.5, v, ALU.mult, ALU.mult))
        link(ops.scalar_tensor_tensor(y, t, 1.5, y, ALU.add, ALU.mult))
    assert done == RSQRT_OPS


def hold(pool, passed):
    pool.sem_inc(passed, 1)


class Names:

    def __init__(self, nc, ctx, stage):
        self.nc, self.ctx, self.stage, self.sems = nc, ctx, stage, {}

    def sem(self, name):
        if name not in self.sems:
            self.sems[name] = self.ctx.enter_context(self.nc.semaphore(f"{self.stage}_{name}"))
        return self.sems[name]

    def clear(self):
        with self.nc.Block() as block:
            @block.gpsimd
            def _(pool):
                for s in self.sems.values():
                    pool.sem_clear(s)

    def sb(self, name, shape, dt=F32):
        return self.ctx.enter_context(self.nc.sbuf_tensor(f"{self.stage}_{name}", shape, dt))

    def ps(self, name, shape, dt=F32):
        return self.ctx.enter_context(self.nc.psum_tensor(f"{self.stage}_{name}", shape, dt))


def patch_tokens(nc, hT, ident, ximg, xblk, xpatch, gam, bet, wtok, btok, rows_dram):
    NCH = 8
    RC = CH * SIDE // NCH
    NALL = 2 * SRC * SIDE * SIDE
    INN = SIDE - 2 * HP
    WSUM = CH * (2 * SIDE * SIDE + 2 * INN * SIDE + INN * INN)
    with ExitStack() as ctx:
        n = Names(nc, ctx, "tok")
        sem = n.sem
        xi = n.sb("xi", [128, NCH, RC * SIDE])
        sq = n.sb("sq", [128, 2, RC * SIDE])
        gam_sb = n.sb("gam", [128, SRC, T])
        bet_sb = n.sb("bet", [128, SRC, T])
        w_sb = n.sb("w", [128, SRC, E])
        b_row = n.sb("b_row", [1, E])
        one_row = n.sb("one_row", [1, T])
        rall = n.sb("rall", [128, CH * SIDE])
        redge = n.sb("redge", [128, CH * SIDE])
        st = n.sb("st", [128, 12])
        bits = n.sb("bits", [128, 1], I32)
        ms = n.sb("ms", [128, 2])
        msT = n.sb("msT", [2, 128])
        rwide = n.sb("rwide", [128, 128])
        rb = n.sb("rb", [128, 128])
        gb_sb = n.sb("gb_sb", [128, 2, 2, E])
        psg = n.ps("psg", [128, 2, 2, 128])
        psm = n.ps("psm", [128, 512])

        with nc.Block() as block:
            @block.sync
            def _(sp):
                sp.dma_start(w_sb[:], wtok).then_inc(sem("w"), 16)
                sp.dma_start(gam_sb[:], gam).then_inc(sem("w"), 16)
                sp.dma_start(bet_sb[:], bet).then_inc(sem("w"), 16)
                sp.dma_start(b_row[:], btok).then_inc(sem("w"), 16)
                for c in range(NCH):
                    sp.dma_start(xi[:, c, :], ximg[:, c, :]).then_inc(sem(f"x{c}"), 16)
                sp.wait_ge(sem("gb"), 1)
                for r in range(2):
                    sp.dma_start(rows_dram[r, 0:128, :], gb_sb[:, 0, r, :]).then_inc(sem("rows"), 16)
                    sp.dma_start(rows_dram[r, 128:T, :], gb_sb[0:REM, 1, r, :]).then_inc(sem("rows"), 16)
                sp.wait_ge(sem("rows"), 64)

            @block.tensor
            def _(pe):
                pe.wait_ge(sem("w"), 64)
                pe.wait_ge(sem("ones"), 1)
                for tt, (t0, m) in enumerate(((0, 128), (128, REM))):
                    for s in range(SRC):
                        nc.tensor.matmul(psg[0:m, tt, 0, :], gam_sb[:, s, t0:t0 + m], w_sb[:, s, :],
                                         start=s == 0, stop=s == SRC - 1)
                    for s in range(SRC):
                        nc.tensor.matmul(psg[0:m, tt, 1, :], bet_sb[:, s, t0:t0 + m], w_sb[:, s, :],
                                         start=s == 0, stop=False)
                    last = nc.tensor.matmul(psg[0:m, tt, 1, :], one_row[:, t0:t0 + m], b_row[:],
                                            start=False, stop=True)
                last.then_inc(sem("g"), 1)
                pe.wait_ge(sem("ms"), 1)
                nc.tensor.matmul(psm[0:2, 0:128], ms[:], ident[:], start=True, stop=True)
                nc.tensor.matmul(psm[:, 128:256], rwide[:], ident[:], start=True, stop=True).then_inc(sem("mt"), 1)

            @block.scalar
            def _(act):
                act.wait_ge(sem("mean"), 1)
                for c in range(NCH):
                    if c >= 2:
                        act.wait_ge(sem("sqread"), c - 1)
                    nc.scalar.activation(sq[:, c % 2, :], xi[:, c, :], ACT.Square,
                                         bias=st[:, 4:5]).then_inc(sem("sq"), 1)

            @block.vector
            def _(dve):
                chain = [0]

                def link(ins):
                    chain[0] += 1
                    ins.then_inc(sem("chain"), 1)
                    dve.wait_ge(sem("chain"), chain[0])

                nc.vector.memset(one_row[:], 1.0).then_inc(sem("ones"), 1)

                def total(src, dst):
                    for c in range(CH):
                        base = c * SIDE
                        link(nc.vector.tensor_reduce(st[:, 0:1], rall[:, base:base + SIDE], AX.X, ALU.add))
                        link(nc.vector.tensor_reduce(st[:, 1:2], rall[:, base + HP:base + SIDE - HP], AX.X, ALU.add))
                        link(nc.vector.tensor_reduce(st[:, 2:3], redge[:, base:base + SIDE], AX.X, ALU.add))
                        link(nc.vector.tensor_reduce(st[:, 3:4], redge[:, base + HP:base + SIDE - HP], AX.X, ALU.add))
                        link(nc.vector.tensor_scalar(st[:, 0:1], st[:, 0:1], 3.0, None, ALU.mult))
                        link(nc.vector.scalar_tensor_tensor(st[:, 0:1], st[:, 1:2], 2.0, st[:, 0:1], ALU.mult, ALU.add))
                        link(nc.vector.tensor_tensor(st[:, 0:1], st[:, 0:1], st[:, 2:3], ALU.subtract))
                        link(nc.vector.tensor_tensor(st[:, 5 + c:6 + c], st[:, 0:1], st[:, 3:4], ALU.subtract))
                    link(nc.vector.tensor_tensor(dst, st[:, 5:6], st[:, 6:7], ALU.add))

                def rows(c, src):
                    v = src.rearrange("p (r c) -> p r c", c=SIDE)
                    nc.vector.tensor_reduce(rall[:, c * RC:(c + 1) * RC], v, AX.X, ALU.add)
                    edges = v.rearrange("p r (a b) -> p r a b", b=HP)[:, :, 0:SIDE // HP:SIDE // HP - 1, :]
                    return nc.vector.tensor_reduce(redge[:, c * RC:(c + 1) * RC], edges, AX.XY, ALU.add)

                for c in range(NCH):
                    dve.wait_ge(sem(f"x{c}"), 16)
                    last = rows(c, xi[:, c, :])
                link(last)
                total(None, st[:, 7:8])
                link(nc.vector.tensor_scalar(ms[:, 0:1], st[:, 7:8], 1.0 / NALL, None, ALU.mult))
                nc.vector.tensor_scalar(st[:, 4:5], ms[:, 0:1], -1.0, None, ALU.mult).then_inc(sem("mean"), 1)
                for c in range(NCH):
                    dve.wait_ge(sem("sq"), c + 1)
                    last = rows(c, sq[:, c % 2, :]).then_inc(sem("sqread"), 1)
                dve.wait_ge(sem("sqread"), NCH)
                total(None, st[:, 7:8])
                link(nc.vector.tensor_tensor(st[:, 10:11], ms[:, 0:1], ms[:, 0:1], ALU.mult))
                link(nc.vector.scalar_tensor_tensor(st[:, 8:9], st[:, 10:11], float(NALL - WSUM), st[:, 7:8],
                                                    ALU.mult, ALU.add))
                link(nc.vector.tensor_scalar(st[:, 8:9], st[:, 8:9], 1.0 / NALL, EPS_TOK, ALU.mult, ALU.add))
                rsqrt(nc, dve, sem("rsqrt"), 0, st[:, 8:9], st[:, 9:10], st[:, 11:12], bits[:])
                link(nc.vector.tensor_tensor(ms[:, 1:2], st[:, 8:9], st[:, 9:10], ALU.mult))
                dve.wait_ge(sem("g"), 1)
                for tt, m in enumerate((128, REM)):
                    nc.vector.tensor_scalar(gb_sb[0:m, tt, 0, :], psg[0:m, tt, 0, :], -1.0, None, ALU.mult)
                    last = nc.vector.tensor_copy(gb_sb[0:m, tt, 1, :], psg[0:m, tt, 1, :])
                last.then_inc(sem("gb"), 1)
                link(nc.vector.memset(rwide[:], 1.0))
                nc.vector.tensor_scalar(rwide[:], rwide[:], st[:, 9:10], None, ALU.mult).then_inc(sem("ms"), 1)
                dve.wait_ge(sem("mt"), 1)
                nc.vector.tensor_copy(msT[:], psm[0:2, 0:128])
                nc.vector.tensor_copy(rb[:], psm[:, 128:256])

        NW = 4
        ring = xi[:, :, :].rearrange("p a b -> p (a b)")
        XB = NBLK * IMG
        XP = GRID * IMG
        blk = [ring[:, r * XB:(r + 1) * XB].rearrange("p (j b) -> p j b", b=IMG) for r in range(4)]
        pat = [ring[:, 4 * XB + r * XP:4 * XB + (r + 1) * XP].rearrange("p (j b) -> p j b", b=IMG) for r in range(2)]
        off = 4 * XB + 2 * XP
        wg = [ring[:, off + r * SRC * E:off + (r + 1) * SRC * E].rearrange("p (s e) -> p s e", e=E) for r in range(NW)]
        off += NW * SRC * E
        gbr = [ring[0:2, off + r * GRID * E:off + (r + 1) * GRID * E] for r in range(2)]
        hv = hT[:, :].rearrange("p (b t) -> p b t", t=T)
        NB = 5
        pst = [n.ps(f"pst{k}", [128, 512]) for k in range(NB)]

        pools = [j for j in range(GRID) if j % 3 == 2]
        dves = [j for j in range(GRID) if j % 3 != 2]

        with nc.Block() as block:
            @block.sync
            def _(sp):
                sp.dma_start(blk[0], xblk[:, 0]).then_inc(sem("blk_first"), 16)

                def load(i, par):
                    after(sp, sem("done"), (i - 1) * GRID)
                    sp.dma_start(blk[(par + 1) % 4], xblk[:, bass.ds(i + 1, 1)]).then_inc(sem(f"blk{par % 2}"), 16)
                    sp.dma_start(pat[par % 2], xpatch[:, bass.ds(i, 1)]).then_inc(sem(f"blk{par % 2}"), 16)
                    sp.dma_start(gbr[par % 2], rows_dram[:, bass.ds(i * GRID, GRID), :].rearrange(
                        "r t e -> r (t e)")).then_inc(sem(f"blk{par % 2}"), 16)

                for i in range(5):
                    load(i, i)
                with sp.Fori(0, 2) as it:
                    for par in range(4):
                        load(it * 4 + (par + 5), par + 1)

            @block.gpsimd
            def _(pool):
                def row(i, par):
                    for j in pools:
                        after(pool, sem("done"), i * GRID + (j - NW + 1))
                        nc.gpsimd.tensor_tensor(wg[(par * GRID + j) % NW], w_sb[:, :, :],
                                                gam_sb[:, :, bass.ds(i * GRID + j, 1)].broadcast_to([128, SRC, E]),
                                                ALU.mult).then_inc(sem("wpool"), 1)
                row(0, 0)
                with pool.Fori(0, 3) as it:
                    for par in range(4):
                        row(it * 4 + par + 1, par + 1)

            @block.vector
            def _(dve):
                def evac(i, par, j):
                    dve.wait_ge(sem("done"), i * GRID + j + 1)
                    nc.vector.tensor_tensor(hv[:, :, bass.ds(i * GRID + j, 1)].rearrange("p b t -> p (b t)"),
                                            pst[j % NB][:, 0:IMG], rb[:], ALU.mult).then_inc(sem("out"), 1)

                def row(i, par):
                    for j in range(GRID):
                        if j in dves:
                            after(dve, sem("done"), i * GRID + (j - NW + 1))
                            nc.vector.tensor_tensor(wg[(par * GRID + j) % NW], w_sb[:, :, :],
                                                    gam_sb[:, :, bass.ds(i * GRID + j, 1)].broadcast_to([128, SRC, E]),
                                                    ALU.mult).then_inc(sem("wdve"), 1)
                        if j >= 2:
                            evac(i, par, j - 2)
                    evac(i, par, GRID - 2)
                    evac(i, par, GRID - 1)
                row(0, 0)
                with dve.Fori(0, 3) as it:
                    for par in range(4):
                        row(it * 4 + par + 1, par + 1)

            @block.tensor
            def _(pe):
                def row(i, par, half):
                    pe.wait_ge(sem(f"blk{par % 2}"), 48 * (half + 1))
                    for j in range(GRID):
                        if j in pools:
                            pe.wait_ge(sem("wpool"), i * len(pools) + pools.index(j) + 1)
                        else:
                            pe.wait_ge(sem("wdve"), i * len(dves) + dves.index(j) + 1)
                        after(pe, sem("out"), i * GRID + (j - NB + 1) if j >= NB else i * GRID)
                        w = wg[(par * GRID + j) % NW]
                        acc = pst[j % NB][:, 0:IMG]
                        top, low = blk[par % 4], blk[(par + 1) % 4]
                        for s, x in enumerate((pat[par % 2][:, j, :], low[:, j, :], low[:, j + 1, :],
                                               top[:, j, :], top[:, j + 1, :])):
                            nc.tensor.matmul(acc, w[:, s, :], x, start=s == 0, stop=False)
                        nc.tensor.matmul(acc, gbr[par % 2][:, j * E:(j + 1) * E], msT[:], start=False,
                                         stop=True).then_inc(sem("done"), 1)
                pe.wait_ge(sem("blk_first"), 16)
                row(0, 0, 0)
                with pe.Fori(0, 3) as it:
                    for par in range(4):
                        row(it * 4 + par + 1, par + 1, it * 2 + (par + 1) // 2)
        n.clear()


PARTS = 3
Q_OF = (0, 0, 1, 1, 0, 2)
K_OF = (0, 1, 0, 1, 2, 0)
KQ = len(Q_OF) * D
KB = KQ + D
UNITS = 8


def attention(nc, hT, ident, mats, weights, cols, scratch, lsh, tT_dram):
    stage = "lsh" if lsh else "att"
    scale = 1.0 / float(np.sqrt(E)) if lsh else 0.25
    NSIDE = 1 if lsh else 2
    NP = PARTS + 1 if lsh else 2 * PARTS
    LOADS = (2 * len(Q_OF) + 2) if lsh else 2 * len(Q_OF)
    with ExitStack() as ctx:
        n = Names(nc, ctx, stage)
        sem = n.sem
        wq = n.sb("wq", [128, E])
        wv = n.sb("wv", [128, E])
        wk = n.sb("wk", [128, E]) if not lsh else None
        wo = n.sb("wo", [128, E]) if not lsh else None
        hyp = n.sb("hyp", [128, E]) if lsh else None
        col = n.sb("col", [128, 8])
        sel_num = n.sb("sel_num", [128, 2, E])
        sel_den = n.sb("sel_den", [128, 4])
        mean_w = n.sb("mean_w", [128, 128])
        cent = n.sb("cent", [128, N2])
        sqr = n.sb("sqr", [128, N2])
        var, vneg, rstd, nwt, half3 = (n.sb(x, [128, 4]) for x in ("var", "vneg", "rstd", "nwt", "half3"))
        nbits = n.sb("nbits", [128, 4], I32)
        NXH = 2 if lsh else 4
        xh = [n.sb(f"xh{p}", [128, N2]) for p in range(NXH)]
        qf = n.sb("qf", [128, N2])
        kf = n.sb("kf", [128, N2]) if not lsh else None
        rst = n.sb("rst", [128, N2])
        att = n.sb("att", [128, N2])
        prj = n.sb("prj", [128, N2]) if lsh else None
        parts = n.sb("parts", [128, NP, 2 * TP], BF16)
        qs = [n.sb(f"qs{p}", [KB, H, 2 * TP], BF16) for p in range(2)]
        ks = [n.sb(f"ks{p}", [KB, H, 2 * TP], BF16) for p in range(2)]
        kb = [n.sb(f"kb{p}", [KB, H, 2 * TP], BF16) for p in range(2)] if lsh else None
        vm = [n.sb(f"vm{p}", [128, 2, H, 32]) for p in range(2)]
        vr = [n.sb(f"vr{p}", [128, 2, H, 32]) for p in range(2)]
        fac = [n.sb(f"fac{p}", [128, 3 * T], BF16) for p in range(2)] if lsh else None
        scr = [n.sb(f"scr{p}", [128, 3 * T]) for p in range(2)] if lsh else None
        mx = [n.sb(f"mx{p}", [128, 3]) for p in range(2)]
        nm = [n.sb(f"nm{p}", [128, 3]) for p in range(2)]
        prob = [n.sb(f"prob{p}", [128, 3 * T]) for p in range(2)]
        ptm = [n.sb(f"ptm{p}", [128, 2 * TP]) for p in range(2)]
        ptr = [n.sb(f"ptr{p}", [128, 2 * TP]) for p in range(2)]
        osb = n.sb("osb", [128, 2, N2])
        num = n.sb("num", [128, N2])
        rec = n.sb("rec", [128, 4, H])
        rec_wide = n.sb("rec_wide", [128, 4, E])
        if not lsh:
            oh, yy, cent2, sqr2, nrm2, tt = (n.sb(x, [128, N2]) for x in ("oh", "yy", "cent2", "sqr2", "nrm2", "tt"))
            var2, vneg2, rstd2 = (n.sb(x, [128, 4]) for x in ("var2", "vneg2", "rstd2"))
        g0, g1 = n.ps("g0", [128, 512]), n.ps("g1", [128, 512])
        ps_s = [n.ps("s0", [128, 512])]
        ps_f = n.ps("f", [128, 512]) if lsh else None
        if not lsh:
            ps_s.append(n.ps("s1", [128, 512]))
        NS = len(ps_s)
        ps_tm, ps_tr = n.ps("tm", [128, 512]), n.ps("tr", [128, 512])
        ps_o = [n.ps(f"o{g}", [128, 512]) for g in range(2)]

        CONST = len(weights) + 4

        def consts(eng):
            eng.wait_ge(sem("const"), 16 * CONST)
            eng.wait_ge(sem("zero"), 1)

        def parts_made(eng, pairs_done):
            if lsh:
                after(eng, sem("parts"), pairs_done)
            else:
                after(eng, sem("split"), 4 * NSIDE * pairs_done)

        def both(ap):
            return ap.rearrange("p (i t) -> p i t", t=TP)[:, :, 0:T]

        def two(ap):
            return ap.rearrange("p (i t) -> p i t", t=T)

        def h_of(i):
            return hT[:, bass.ds(i * N2, N2)]

        UNROLL = 2 if lsh else 4

        def pairs(eng, head, step):
            head()
            step(0, 0, 0)
            step(1, 1, 0)
            with eng.Fori(0, (PAIRS - 4) // UNROLL) as it:
                for k in range(UNROLL):
                    step(it * UNROLL + (2 + k), (2 + k) % 4, it * (UNROLL // 2) + (2 + k) // 2)
            step(PAIRS - 2, (PAIRS - 2) % 4, (PAIRS - 2) // 2)
            step(PAIRS - 1, (PAIRS - 1) % 4, (PAIRS - 1) // 2)

        def is_last(i, k):
            return isinstance(i, int) and i + k >= PAIRS

        def first(i):
            return isinstance(i, int) and i == 0

        with nc.Block() as block:
            @block.sync
            def _(sp):
                for dst, src in zip((wq, wv, hyp) if lsh else (wq, wv, wk, wo), weights):
                    sp.dma_start(dst[:], src).then_inc(sem("const"), 16)
                sp.dma_start(col[:], cols).then_inc(sem("const"), 16)
                sp.dma_start(sel_num[:], mats[0]).then_inc(sem("const"), 16)
                sp.dma_start(sel_den[:], mats[1]).then_inc(sem("const"), 16)
                sp.dma_start(mean_w[:], mats[2]).then_inc(sem("const"), 16)
                sp.wait_ge(sem("zero"), 1)

                def stack(i, par):
                    parts_made(sp, i + 1)
                    sp.dma_start(scratch[par, 0:NP].rearrange("s p t -> p s t"), parts[:]).then_inc(sem("store"), 16)
                    sp.wait_ge(sem("store"), 16 * (i + 1))
                    after(sp, sem("s"), UNITS * (i - 1))
                    if lsh:
                        after(sp, sem("f"), UNITS * (i - 1))

                    def load(dst, row, part):
                        sp.dma_start(dst[row:row + D], scratch[par, part].rearrange(
                            "(h d) t -> d h t", d=D)).then_inc(sem(f"load{par}"), 16)
                    for j, (a, b) in enumerate(zip(Q_OF, K_OF)):
                        load(qs[par], j * D, a)
                        load(ks[par], j * D, b if lsh else b + PARTS)
                    if lsh:
                        load(qs[par], KQ, PARTS)
                        load(kb[par], KQ, PARTS)

                def head():
                    stack(0, 0)
                    stack(1, 1)

                def step(i, m, half):
                    if not is_last(i, 2):
                        stack(i + 2, m % 2)
                    if not lsh and not first(i) and not first(i - 1):
                        sp.wait_ge(sem("tt"), i - 1)
                        sp.dma_start(tT_dram[:, bass.ds((i - 2) * N2, N2)], tt[:]).then_inc(sem("out"), 16)
                pairs(sp, head, step)
                if not lsh:
                    for i in (PAIRS - 2, PAIRS - 1):
                        sp.wait_ge(sem("tt"), i + 1)
                        sp.dma_start(tT_dram[:, i * N2:(i + 1) * N2], tt[:]).then_inc(sem("out"), 16)
                    sp.wait_ge(sem("out"), 16 * PAIRS)

            @block.tensor
            def _(pe):
                mm = nc.tensor.matmul
                reader = [None, None]

                def bank(b, i, name, m, c):
                    if reader[b]:
                        pe.wait_ge(sem(reader[b][0]), i * reader[b][1] + reader[b][2])
                    reader[b] = (name, m, c)
                    return (g0, g1)[b]

                def next_step():
                    for b in range(2):
                        if reader[b]:
                            name, m, c = reader[b]
                            reader[b] = (name, m, c - m)

                def mean(i, b):
                    g = bank(b, i, "cent", 1, 3)
                    mm(g[:, 0:N2], mean_w[:], h_of(i + 2), start=True, stop=True).then_inc(sem("mean"), 1)

                def token_means(g, x):
                    for im in range(2):
                        for k, t0 in enumerate((im * T, im * T + REM)):
                            last = mm(g[:, 2 * im + k:2 * im + k + 1], x[:, t0:t0 + 128], mean_w[:, 0:1],
                                      start=True, stop=True)
                    return last

                def spread(g, column):
                    for im in range(2):
                        mm(g[:, im * T:im * T + 128], column(2 * im), ident[:], start=True, stop=True)
                        last = mm(g[:, im * T + 128:(im + 1) * T], column(2 * im + 1), ident[:, 128 - REM:128],
                                  start=True, stop=True)
                    return last

                def same(x):
                    return lambda c: x[:, c:c + 1].broadcast_to([128, 128])

                def variance(i, b):
                    g = bank(b, i, "vcp", 1, 3)
                    pe.wait_ge(sem("sq"), i + 3)
                    token_means(g, sqr).then_inc(sem("var"), 1)

                def deviation(i, b):
                    g = bank(b, i, "xh", 1, 3)
                    pe.wait_ge(sem("rs"), NEWTON_OPS * (i + 3))
                    spread(g, same(rstd)).then_inc(sem("rbc"), 1)

                def project(w, i, m, b, name, name_read):
                    g = bank(b, i, name_read, 1, 3)
                    pe.wait_ge(sem("xh"), i + 3)
                    mm(g[:, 0:N2], w[:], xh[(m + 2) % NXH][:], start=True, stop=True).then_inc(sem(name), 1)

                def hyperplanes(i, b):
                    g = bank(b, i, "prc", 1, 3)
                    pe.wait_ge(sem("qf"), i + 3)
                    mm(g[:, 0:N2], hyp[:], qf[:], start=True, stop=True).then_inc(sem("pr"), 1)

                def values(i, m, b):
                    g = bank(b, i, "v_copied", 1, 2)
                    pe.wait_ge(sem("xh"), i + 2)
                    for im in range(2):
                        x = xh[(m + 1) % NXH][:, im * T:(im + 1) * T]
                        mm(g[:, im * E:(im + 1) * E], x[:, 0:128], wv[:], start=True, stop=True)
                        last = mm(g[0:REM, (2 + im) * E:(3 + im) * E], x[:, 128:T], wv[:], start=True, stop=True)
                    last.then_inc(sem("v"), 1)

                def scores(i, par, half, u):
                    im, a = u // 4, 2 * (u % 4)
                    n_u = i * UNITS + u
                    if u == 0:
                        pe.wait_ge(sem(f"load{par}"), 16 * LOADS * (half + 1))
                    def products(dst, rows, k):
                        q0 = im * TP
                        for x in range(2):
                            mm(dst[:, x * T:(x + 1) * T], qs[par][0:rows, a + x, q0:q0 + 128],
                               k[par][0:rows, a + x, q0:q0 + T], start=True, stop=True)
                            last = mm(dst[64 * x:64 * x + 64, 2 * T:3 * T], qs[par][0:rows, a + x, q0 + 128:q0 + TP],
                                      k[par][0:rows, a + x, q0:q0 + T], start=True, stop=True)
                        return last
                    if lsh:
                        after(pe, sem("f_read"), n_u)
                        products(ps_f, KB, kb).then_inc(sem("f"), 1)
                    after(pe, sem("scr" if lsh else "exp"), n_u - (NS - 1))
                    products(ps_s[u % NS], KQ, ks).then_inc(sem("s"), 1)

                def transposes(i, u):
                    n_u = i * UNITS + u
                    pe.wait_ge(sem("exp"), n_u + 1)
                    after(pe, sem("tm_read"), n_u)
                    after(pe, sem("tr_read"), n_u)
                    p = prob[u % 2]
                    for x in range(2):
                        nc.tensor.transpose(ps_tm[:, x * TP:x * TP + 128], p[:, x * T:x * T + 128], ident[:])
                        nc.tensor.transpose(ps_tr[0:REM, x * TP:x * TP + 128], p[:, x * T + 128:(x + 1) * T], ident[:])
                    rest_m = ps_tm[:, 0:2 * TP].rearrange("p (x t) -> p x t", t=TP)[:, :, 128:TP]
                    rest_r = ps_tr[0:REM, 0:2 * TP].rearrange("p (x t) -> p x t", t=TP)[:, :, 128:TP]
                    nc.tensor.transpose(rest_m, p[:, 2 * T:2 * T + 128], ident[:])
                    nc.tensor.transpose(rest_r, p[:, 2 * T + 128:3 * T], ident[:]).then_inc(sem("t"), 1)

                def weighted(i, par, u):
                    im, a = u // 4, 2 * (u % 4)
                    n_u = i * UNITS + u
                    pe.wait_ge(sem("tm_read"), n_u + 1)
                    pe.wait_ge(sem("tr_read"), n_u + 1)
                    if u == 0:
                        pe.wait_ge(sem("v_copied"), i + 1)
                        after(pe, sem("o0"), i)
                        after(pe, sem("o1"), i)
                    for x in range(2):
                        hd = a + x
                        out = ps_o[hd // 4][32 * (hd % 4):32 * (hd % 4) + 32, im * T:(im + 1) * T]
                        mm(out, vm[par][:, im, hd, :], ptm[u % 2][:, x * TP:x * TP + T], start=True, stop=False)
                        last = mm(out, vr[par][:, im, hd, :], ptr[u % 2][:, x * TP:x * TP + T], start=False, stop=True)
                    last.then_inc(sem("pv"), 1)

                def finish(i):
                    pe.wait_ge(sem("o0"), i)
                    pe.wait_ge(sem("o1"), i)
                    g = bank(0, i, "num_copied", 1, 0)
                    mm(g[:, 0:N2], sel_num[:, 0, :], osb[:, 0, :], start=True, stop=False)
                    mm(g[:, 0:N2], sel_num[:, 1, :], osb[:, 1, :], start=False, stop=True).then_inc(sem("num"), 1)
                    g = bank(1, i, "rec", 1, 0)
                    for im in range(2):
                        for k, t0 in enumerate((im * T, im * T + REM)):
                            for grp in range(2):
                                c = (2 * im + k) * H + grp * 4
                                last = mm(g[:, c:c + 4], osb[:, grp, t0:t0 + 128], sel_den[:], start=True, stop=True)
                    last.then_inc(sem("den"), 1)

                def spread_denominators(i):
                    g = bank(1, i, "tn", 1, 0)
                    pe.wait_ge(sem("rec_wide"), i)
                    spread(g, lambda c: rec_wide[:, c, :]).then_inc(sem("dbc"), 1)

                def output(i, k):
                    ready, done, read = (("oh", "wo", "yy"), ("yy", "mean2", "cent2"), ("sq2", "var2", "vcp2"))[k]
                    g = bank(1, i, read, 1, 0)
                    pe.wait_ge(sem(ready), i)
                    if k == 2:
                        last = token_means(g, sqr2)
                    else:
                        w, x = ((wo, oh), (mean_w, yy))[k]
                        last = mm(g[:, 0:N2], w[:], x[:], start=True, stop=True)
                    last.then_inc(sem(done), 1)

                def deviation2(i, back):
                    g = bank(1, i, "tn2", 1, 1 - back)
                    pe.wait_ge(sem("rs2"), (i + (1 - back)) * NEWTON_OPS)
                    spread(g, same(rstd2)).then_inc(sem("rbc2"), 1)

                def head():
                    consts(pe)
                    for a in (-2, -1):
                        mean(a, 0)
                        variance(a, 1)
                        deviation(a, 0)
                        project(wq, a, a, 1, "q", "qf")
                        if lsh:
                            hyperplanes(a, 0)
                        else:
                            project(wk, a, a, 0, "k", "kf")
                        if a == -2:
                            next_step()
                    values(-1, -1, 1)
                    scores(0, 0, 0, 0)
                    scores(0, 0, 0, 1)

                def step(i, m, half):
                    par = m % 2
                    next_step()
                    have_a, have_v = not is_last(i, 2), not is_last(i, 1)
                    for u in range(UNITS):
                        if u < 6:
                            scores(i, par, half, u + 2)
                        elif have_v:
                            scores(i + 1, 1 - par, half + par, u - 6)
                        transposes(i, u)
                        if u > 0:
                            weighted(i, par, u - 1)
                        elif not first(i):
                            weighted(i - 1, 1 - par, UNITS - 1)
                        later = not lsh and not first(i)
                        if u == 0 and have_a:
                            mean(i, 0 if lsh else 1)
                        if u == 1 and not first(i):
                            finish(i)
                        if u == 2 and have_a:
                            variance(i, 0)
                        if u == 2 and not first(i):
                            spread_denominators(i)
                        if u == 3 and later and not first(i - 1):
                            deviation2(i, 2)
                        if u == 4 and later:
                            output(i, 0)
                        if u == 4 and have_a:
                            deviation(i, 0)
                        if u == 5 and later:
                            output(i, 1)
                        if u == 5 and have_a:
                            project(wq, i, m, 1 if lsh else 0, "q", "qf")
                        if u == 5 and have_v and lsh:
                            values(i, m, 0)
                        if u == 6 and have_a:
                            if lsh:
                                hyperplanes(i, 1)
                            else:
                                project(wk, i, m, 0, "k", "kf")
                        if u == 6 and have_v and not lsh:
                            values(i, m, 1)
                        if u == 7 and later:
                            output(i, 2)
                pairs(pe, head, step)
                weighted(PAIRS - 1, 1, UNITS - 1)
                next_step()
                finish(PAIRS)
                spread_denominators(PAIRS)
                if not lsh:
                    deviation2(PAIRS, 2)
                    for k in range(3):
                        output(PAIRS, k)
                    deviation2(PAIRS, 1)

            @block.scalar
            def _(act):
                fn = nc.scalar.activation

                def factors(i, u):
                    n_u = i * UNITS + u
                    act.wait_ge(sem("f"), n_u + 1)
                    after(act, sem("scr"), n_u - 1)
                    fn(fac[u % 2][:], ps_f[:, 0:3 * T], ACT.Copy, bias=-1.0, scale=8.0).then_inc(sem("f_read"), 1)

                def exponentials(i, u):
                    n_u = i * UNITS + u
                    act.wait_ge(sem("nm"), n_u + 1)
                    after(act, sem("t"), n_u - 1)
                    src = scr[u % 2] if lsh else ps_s[u % NS]
                    for x in range(3):
                        last = fn(prob[u % 2][:, x * T:(x + 1) * T], src[:, x * T:(x + 1) * T], ACT.Exp,
                                  bias=nm[u % 2][:, x:x + 1], scale=scale)
                    last.then_inc(sem("exp"), 1)

                def rest_keys(i, u):
                    n_u = i * UNITS + u
                    act.wait_ge(sem("t"), n_u + 1)
                    after(act, sem("pv"), n_u - 1)
                    fn(ptr[u % 2][0:REM, :], ps_tr[0:REM, 0:2 * TP], ACT.Copy).then_inc(sem("tr_read"), 1)

                def square(i):
                    act.wait_ge(sem("cent"), i + 3)
                    after(act, sem("var"), i + 2)
                    fn(sqr[:], cent[:], ACT.Square).then_inc(sem("sq"), 1)

                def with_bias(i, dst, g, bias, name, done):
                    act.wait_ge(sem(name), i + 3)
                    parts_made(act, i + 2)
                    fn(dst[:], g[:, 0:N2], ACT.Identity, bias=col[:, bias:bias + 1]).then_inc(sem(done), 1)

                def v_copy(i, par, g):
                    act.wait_ge(sem("v"), i + 2)
                    after(act, sem("pv"), UNITS * i)
                    fn(vm[par][:, :, :, 0:D], g[:, 0:2 * E].rearrange("p (i h d) -> p i h d", i=2, d=D), ACT.Copy)
                    fn(vr[par][0:REM, :, :, 0:D], g[0:REM, 2 * E:4 * E].rearrange("p (i h d) -> p i h d", i=2, d=D),
                       ACT.Copy).then_inc(sem("v_copied"), 1)

                def numerators(i):
                    act.wait_ge(sem("num"), i)
                    after(act, sem("tn"), i - 1)
                    fn(num[:], g0[:, 0:N2], ACT.Copy).then_inc(sem("num_copied"), 1)

                def head():
                    consts(act)
                    for a in (-2, -1):
                        square(a)
                        with_bias(a, qf, g1, 0, "q", "qf")
                        if lsh:
                            with_bias(a, prj, g0, 1, "pr", "prc")
                        else:
                            with_bias(a, kf, g0, 1, "k", "kf")
                    v_copy(-1, 0, g1)
                    if lsh:
                        factors(0, 0)
                        factors(0, 1)

                def step(i, m, half):
                    have_a, have_v = not is_last(i, 2), not is_last(i, 1)
                    for u in range(UNITS):
                        exponentials(i, u)
                        if u > 0:
                            rest_keys(i, u - 1)
                        elif not first(i):
                            rest_keys(i - 1, UNITS - 1)
                        if lsh and u < 6:
                            factors(i, u + 2)
                        elif lsh and have_v:
                            factors(i + 1, u - 6)
                        if u == 0 and not first(i):
                            outputs(i)
                        if u == 2 and not first(i):
                            numerators(i)
                        if u == 2 and have_a:
                            square(i)
                        if u == 6 and have_a:
                            with_bias(i, qf, g1 if lsh else g0, 0, "q", "qf")
                        if u == 7 and have_a:
                            if lsh:
                                with_bias(i, prj, g1, 1, "pr", "prc")
                            else:
                                with_bias(i, kf, g0, 1, "k", "kf")
                        if u == (6 if lsh else 7) and have_v:
                            v_copy(i, (m + 1) % 2, g0 if lsh else g1)
                        if u == 7 and not lsh and not first(i):
                            square2(i)

                def outputs(i):
                    act.wait_ge(sem("pv"), UNITS * i)
                    after(act, sem("den"), i - 1)
                    fn(osb[:, 1, :], ps_o[1][:, 0:N2], ACT.Copy).then_inc(sem("o1"), 1)

                def square2(i):
                    act.wait_ge(sem("cent2"), i)
                    after(act, sem("var2"), i - 1)
                    fn(sqr2[:], cent2[:], ACT.Square).then_inc(sem("sq2"), 1)

                pairs(act, head, step)
                rest_keys(PAIRS - 1, UNITS - 1)
                outputs(PAIRS)
                numerators(PAIRS)
                if not lsh:
                    square2(PAIRS)

            @block.vector
            def _(dve):
                def row_max(i, u, between):
                    n_u = i * UNITS + u
                    dve.wait_ge(sem("s"), n_u + 1)
                    if lsh:
                        dve.wait_ge(sem("f_read"), n_u + 1)
                        after(dve, sem("exp"), n_u - 1)
                        nc.vector.scalar_tensor_tensor(scr[u % 2][:], fac[u % 2][:], 30.0, ps_s[0][:, 0:3 * T],
                                                       ALU.max, ALU.mult).then_inc(sem("scr"), 1)
                        between()
                        dve.wait_ge(sem("scr"), n_u + 1)
                    src = scr[u % 2] if lsh else ps_s[u % NS]
                    nc.vector.tensor_reduce(mx[u % 2][:], src[:, 0:3 * T].rearrange("p (x t) -> p x t", t=T),
                                            AX.X, ALU.max).then_inc(sem("mx"), 1)
                    if not lsh:
                        between()
                    dve.wait_ge(sem("mx"), n_u + 1)
                    after(dve, sem("exp"), n_u - 1)
                    nc.vector.tensor_scalar(nm[u % 2][:], mx[u % 2][:], -scale, None, ALU.mult).then_inc(sem("nm"), 1)

                def main_keys(i, u):
                    n_u = i * UNITS + u
                    dve.wait_ge(sem("t"), n_u + 1)
                    after(dve, sem("pv"), n_u - 1)
                    nc.vector.tensor_copy(ptm[u % 2][:], ps_tm[:, 0:2 * TP]).then_inc(sem("tm_read"), 1)

                def center(i, g):
                    dve.wait_ge(sem("mean"), i + 3)
                    after(dve, sem("sq"), i + 2)
                    after(dve, sem("xh"), i + 2)
                    nc.vector.tensor_tensor(cent[:], h_of(i + 2), g[:, 0:N2], ALU.subtract).then_inc(sem("cent"), 1)

                def guess(g, v, vn, y, ready, copied, spread_done, seeded, newton, nth):
                    dve.wait_ge(sem(ready), nth + 1)
                    after(dve, sem(newton), nth * NEWTON_OPS)
                    after(dve, sem(spread_done), nth)
                    nc.vector.tensor_scalar(v[:], g[:, 0:4], EPS_LN, None, ALU.add).then_inc(sem(copied), 1)
                    dve.wait_ge(sem(copied), nth + 1)
                    nc.vector.tensor_scalar(nbits[:], v[:].bitcast(I32), 1, None,
                                            ALU.arith_shift_right).then_inc(sem(seeded), 1)
                    dve.wait_ge(sem(seeded), 3 * nth + 1)
                    nc.vector.tensor_scalar(vn[:], v[:], -0.5, None, ALU.mult).then_inc(sem(seeded), 1)
                    nc.vector.tensor_scalar(y[:].bitcast(I32), nbits[:], -1.0, RSQRT_MAGIC, ALU.mult,
                                            ALU.add).then_inc(sem(seeded), 1)

                def normal(i, m, g):
                    dve.wait_ge(sem("rbc"), i + 3)
                    dve.wait_ge(sem("cent"), i + 3)
                    if not first(i + 2):
                        after(dve, sem("v"), i + 3 - NXH)
                        if not lsh:
                            after(dve, sem("yy"), i + 3 - NXH)
                            after(dve, sem("k"), i + 3 - NXH)
                        after(dve, sem("q"), i + 3 - NXH)
                    nc.vector.tensor_tensor(xh[(m + 2) % NXH][:], cent[:], g[:, 0:N2], ALU.mult).then_inc(sem("xh"), 1)

                def outputs(i):
                    dve.wait_ge(sem("pv"), UNITS * i)
                    after(dve, sem("den"), i - 1)
                    nc.vector.tensor_copy(osb[:, 0, :], ps_o[0][:, 0:N2]).then_inc(sem("o0"), 1)

                def denominators(i):
                    dve.wait_ge(sem("den"), i)
                    nc.vector.reciprocal(rec[:, :, :].rearrange("p c h -> p (c h)"), g1[:, 0:4 * H]).then_inc(sem("rec"), 1)
                    dve.wait_ge(sem("rec"), i)
                    after(dve, sem("dbc"), i - 1)
                    nc.vector.tensor_copy(
                        rec_wide[:, :, :].rearrange("p c (h d) -> p (c h) d", d=D),
                        rec[:, :, :].rearrange("p c (h o) -> p (c h) o", o=1).broadcast_to([128, 4 * H, D])
                    ).then_inc(sem("rec_wide"), 1)

                def divide(i):
                    dve.wait_ge(sem("dbc"), i)
                    dve.wait_ge(sem("num_copied"), i)
                    if not lsh:
                        after(dve, sem("oh"), i - 1)
                    nc.vector.tensor_tensor(att[:], num[:], g1[:, 0:N2], ALU.mult).then_inc(sem("tn"), 1)
                    if lsh:
                        dve.wait_ge(sem("tn"), i)
                        nc.vector.scalar_tensor_tensor(h_of(i - 1), att[:], col[:, 2:3], h_of(i - 1),
                                                       ALU.add, ALU.add).then_inc(sem("hnew"), 1)

                def residual(i, m):
                    dve.wait_ge(sem("wo"), i)
                    after(dve, sem("mean2"), i - 1)
                    after(dve, sem("cent2"), i - 1)
                    nc.vector.scalar_tensor_tensor(yy[:], g1[:, 0:N2], col[:, 3:4], xh[(m + 3) % 4][:],
                                                   ALU.add, ALU.add).then_inc(sem("yy"), 1)

                def center2(i):
                    dve.wait_ge(sem("mean2"), i)
                    dve.wait_ge(sem("yy"), i)
                    after(dve, sem("sq2"), i - 1)
                    after(dve, sem("tn2"), i - 1)
                    nc.vector.tensor_tensor(cent2[:], yy[:], g1[:, 0:N2], ALU.subtract).then_inc(sem("cent2"), 1)

                def normal2(i):
                    dve.wait_ge(sem("rbc2"), i)
                    dve.wait_ge(sem("cent2"), i)
                    after(dve, sem("tt"), i - 1)
                    nc.vector.tensor_tensor(nrm2[:], cent2[:], g1[:, 0:N2], ALU.mult).then_inc(sem("tn2"), 1)

                gm = g0 if lsh else g1

                def guess2(nth):
                    guess(g1, var2, vneg2, rstd2, "var2", "vcp2", "rbc2", "seed2", "rs2", nth)

                def head():
                    for b in [parts, *vm, *vr, *ptr]:
                        nc.vector.memset(b[:], 0.0)
                    nc.vector.memset(ptm[0][:], 0.0)
                    if lsh:
                        for b in kb:
                            nc.vector.memset(b[:], 0.0)
                    nc.vector.memset(half3[:], 1.5)
                    nc.vector.memset(ptm[1][:], 0.0).then_inc(sem("zdone"), 1)
                    dve.wait_ge(sem("zdone"), 1)
                    for b in (*vm, *vr):
                        last = nc.vector.memset(b[:, :, :, D:D + 1], 1.0)
                    last.then_inc(sem("zero"), 1)
                    consts(dve)
                    for a in (-2, -1):
                        center(a, g0)
                        guess(g1, var, vneg, rstd, "var", "vcp", "rbc", "seed", "rs", a + 2)
                        normal(a, a, g0)
                    row_max(0, 0, lambda: None)

                def step(i, m, half):
                    have_a, have_v = not is_last(i, 2), not is_last(i, 1)
                    for u in range(UNITS):
                        def last_keys():
                            if u > 0:
                                main_keys(i, u - 1)
                            elif not first(i):
                                main_keys(i - 1, UNITS - 1)
                        if u < 7:
                            row_max(i, u + 1, last_keys)
                        elif have_v:
                            row_max(i + 1, 0, last_keys)
                        else:
                            last_keys()
                        later = not lsh and not first(i)
                        if u == 0 and not first(i):
                            outputs(i)
                        if u == 0 and later and not first(i - 1):
                            guess2(i - 2)
                        if u == 1 and have_a:
                            center(i, gm)
                        if u == 2 and not first(i):
                            denominators(i)
                        if u == 3 and have_a:
                            guess(g0, var, vneg, rstd, "var", "vcp", "rbc", "seed", "rs", i + 2)
                        if u == 3 and not first(i):
                            divide(i)
                        if u == 4 and later and not first(i - 1):
                            normal2(i - 1)
                        if u == 5 and later:
                            residual(i, m)
                        if u == 5 and have_a:
                            normal(i, m, g0)
                        if u == 6 and later:
                            center2(i)
                pairs(dve, head, step)
                main_keys(PAIRS - 1, UNITS - 1)
                outputs(PAIRS)
                if not lsh:
                    guess2(PAIRS - 2)
                denominators(PAIRS)
                divide(PAIRS)
                if lsh:
                    dve.wait_ge(sem("hnew"), PAIRS)
                else:
                    normal2(PAIRS - 1)
                    residual(PAIRS, PAIRS % 4)
                    center2(PAIRS)
                    guess2(PAIRS - 1)
                    normal2(PAIRS)

            @block.gpsimd
            def _(pool):
                def newton(vn, y, seeded, done, nth):
                    pool.wait_ge(sem(seeded), 3 * nth + 3)
                    k = 0
                    for _ in range(3):
                        for dst, a, b, op in ((nwt, y, y, ALU.mult), (nwt, nwt, vn, ALU.mult),
                                              (nwt, nwt, half3, ALU.add), (y, y, nwt, ALU.mult)):
                            nc.gpsimd.tensor_tensor(dst[:], a[:], b[:], op).then_inc(sem(done), 1)
                            k += 1
                            pool.wait_ge(sem(done), nth * NEWTON_OPS + k)

                def split(i, src, ready, base, k):
                    pool.wait_ge(sem(ready), i + 3)
                    after(pool, sem("store"), 16 * (i + 2))
                    hold(pool, sem("pass"))
                    hi, mid, low = (both(parts[:, base + p, :]) for p in range(3))
                    n_s = (i + 2) * NSIDE * 4 + 4 * k
                    nc.gpsimd.tensor_copy(hi, two(src[:])).then_inc(sem("split"), 1)
                    pool.wait_ge(sem("split"), n_s + 1)
                    nc.gpsimd.tensor_tensor(two(rst[:]), two(src[:]), hi, ALU.subtract).then_inc(sem("split"), 1)
                    pool.wait_ge(sem("split"), n_s + 2)
                    hold(pool, sem("pass"))
                    nc.gpsimd.tensor_copy(mid, two(rst[:])).then_inc(sem("split"), 1)
                    pool.wait_ge(sem("split"), n_s + 3)
                    last = nc.gpsimd.tensor_tensor(low, two(rst[:]), mid, ALU.subtract)
                    last.then_inc(sem("split"), 1)
                    pool.wait_ge(sem("split"), n_s + 4)

                def make_parts(i):
                    split(i, qf, "qf", 0, 0)
                    if lsh:
                        pool.wait_ge(sem("prc"), i + 3)
                        hold(pool, sem("pass"))
                        nc.gpsimd.tensor_scalar(both(parts[:, PARTS, :]), two(prj[:]), 0.0, 0.5,
                                                ALU.is_ge, ALU.subtract).then_inc(sem("parts"), 1)
                    else:
                        split(i, kf, "kf", PARTS, 1)

                def head():
                    consts(pool)
                    for a in (-2, -1):
                        newton(vneg, rstd, "seed", "rs", a + 2)
                        make_parts(a)

                def step(i, m, half):
                    later = not lsh and not first(i)
                    if later and not first(i - 1):
                        newton(vneg2, rstd2, "seed2", "rs2", i - 2)
                    if not is_last(i, 2):
                        newton(vneg, rstd, "seed", "rs", i + 2)
                    if later:
                        v_bias(i)
                        if not first(i - 1):
                            affine(i - 1)
                    if not is_last(i, 2):
                        make_parts(i)

                def v_bias(i):
                    pool.wait_ge(sem("tn"), i)
                    after(pool, sem("wo"), i - 1)
                    hold(pool, sem("pass"))
                    nc.gpsimd.tensor_scalar(oh[:], att[:], col[:, 2:3], None, ALU.add).then_inc(sem("oh"), 1)

                def affine(i):
                    pool.wait_ge(sem("tn2"), i)
                    after(pool, sem("out"), 16 * (i - 1))
                    hold(pool, sem("pass"))
                    nc.gpsimd.tensor_scalar(tt[:], nrm2[:], col[:, 4:5], col[:, 5:6], ALU.mult,
                                            ALU.add).then_inc(sem("tt"), 1)

                pairs(pool, head, step)
                if not lsh:
                    newton(vneg2, rstd2, "seed2", "rs2", PAIRS - 2)
                    v_bias(PAIRS)
                    affine(PAIRS - 1)
                    newton(vneg2, rstd2, "seed2", "rs2", PAIRS - 1)
                    affine(PAIRS)
        n.clear()


def chunks(eng, step):
    for k in range(3):
        step(k, k % 2, k // 2)
    with eng.Fori(0, (NC - 3) // 2) as it:
        for p in range(2):
            step(it * 2 + (p + 3), 1 - p, it + (p + 1))


def route(nc, hT, ident, tT_dram, t_dram, sorted_dram, gate_w, gate_b, prefix_w, logit, dest, best, tile_expert):
    with ExitStack() as ctx:
        n = Names(nc, ctx, "route")
        sem = n.sem
        gw = n.sb("gw", [128, NE])
        gb = n.sb("gb", [128, NE])
        upper = n.sb("upper", [128, 128])
        ones = n.sb("ones", [128, 128])
        tc = [n.sb(f"tc{p}", [128, CT * 128]) for p in range(2)]
        tok = [n.sb(f"tok{p}", [128, CT, 128]) for p in range(2)]
        zeros = n.sb("zeros", [128, 8 * 128])
        ps_l = [n.ps(f"l{p}", [128, 512]) for p in range(2)]
        ps_t = [n.ps(f"t{p}", [128, 512]) for p in range(2)]
        hot = n.sb("hot", [128, TILES, NE])
        rank = n.sb("rank", [128, TILES, NE])
        count = n.sb("count", [128, TILES, NE])
        cum = n.sb("cum", [128, NE, TILES])
        top = n.sb("top", [128, TILES])
        work = n.sb("work", [128, TILES, NE])
        pick = n.sb("pick", [128, TILES])
        idx_e = n.sb("idx_e", [128, NE])
        tot = n.sb("tot", [128, NE])
        tot_i = n.sb("tot_i", [128, NE], I32)
        tiles = n.sb("tiles", [128, NE])
        ends = n.sb("ends", [128, NE])
        starts = n.sb("starts", [128, NE])
        slot_no = n.sb("slot_no", [1, SLOTS])
        acc = [n.sb(f"acc{p}", [1, SLOTS]) for p in range(2)]

        with nc.Block() as block:
            @block.sync
            def _(sp):
                for dst, src in ((gw, gate_w), (gb, gate_b), (upper, prefix_w)):
                    sp.dma_start(dst[:], src).then_inc(sem("const"), 16)
                sp.wait_ge(sem("zeros"), 1)
                for k in range(SLOTS // 8):
                    sp.dma_start(sorted_dram[k * 1024:(k + 1) * 1024, :].rearrange("(p r) e -> p (r e)", r=8),
                                 zeros[:]).then_inc(sem("cleared"), 16)

                def load(k, p):
                    after(sp, sem("turned"), (k - 1) * CT)
                    sp.dma_start(tc[p][:], tT_dram[:, bass.ds(k * (CT * 128), CT * 128)]).then_inc(sem(f"load{p}"), 16)

                def store(k, p):
                    sp.wait_ge(sem("tok"), (k + 1) * CT)
                    sp.dma_start(t_dram[bass.ds(k * (CT * 128), CT * 128), :].rearrange("(c p) e -> p c e", p=128),
                                 tok[p][:]).then_inc(sem(f"store{p}"), 16)

                load(0, 0)
                for k in range(2):
                    load(k + 1, 1 - k)
                    store(k, k)
                with sp.Fori(0, (NC - 3) // 2) as it:
                    for p in range(2):
                        load(it * 2 + (p + 3), 1 - p)
                        store(it * 2 + (p + 2), p)
                store(NC - 1, 0)
                sp.wait_ge(sem("store0"), 16 * ((NC + 1) // 2))
                sp.wait_ge(sem("store1"), 16 * (NC // 2))
                sp.wait_ge(sem("cleared"), 16 * (SLOTS // 8))

            @block.tensor
            def _(pe):
                pe.wait_ge(sem("const"), 48)

                def chunk(k, p, half):
                    pe.wait_ge(sem(f"load{p}"), 16 * (half + 1))
                    after(pe, sem("logit"), k - 1)
                    for c in range(CT):
                        x = tc[p][:, c * 128:(c + 1) * 128]
                        nc.tensor.matmul(ps_l[p][:, c * NE:(c + 1) * NE], x, gw[:], start=True,
                                         stop=True).then_inc(sem("gate"), 1)
                        after(pe, sem("tok"), k * CT + (c - 1))
                        nc.tensor.transpose(ps_t[(p * CT + c) % 2][:, 0:128], x, ident[:]).then_inc(sem("turned"), 1)
                chunks(pe, chunk)

            @block.vector
            def _(dve):
                nc.vector.memset(ones[:], 1.0)
                nc.vector.memset(zeros[:], 0.0).then_inc(sem("zeros"), 1)
                dve.wait_ge(sem("const"), 48)

                def chunk(k, p, half):
                    after(dve, sem(f"store{p}"), 16 * half)
                    for c in range(CT):
                        dve.wait_ge(sem("turned"), k * CT + (c + 1))
                        nc.vector.tensor_copy(tok[p][:, c, :], ps_t[(p * CT + c) % 2][:, 0:128]).then_inc(sem("tok"), 1)
                    dve.wait_ge(sem("gate"), (k + 1) * CT)
                    nc.vector.tensor_tensor(logit[:, bass.ds(k * CT, CT), :],
                                            ps_l[p][:, 0:CT * NE].rearrange("p (c e) -> p c e", e=NE),
                                            gb[:, :].rearrange("p (o e) -> p o e", o=1).broadcast_to([128, CT, NE]),
                                            ALU.add).then_inc(sem("logit"), 1)
                chunks(dve, chunk)

        def per_token(x):
            return x.rearrange("p (c o) -> p c o", o=1).broadcast_to([128, TILES, NE])

        def per_expert(x):
            return x.rearrange("p (o e) -> p o e", o=1).broadcast_to([128, TILES, NE])

        with nc.Block() as block:
            @block.gpsimd
            def _(pool):
                nc.gpsimd.iota(idx_e[:], pattern=[[1, NE]], base=-NE, channel_multiplier=0,
                               allow_small_or_imprecise_dtypes=True)
                nc.gpsimd.iota(slot_no[:], pattern=[[1, SLOTS]], base=0, channel_multiplier=0,
                               allow_small_or_imprecise_dtypes=True).then_inc(sem("iota"), 1)

            @block.scalar
            def _(act):
                act.wait_ge(sem("shifted"), 1)
                nc.scalar.activation(work[:], work[:], ACT.Exp).then_inc(sem("gate_exp"), 1)

            @block.tensor
            def _(pe):
                pe.wait_ge(sem("hot"), 1)
                flat = hot[:, :, :].rearrange("p c e -> p (c e)")
                W = TILES * NE
                for k in range(0, W, 512):
                    w = min(512, W - k)
                    b = k // 512
                    if b:
                        pe.wait_ge(sem("cnt"), b)
                    nc.tensor.matmul(ps_l[0][:, 0:w], upper[:], flat[:, k:k + w], start=True, stop=True)
                    nc.tensor.matmul(ps_l[1][:, 0:w], ones[:], flat[:, k:k + w], start=True,
                                     stop=True).then_inc(sem("ranked"), 1)

            @block.vector
            def _(dve):
                chain = [0]

                def link(ins):
                    chain[0] += 1
                    ins.then_inc(sem("chain"), 1)
                    dve.wait_ge(sem("chain"), chain[0])

                tt_, ts_ = nc.vector.tensor_tensor, nc.vector.tensor_scalar
                link(nc.vector.tensor_reduce(top[:], logit[:], AX.X, ALU.max))
                link(tt_(work[:], logit[:], per_token(top[:]), ALU.subtract))
                dve.wait_ge(sem("iota"), 1)
                link(ts_(hot[:], work[:], 0.0, None, ALU.is_equal))
                link(tt_(hot[:], hot[:], per_expert(idx_e[:]), ALU.mult))
                link(nc.vector.tensor_reduce(pick[:], hot[:], AX.X, ALU.min))
                nc.vector.tensor_copy(rank[:], per_expert(idx_e[:])).then_inc(sem("shifted"), 1)
                dve.wait_ge(sem("shifted"), 1)
                tt_(hot[:], rank[:], per_token(pick[:]), ALU.is_equal).then_inc(sem("hot"), 1)
                dve.wait_ge(sem("gate_exp"), 1)
                link(nc.vector.tensor_reduce(top[:], work[:], AX.X, ALU.add))
                link(nc.vector.reciprocal(best[:], top[:]))
                dve.wait_ge(sem("hot"), 1)
                W = TILES * NE
                rf, cf = (x[:, :, :].rearrange("p c e -> p (c e)") for x in (rank, count))
                for k in range(0, W, 512):
                    w = min(512, W - k)
                    dve.wait_ge(sem("ranked"), k // 512 + 1)
                    nc.vector.tensor_copy(rf[:, k:k + w], ps_l[0][:, 0:w])
                    last = nc.vector.tensor_copy(cf[:, k:k + w], ps_l[1][:, 0:w]).then_inc(sem("cnt"), 1)
                dve.wait_ge(sem("cnt"), (W + 511) // 512)
                for e in range(NE):
                    c = count[:, :, e]
                    last = nc.vector.tensor_tensor_scan(cum[:, e, :], c, c, 0.0, ALU.add, ALU.bypass)
                link(last)
                cv = cum[:, :, :].rearrange("p e c -> p c e")
                link(tt_(work[:], cv, count[:], ALU.subtract))
                link(tt_(rank[:], rank[:], work[:], ALU.add))
                link(ts_(tot_i[:], cum[:, :, TILES - 1], 127.0, None, ALU.add))
                link(ts_(tot_i[:], tot_i[:], 7, None, ALU.arith_shift_right))
                link(nc.vector.tensor_copy(tiles[:], tot_i[:]))
                link(nc.vector.tensor_tensor_scan(ends[:], tiles[:], tiles[:], 0.0, ALU.add, ALU.bypass))
                link(tt_(starts[:], ends[:], tiles[:], ALU.subtract))
                link(ts_(starts[:], starts[:], 128.0, None, ALU.mult))
                link(tt_(rank[:], rank[:], per_expert(starts[:]), ALU.add))
                link(tt_(rank[:], rank[:], hot[:], ALU.mult))
                link(nc.vector.tensor_reduce(pick[:], rank[:], AX.X, ALU.add))
                link(nc.vector.tensor_copy(dest[:], pick[:]))
                link(ts_(acc[0][:], slot_no[:], ends[0:1, 0:1], None, ALU.is_ge))
                for e in range(1, NE - 1):
                    link(nc.vector.scalar_tensor_tensor(acc[e % 2][:], slot_no[:], ends[0:1, e:e + 1],
                                                        acc[(e + 1) % 2][:], ALU.is_ge, ALU.add))
                link(nc.vector.tensor_copy(tile_expert[:], acc[(NE - 2) % 2][:]))

        with nc.Block() as block:
            @block.sync
            def _(sp):
                def load(k, p, half):
                    after(sp, sem(f"scattered{p}"), 16 * CT * half)
                    sp.dma_start(tok[p][:], t_dram[bass.ds(k * (CT * 128), CT * 128), :].rearrange(
                        "(c p) e -> p c e", p=128)).then_inc(sem(f"back{p}"), 16)
                chunks(sp, load)

            @block.gpsimd
            def _(pool):
                ids = [n.sb(f"ids{p}", [128, CT], U32) for p in range(2)]

                def chunk(k, p, half):
                    after(pool, sem(f"scattered{p}"), 16 * CT * half)
                    hold(pool, sem("pass"))
                    nc.gpsimd.tensor_copy(ids[p][:], dest[:, bass.ds(k * CT, CT)]).then_inc(sem("ids"), 1)
                    pool.wait_ge(sem("ids"), k + 1)
                    pool.wait_ge(sem(f"back{p}"), 16 * (half + 1))
                    hold(pool, sem("pass"))
                    for c in range(CT):
                        nc.gpsimd.indirect_dma_start(
                            sorted_dram[:, :], bass.IndirectOffsetOnAxis(ap=ids[p][:, c:c + 1], axis=0),
                            tok[p][:, c, :], None).then_inc(sem(f"scattered{p}"), 16)
                chunks(pool, chunk)
                pool.wait_ge(sem("scattered0"), 16 * CT * ((NC + 1) // 2))
                pool.wait_ge(sem("scattered1"), 16 * CT * (NC // 2))


def tiles(eng, step):
    for s in range(4):
        step(s, s, 0)
    with eng.Fori(0, SLOTS // 4 - 2) as it:
        for k in range(4):
            step(it * 4 + (k + 4), k, it + 1)
    for s in range(SLOTS - 4, SLOTS):
        step(s, s % 4, s // 4)


def experts(nc, ident, sorted_dram, y_dram, w1, b1, w2, b2, tile_expert):
    FC = FF // 128
    with ExitStack() as ctx:
        n = Names(nc, ctx, "moe")
        sem = n.sem
        w1_sb = n.sb("w1", [128, NE * FF])
        b1_sb = n.sb("b1", [128, NE * FF])
        w2_sb = n.sb("w2", [128, NE * FC * E])
        b2_sb = n.sb("b2", [128, NE * E])
        xs = [n.sb(f"xs{p}", [128, E]) for p in range(4)]
        xt = [n.sb(f"xt{p}", [128, E]) for p in range(2)]
        pre = [n.sb(f"pre{p}", [128, FF]) for p in range(2)]
        hid = [n.sb(f"hid{p}", [128, FF]) for p in range(2)]
        hidT = [n.sb(f"hidT{p}", [128, FF]) for p in range(2)]
        ys = [n.sb(f"ys{p}", [128, E]) for p in range(4)]
        ps_x, ps_h, ps_t, ps_y = ([n.ps(f"{x}{p}", [128, 512]) for p in range(2)] for x in "xhty")

        def has(s):
            return not isinstance(s, int) or 0 <= s < SLOTS

        with nc.Block() as block:
            @block.sync
            def _(sp):
                for dst, src in ((w1_sb, w1), (b1_sb, b1), (w2_sb, w2), (b2_sb, b2)):
                    sp.dma_start(dst[:], src).then_inc(sem("w"), 16)

                def load(s, k):
                    after(sp, sem("xT"), s - 3)
                    sp.dma_start(xs[k][:], sorted_dram[bass.ds(s * 128, 128), :]).then_inc(sem(f"load{k}"), 16)

                def step(s, k, quarter):
                    if has(s + 4):
                        load(s + 4, k)
                for s in range(4):
                    load(s, s)
                tiles(sp, step)

            @block.gpsimd
            def _(pool):
                def step(s, k, quarter):
                    pool.wait_ge(sem("ys"), s + 1)
                    hold(pool, sem("pass"))
                    pool.dma_start(y_dram[bass.ds(s * 128, 128), :], ys[k][:]).then_inc(sem(f"store{k}"), 16)
                tiles(pool, step)
                for k in range(4):
                    pool.wait_ge(sem(f"store{k}"), 16 * (SLOTS // 4))

            def expert_of(eng, s):
                return eng.value_load(tile_expert[0:1, bass.ds(s, 1)], min_val=0, max_val=NE - 1)

            @block.tensor
            def _(pe):
                def turn_rows(s, k, quarter):
                    pe.wait_ge(sem(f"load{k}"), 16 * (quarter + 1))
                    after(pe, sem("xt"), s - 1)
                    nc.tensor.transpose(ps_x[k % 2][:, 0:128], xs[k][:], ident[:]).then_inc(sem("xT"), 1)

                def first(s, p):
                    e = expert_of(pe, s)
                    pe.wait_ge(sem("xt"), s + 1)
                    after(pe, sem("pre"), s - 1)
                    nc.tensor.matmul(ps_h[p][:], xt[p][:], w1_sb[:, bass.ds(e * FF, FF)], start=True,
                                     stop=True).then_inc(sem("h"), 1)

                def turn_hidden(s, p):
                    pe.wait_ge(sem("gelu"), s + 1)
                    after(pe, sem("hT"), s - 1)
                    for f in range(FC):
                        last = nc.tensor.transpose(ps_t[p][:, f * 128:(f + 1) * 128], hid[p][:, f * 128:(f + 1) * 128],
                                                   ident[:])
                    last.then_inc(sem("ht"), 1)

                def second(s, p):
                    e = expert_of(pe, s)
                    pe.wait_ge(sem("hT"), s + 1)
                    after(pe, sem("ys"), s - 1)
                    for f in range(FC):
                        last = nc.tensor.matmul(ps_y[p][:, 0:E], hidT[p][:, f * 128:(f + 1) * 128],
                                                w2_sb[:, bass.ds(e * (FC * E) + f * E, E)], start=f == 0,
                                                stop=f == FC - 1)
                    last.then_inc(sem("y"), 1)

                def step(s, k, quarter):
                    if has(s + 2):
                        first(s + 2, k % 2)
                    turn_hidden(s, k % 2)
                    if has(s + 3):
                        turn_rows(s + 3, (k + 3) % 4, quarter + (k + 3) // 4)
                    if has(s - 1):
                        second(s - 1, (k + 1) % 2)
                pe.wait_ge(sem("w"), 64)
                turn_rows(0, 0, 0)
                turn_rows(1, 1, 0)
                first(0, 0)
                turn_rows(2, 2, 0)
                first(1, 1)
                tiles(pe, step)
                second(SLOTS - 1, 1)

            @block.scalar
            def _(act):
                def gelu(s, p):
                    act.wait_ge(sem("pre"), s + 1)
                    after(act, sem("ht"), s - 1)
                    nc.scalar.activation(hid[p][:], pre[p][:], ACT.Gelu_apprx_tanh).then_inc(sem("gelu"), 1)

                def step(s, k, quarter):
                    if has(s + 1):
                        gelu(s + 1, (k + 1) % 2)
                    act.wait_ge(sem("ht"), s + 1)
                    after(act, sem("y"), s - 1)
                    nc.scalar.activation(hidT[k % 2][:], ps_t[k % 2][:], ACT.Copy).then_inc(sem("hT"), 1)
                gelu(0, 0)
                tiles(act, step)

            @block.vector
            def _(dve):
                def rows(s, p):
                    dve.wait_ge(sem("xT"), s + 1)
                    after(dve, sem("h"), s - 1)
                    nc.vector.tensor_copy(xt[p][:], ps_x[p][:, 0:128]).then_inc(sem("xt"), 1)

                def hidden(s, p):
                    e = expert_of(dve, s)
                    dve.wait_ge(sem("h"), s + 1)
                    after(dve, sem("gelu"), s - 1)
                    nc.vector.tensor_tensor(pre[p][:], ps_h[p][:], b1_sb[:, bass.ds(e * FF, FF)],
                                            ALU.add).then_inc(sem("pre"), 1)

                def result(s, k, quarter):
                    e = expert_of(dve, s)
                    dve.wait_ge(sem("y"), s + 1)
                    after(dve, sem(f"store{k}"), 16 * quarter)
                    nc.vector.tensor_tensor(ys[k][:], ps_y[k % 2][:, 0:E], b2_sb[:, bass.ds(e * E, E)],
                                            ALU.add).then_inc(sem("ys"), 1)

                def step(s, k, quarter):
                    if has(s + 2):
                        hidden(s + 2, k % 2)
                    if has(s + 3):
                        rows(s + 3, (k + 1) % 2)
                    if has(s - 1):
                        result(s - 1, (k + 3) % 4, quarter + (k + 3) // 4 - 1)
                dve.wait_ge(sem("w"), 64)
                rows(0, 0)
                rows(1, 1)
                hidden(0, 0)
                rows(2, 0)
                hidden(1, 1)
                tiles(dve, step)
                result(SLOTS - 1, 3, SLOTS // 4 - 1)


def combine(nc, hT, ident, y_dram, dest, best, out):
    with ExitStack() as ctx:
        n = Names(nc, ctx, "comb")
        sem = n.sem
        ids = [n.sb(f"ids{p}", [128, CT], U32) for p in range(2)]
        rows = [n.sb(f"rows{p}", [128, CT, E]) for p in range(2)]
        hc = [n.sb(f"hc{p}", [128, CT * 128]) for p in range(2)]
        fin = [n.sb(f"fin{p}", [128, CT, E]) for p in range(2)]
        pr = [n.sb(f"pr{p}", [128, CT]) for p in range(2)]
        ps = [n.ps(f"ps{p}", [128, 512]) for p in range(2)]
        with nc.Block() as block:
            @block.gpsimd
            def _(pool):
                def chunk(k, p, half):
                    after(pool, sem("fin"), CT * (k - 1))
                    hold(pool, sem("pass"))
                    nc.gpsimd.tensor_copy(ids[p][:], dest[:, bass.ds(k * CT, CT)]).then_inc(sem("ids"), 1)
                    pool.wait_ge(sem("ids"), k + 1)
                    hold(pool, sem("pass"))
                    for c in range(CT):
                        nc.gpsimd.indirect_dma_start(
                            rows[p][:, c, :], None, y_dram[:, :],
                            bass.IndirectOffsetOnAxis(ap=ids[p][:, c:c + 1], axis=0)).then_inc(sem(f"rows{p}"), 16)
                chunks(pool, chunk)

            @block.scalar
            def _(act):
                def chunk(k, p, half):
                    after(act, sem("turned"), CT * (k - 1))
                    nc.scalar.activation(hc[p][:], hT[:, bass.ds(k * (CT * 128), CT * 128)], ACT.Copy
                                         ).then_inc(sem("hc"), 1)
                chunks(act, chunk)

            @block.tensor
            def _(pe):
                def chunk(k, p, half):
                    pe.wait_ge(sem("hc"), k + 1)
                    for c in range(CT):
                        after(pe, sem("fin"), k * CT + (c - 1))
                        nc.tensor.transpose(ps[(p * CT + c) % 2][:, 0:128], hc[p][:, c * 128:(c + 1) * 128],
                                            ident[:]).then_inc(sem("turned"), 1)
                chunks(pe, chunk)

            @block.vector
            def _(dve):
                def chunk(k, p, half):
                    after(dve, sem(f"store{p}"), 16 * half)
                    dve.wait_ge(sem(f"rows{p}"), 16 * CT * (half + 1))
                    nc.vector.tensor_copy(pr[p][:], best[:, bass.ds(k * CT, CT)]).then_inc(sem("pr"), 1)
                    dve.wait_ge(sem("pr"), k + 1)
                    for c in range(CT):
                        dve.wait_ge(sem("turned"), k * CT + (c + 1))
                        nc.vector.scalar_tensor_tensor(fin[p][:, c, :], rows[p][:, c, :], pr[p][:, c:c + 1],
                                                       ps[(p * CT + c) % 2][:, 0:128], ALU.mult,
                                                       ALU.add).then_inc(sem("fin"), 1)
                chunks(dve, chunk)

            @block.sync
            def _(sp):
                def chunk(k, p, half):
                    sp.wait_ge(sem("fin"), CT * (k + 1))
                    sp.dma_start(out[bass.ds(k * (CT * 128), CT * 128), :].rearrange("(c p) e -> p c e", p=128),
                                 fin[p][:]).then_inc(sem(f"store{p}"), 16)
                chunks(sp, chunk)
                sp.wait_ge(sem("store0"), 16 * ((NC + 1) // 2))
                sp.wait_ge(sem("store1"), 16 * (NC // 2))


def tower(nc, a, out):
    scratch = nc.dram_tensor("qk_parts", [2, 2 * PARTS, 128, 2 * TP], BF16).ap()
    rows_dram = nc.dram_tensor("tok_rows", [2, T, E], F32).ap()
    tT_dram = nc.dram_tensor("t_features", [E, NT], F32).ap()
    t_dram = nc.dram_tensor("t_tokens", [NT, E], F32).ap()
    sorted_dram = nc.dram_tensor("t_sorted", [SLOTS * 128, E], F32).ap()
    y_dram = nc.dram_tensor("y_sorted", [SLOTS * 128, E], F32).ap()
    with ExitStack() as ctx:
        hT = ctx.enter_context(nc.sbuf_tensor("hT", [128, NT], F32))
        ident = ctx.enter_context(nc.sbuf_tensor("ident", [128, 128], F32))
        ld = ctx.enter_context(nc.semaphore("ident_loaded"))
        with nc.Block() as block:
            @block.sync
            def _(sp):
                sp.dma_start(ident[:], a["ident"]).then_inc(ld, 16)
                sp.wait_ge(ld, 16)
        patch_tokens(nc, hT, ident, a["ximg"], a["xblk"], a["xpatch"], a["gam"], a["bet"], a["wtok"], a["btok"],
                     rows_dram)
        mats = (a["sel_num"], a["sel_den"], a["mean_w"])
        attention(nc, hT, ident, mats, (a["lsh_wq"], a["lsh_wv"], a["lsh_hyp"]), a["lsh_cols"], scratch, True, None)
        attention(nc, hT, ident, mats, (a["att_wq"], a["att_wv"], a["att_wk"], a["att_wo"]), a["att_cols"], scratch,
                  False, tT_dram)
        with ExitStack() as tail:
            dest = tail.enter_context(nc.sbuf_tensor("dest", [128, TILES], U32))
            best = tail.enter_context(nc.sbuf_tensor("best", [128, TILES], F32))
            tile_expert = tail.enter_context(nc.sbuf_tensor("tile_expert", [1, SLOTS], I32))
            logit = tail.enter_context(nc.sbuf_tensor("logit", [128, TILES, NE], F32))
            route(nc, hT, ident, tT_dram, t_dram, sorted_dram, a["gate_w"], a["gate_b"], a["prefix_w"], logit, dest,
                  best, tile_expert)
            experts(nc, ident, sorted_dram, y_dram, a["w1"], a["b1"], a["w2"], a["b2"], tile_expert)
            combine(nc, hT, ident, y_dram, dest, best, out)


def constants():
    num, den = np.zeros((128, 2, E), np.float32), np.zeros((128, 4), np.float32)
    for h in range(H):
        g, s = h // 4, h % 4
        for d in range(D):
            num[32 * s + d, g, h * D + d] = 1.0
        den[32 * s + D, s] = 1.0
    return {"sel_num": num, "sel_den": den, "mean_w": np.full((128, 128), 1.0 / E, np.float32),
            "ident": np.eye(128, dtype=np.float32), "prefix_w": np.triu(np.ones((128, 128), np.float32), 1)}


def layout(v):
    x = v["x"]
    wide = np.pad(x, ((0, 0), (0, 0), (HP, HP), (HP, HP)))

    def blocks(z, k):
        return z.reshape(IMG, CH, k, PATCH, k, PATCH).transpose(1, 3, 5, 2, 4, 0).reshape(E, k, k, IMG)

    def patches(z):
        return z.reshape(SRC, CH, GRID, PATCH, GRID, PATCH).transpose(1, 3, 5, 0, 2, 4).reshape(E, SRC, T)

    def columns(*arrays):
        c = np.zeros((E, 8), np.float32)
        for k, z in enumerate(arrays):
            c[:, k] = z
        return c
    hp = v["L0_attn_hyperplanes"]
    hyp, hyp_b = np.zeros((E, E), np.float32), np.zeros(E, np.float32)
    for h in range(H):
        hyp[h * D:(h + 1) * D, h * D:h * D + hp.shape[1]] = hp[:D]
        hyp_b[h * D:h * D + hp.shape[1]] = hp[D]
    W1, W2 = v["L0_ffn_W1"], v["L0_ffn_W2"]
    return {
        "ximg": x.reshape(IMG, 8, -1), "xblk": blocks(wide, NBLK), "xpatch": blocks(x, GRID),
        "gam": patches(v["L0_tok_gamma"]), "bet": patches(v["L0_tok_beta"]),
        "wtok": v["L0_tok_W"].reshape(E, SRC, CH, PATCH, PATCH).transpose(2, 3, 4, 1, 0).reshape(E, SRC, E),
        "btok": v["L0_tok_b"].reshape(1, E),
        "lsh_wq": v["L0_attn_Wq"], "lsh_wv": v["L0_attn_Wv"], "lsh_hyp": hyp,
        "lsh_cols": columns(v["L0_attn_bq"], hyp_b, v["L0_attn_bv"]),
        "att_wq": v["L0_ffn_Wq"], "att_wv": v["L0_ffn_Wv"], "att_wk": v["L0_ffn_Wk"], "att_wo": v["L0_ffn_Wo"],
        "att_cols": columns(*(v["L0_ffn_" + k] for k in ("bq", "bk", "bv", "bo", "ln1_g", "ln1_b"))),
        "gate_w": v["L0_ffn_gate_W"], "gate_b": np.broadcast_to(v["L0_ffn_gate_b"], (128, NE)),
        "w1": W1.transpose(1, 0, 2).reshape(E, NE * FF),
        "b1": np.broadcast_to(v["L0_ffn_b1"].reshape(1, -1), (128, NE * FF)),
        "w2": W2.reshape(NE, FF // 128, 128, E).transpose(2, 0, 1, 3).reshape(128, -1),
        "b2": np.broadcast_to(v["L0_ffn_b2"].reshape(1, -1), (128, NE * E)),
        **constants(),
    }


def kernel(**inputs):
    from concourse import bacc
    from concourse.bass_utils import run_bass_kernel_spmd

    nc = bacc.Bacc("TRN2", target_bir_lowering=False, num_devices=1)
    arrays = {k: np.ascontiguousarray(z) for k, z in layout({k: np.asarray(z) for k, z in inputs.items()}).items()}
    args = {k: nc.dram_tensor("in_" + k, z.shape, mybir.dt.from_np(z.dtype), kind="ExternalInput").ap()
            for k, z in arrays.items()}
    out = nc.dram_tensor("out", (NT, E), F32, kind="ExternalOutput").ap()
    tower(nc, args, out)
    result = run_bass_kernel_spmd(nc, [{"in_" + k: z for k, z in arrays.items()}], core_ids=[0])
    return result.results[0]["out"].reshape(IMG, T, E)
```

```python
from contextlib import ExitStack

import concourse.bass as bass
import numpy as np
from concourse import mybir

F32 = mybir.dt.float32
BF16 = mybir.dt.bfloat16
I32 = mybir.dt.int32
U32 = mybir.dt.uint32
ALU = mybir.AluOpType
ACT = mybir.ActivationFunctionType
AX = mybir.AxisListType

IMG, CH, SIDE, HP, PATCH = 128, 2, 104, 4, 8
GRID = SIDE // PATCH
T = GRID * GRID
NBLK = GRID + 1
E = 128
H, D = 8, 16
SRC = 5
PAIRS = IMG // 2
N2 = 2 * T
TP = 192
REM = T - 128
NT = IMG * T
TILES = NT // 128
NE, FF = 8, 512
SLOTS = TILES + NE - 1
CT = 13
NC = TILES // CT
BODY = 8
DUMP = BODY * 128
ROW = E + 1
EPS_TOK, EPS_LN = 1e-7, 1e-5


def after(eng, sem, value):
    if isinstance(value, int) and value <= 0:
        return
    eng.wait_ge(sem, value)


RSQRT_MAGIC = float(0x5F3759DF)
RSQRT_OPS = 11
NEWTON_OPS = 12


def rsqrt(nc, eng, sem, before, v, y, t, bits):
    ops = nc.vector
    done = 0

    def link(ins):
        nonlocal done
        done += 1
        ins.then_inc(sem, 1)
        eng.wait_ge(sem, before + done)
    link(ops.tensor_scalar(bits, v.bitcast(I32), 1, None, ALU.arith_shift_right))
    link(ops.tensor_scalar(y.bitcast(I32), bits, -1.0, RSQRT_MAGIC, ALU.mult, ALU.add))
    for _ in range(3):
        link(ops.tensor_tensor(t, y, y, ALU.mult))
        link(ops.scalar_tensor_tensor(t, t, -0.5, v, ALU.mult, ALU.mult))
        link(ops.scalar_tensor_tensor(y, t, 1.5, y, ALU.add, ALU.mult))
    assert done == RSQRT_OPS


def hold(pool, passed):
    pool.sem_inc(passed, 1)


class Names:

    def __init__(self, nc, ctx, stage):
        self.nc, self.ctx, self.stage, self.sems = nc, ctx, stage, {}

    def sem(self, name):
        if name not in self.sems:
            self.sems[name] = self.ctx.enter_context(self.nc.semaphore(f"{self.stage}_{name}"))
        return self.sems[name]

    def clear(self):
        with self.nc.Block() as block:
            @block.gpsimd
            def _(pool):
                for s in self.sems.values():
                    pool.sem_clear(s)

    def sb(self, name, shape, dt=F32):
        return self.ctx.enter_context(self.nc.sbuf_tensor(f"{self.stage}_{name}", shape, dt))

    def ps(self, name, shape, dt=F32):
        return self.ctx.enter_context(self.nc.psum_tensor(f"{self.stage}_{name}", shape, dt))


def patch_tokens(nc, hT, ident, ximg, xblk, xpatch, gam, bet, wtok, btok, rows_dram, sorted_dram):
    NCH = 8
    RC = CH * SIDE // NCH
    NALL = 2 * SRC * SIDE * SIDE
    INN = SIDE - 2 * HP
    WSUM = CH * (2 * SIDE * SIDE + 2 * INN * SIDE + INN * INN)
    with ExitStack() as ctx:
        n = Names(nc, ctx, "tok")
        sem = n.sem
        xi = n.sb("xi", [128, NCH, RC * SIDE])
        sq = n.sb("sq", [128, 2, RC * SIDE])
        gam_sb = n.sb("gam", [128, SRC, T])
        bet_sb = n.sb("bet", [128, SRC, T])
        w_sb = n.sb("w", [128, SRC, E])
        b_row = n.sb("b_row", [1, E])
        one_row = n.sb("one_row", [1, T])
        rall = n.sb("rall", [128, CH * SIDE])
        redge = n.sb("redge", [128, CH * SIDE])
        st = n.sb("st", [128, 12])
        bits = n.sb("bits", [128, 1], I32)
        ms = n.sb("ms", [128, 2])
        msT = n.sb("msT", [2, 128])
        rwide = n.sb("rwide", [128, 128])
        rb = n.sb("rb", [128, 128])
        gb_sb = n.sb("gb_sb", [128, 2, 2, E])
        psg = n.ps("psg", [128, 2, 2, 128])
        psm = n.ps("psm", [128, 512])

        with nc.Block() as block:
            @block.sync
            def _(sp):
                sp.dma_start(w_sb[:], wtok).then_inc(sem("w"), 16)
                sp.dma_start(gam_sb[:], gam).then_inc(sem("w"), 16)
                sp.dma_start(bet_sb[:], bet).then_inc(sem("w"), 16)
                sp.dma_start(b_row[:], btok).then_inc(sem("w"), 16)
                for c in range(NCH):
                    sp.dma_start(xi[:, c, :], ximg[:, c, :]).then_inc(sem(f"x{c}"), 16)
                sp.wait_ge(sem("gb"), 1)
                for r in range(2):
                    sp.dma_start(rows_dram[r, 0:128, :], gb_sb[:, 0, r, :]).then_inc(sem("rows"), 16)
                    sp.dma_start(rows_dram[r, 128:T, :], gb_sb[0:REM, 1, r, :]).then_inc(sem("rows"), 16)
                sp.wait_ge(sem("rows"), 64)

            @block.tensor
            def _(pe):
                pe.wait_ge(sem("w"), 64)
                pe.wait_ge(sem("ones"), 1)
                for tt, (t0, m) in enumerate(((0, 128), (128, REM))):
                    for s in range(SRC):
                        nc.tensor.matmul(psg[0:m, tt, 0, :], gam_sb[:, s, t0:t0 + m], w_sb[:, s, :],
                                         start=s == 0, stop=s == SRC - 1)
                    for s in range(SRC):
                        nc.tensor.matmul(psg[0:m, tt, 1, :], bet_sb[:, s, t0:t0 + m], w_sb[:, s, :],
                                         start=s == 0, stop=False)
                    last = nc.tensor.matmul(psg[0:m, tt, 1, :], one_row[:, t0:t0 + m], b_row[:],
                                            start=False, stop=True)
                last.then_inc(sem("g"), 1)
                pe.wait_ge(sem("ms"), 1)
                nc.tensor.matmul(psm[0:2, 0:128], ms[:], ident[:], start=True, stop=True)
                nc.tensor.matmul(psm[:, 128:256], rwide[:], ident[:], start=True, stop=True).then_inc(sem("mt"), 1)

            @block.scalar
            def _(act):
                act.wait_ge(sem("mean"), 1)
                for c in range(NCH):
                    if c >= 2:
                        act.wait_ge(sem("sqread"), c - 1)
                    nc.scalar.activation(sq[:, c % 2, :], xi[:, c, :], ACT.Square,
                                         bias=st[:, 4:5]).then_inc(sem("sq"), 1)

            @block.vector
            def _(dve):
                chain = [0]

                def link(ins):
                    chain[0] += 1
                    ins.then_inc(sem("chain"), 1)
                    dve.wait_ge(sem("chain"), chain[0])

                nc.vector.memset(one_row[:], 1.0).then_inc(sem("ones"), 1)

                def total(src, dst):
                    for c in range(CH):
                        base = c * SIDE
                        link(nc.vector.tensor_reduce(st[:, 0:1], rall[:, base:base + SIDE], AX.X, ALU.add))
                        link(nc.vector.tensor_reduce(st[:, 1:2], rall[:, base + HP:base + SIDE - HP], AX.X, ALU.add))
                        link(nc.vector.tensor_reduce(st[:, 2:3], redge[:, base:base + SIDE], AX.X, ALU.add))
                        link(nc.vector.tensor_reduce(st[:, 3:4], redge[:, base + HP:base + SIDE - HP], AX.X, ALU.add))
                        link(nc.vector.tensor_scalar(st[:, 0:1], st[:, 0:1], 3.0, None, ALU.mult))
                        link(nc.vector.scalar_tensor_tensor(st[:, 0:1], st[:, 1:2], 2.0, st[:, 0:1], ALU.mult, ALU.add))
                        link(nc.vector.tensor_tensor(st[:, 0:1], st[:, 0:1], st[:, 2:3], ALU.subtract))
                        link(nc.vector.tensor_tensor(st[:, 5 + c:6 + c], st[:, 0:1], st[:, 3:4], ALU.subtract))
                    link(nc.vector.tensor_tensor(dst, st[:, 5:6], st[:, 6:7], ALU.add))

                def rows(c, src):
                    v = src.rearrange("p (r c) -> p r c", c=SIDE)
                    nc.vector.tensor_reduce(rall[:, c * RC:(c + 1) * RC], v, AX.X, ALU.add)
                    edges = v.rearrange("p r (a b) -> p r a b", b=HP)[:, :, 0:SIDE // HP:SIDE // HP - 1, :]
                    return nc.vector.tensor_reduce(redge[:, c * RC:(c + 1) * RC], edges, AX.XY, ALU.add)

                for c in range(NCH):
                    dve.wait_ge(sem(f"x{c}"), 16)
                    last = rows(c, xi[:, c, :])
                link(last)
                total(None, st[:, 7:8])
                link(nc.vector.tensor_scalar(ms[:, 0:1], st[:, 7:8], 1.0 / NALL, None, ALU.mult))
                nc.vector.tensor_scalar(st[:, 4:5], ms[:, 0:1], -1.0, None, ALU.mult).then_inc(sem("mean"), 1)
                for c in range(NCH):
                    dve.wait_ge(sem("sq"), c + 1)
                    last = rows(c, sq[:, c % 2, :]).then_inc(sem("sqread"), 1)
                dve.wait_ge(sem("sqread"), NCH)
                total(None, st[:, 7:8])
                link(nc.vector.tensor_tensor(st[:, 10:11], ms[:, 0:1], ms[:, 0:1], ALU.mult))
                link(nc.vector.scalar_tensor_tensor(st[:, 8:9], st[:, 10:11], float(NALL - WSUM), st[:, 7:8],
                                                    ALU.mult, ALU.add))
                link(nc.vector.tensor_scalar(st[:, 8:9], st[:, 8:9], 1.0 / NALL, EPS_TOK, ALU.mult, ALU.add))
                rsqrt(nc, dve, sem("rsqrt"), 0, st[:, 8:9], st[:, 9:10], st[:, 11:12], bits[:])
                link(nc.vector.tensor_tensor(ms[:, 1:2], st[:, 8:9], st[:, 9:10], ALU.mult))
                dve.wait_ge(sem("g"), 1)
                for tt, m in enumerate((128, REM)):
                    nc.vector.tensor_scalar(gb_sb[0:m, tt, 0, :], psg[0:m, tt, 0, :], -1.0, None, ALU.mult)
                    last = nc.vector.tensor_copy(gb_sb[0:m, tt, 1, :], psg[0:m, tt, 1, :])
                last.then_inc(sem("gb"), 1)
                link(nc.vector.memset(rwide[:], 1.0))
                nc.vector.tensor_scalar(rwide[:], rwide[:], st[:, 9:10], None, ALU.mult).then_inc(sem("ms"), 1)
                dve.wait_ge(sem("mt"), 1)
                nc.vector.tensor_copy(msT[:], psm[0:2, 0:128])
                nc.vector.tensor_copy(rb[:], psm[:, 128:256])

        NW = 4
        ring = xi[:, :, :].rearrange("p a b -> p (a b)")
        XB = NBLK * IMG
        XP = GRID * IMG
        blk = [ring[:, r * XB:(r + 1) * XB].rearrange("p (j b) -> p j b", b=IMG) for r in range(4)]
        pat = [ring[:, 4 * XB + r * XP:4 * XB + (r + 1) * XP].rearrange("p (j b) -> p j b", b=IMG) for r in range(2)]
        off = 4 * XB + 2 * XP
        wg = [ring[:, off + r * SRC * E:off + (r + 1) * SRC * E].rearrange("p (s e) -> p s e", e=E) for r in range(NW)]
        off += NW * SRC * E
        gbr = [ring[0:2, off + r * GRID * E:off + (r + 1) * GRID * E] for r in range(2)]
        hv = hT[:, :].rearrange("p (b t) -> p b t", t=T)
        NB = 5
        pst = [n.ps(f"pst{k}", [128, 512]) for k in range(NB)]

        pools = [j for j in range(GRID) if j % 3 == 2]
        dves = [j for j in range(GRID) if j % 3 != 2]

        with nc.Block() as block:
            @block.scalar
            def _(act):
                zeros = sq[:, 0, 0:8 * ROW]
                act.wait_ge(sem("zeros"), 1)
                for k in range(SLOTS // 8):
                    act.dma_start(sorted_dram[k * 1024:(k + 1) * 1024, :].rearrange("(p r) e -> p (r e)", r=8),
                                  zeros).then_inc(sem("cleared"), 16)
                act.wait_ge(sem("cleared"), 16 * (SLOTS // 8))

            @block.sync
            def _(sp):
                sp.dma_start(blk[0], xblk[:, 0]).then_inc(sem("blk_first"), 16)

                def load(i, par):
                    after(sp, sem("done"), (i - 1) * GRID)
                    sp.dma_start(blk[(par + 1) % 4], xblk[:, bass.ds(i + 1, 1)]).then_inc(sem(f"blk{par % 2}"), 16)
                    sp.dma_start(pat[par % 2], xpatch[:, bass.ds(i, 1)]).then_inc(sem(f"blk{par % 2}"), 16)
                    sp.dma_start(gbr[par % 2], rows_dram[:, bass.ds(i * GRID, GRID), :].rearrange(
                        "r t e -> r (t e)")).then_inc(sem(f"blk{par % 2}"), 16)

                for i in range(5):
                    load(i, i)
                with sp.Fori(0, 2) as it:
                    for par in range(4):
                        load(it * 4 + (par + 5), par + 1)

            @block.gpsimd
            def _(pool):
                def row(i, par):
                    for j in pools:
                        after(pool, sem("done"), i * GRID + (j - NW + 1))
                        nc.gpsimd.tensor_tensor(wg[(par * GRID + j) % NW], w_sb[:, :, :],
                                                gam_sb[:, :, bass.ds(i * GRID + j, 1)].broadcast_to([128, SRC, E]),
                                                ALU.mult).then_inc(sem("wpool"), 1)
                row(0, 0)
                with pool.Fori(0, 3) as it:
                    for par in range(4):
                        row(it * 4 + par + 1, par + 1)

            @block.vector
            def _(dve):
                nc.vector.memset(sq[:, 0, 0:8 * ROW], 0.0).then_inc(sem("zeros"), 1)

                def evac(i, par, j):
                    dve.wait_ge(sem("done"), i * GRID + j + 1)
                    nc.vector.tensor_tensor(hv[:, :, bass.ds(i * GRID + j, 1)].rearrange("p b t -> p (b t)"),
                                            pst[j % NB][:, 0:IMG], rb[:], ALU.mult).then_inc(sem("out"), 1)

                def row(i, par):
                    for j in range(GRID):
                        if j in dves:
                            after(dve, sem("done"), i * GRID + (j - NW + 1))
                            nc.vector.tensor_tensor(wg[(par * GRID + j) % NW], w_sb[:, :, :],
                                                    gam_sb[:, :, bass.ds(i * GRID + j, 1)].broadcast_to([128, SRC, E]),
                                                    ALU.mult).then_inc(sem("wdve"), 1)
                        if j >= 2:
                            evac(i, par, j - 2)
                    evac(i, par, GRID - 2)
                    evac(i, par, GRID - 1)
                row(0, 0)
                with dve.Fori(0, 3) as it:
                    for par in range(4):
                        row(it * 4 + par + 1, par + 1)

            @block.tensor
            def _(pe):
                def row(i, par, half):
                    pe.wait_ge(sem(f"blk{par % 2}"), 48 * (half + 1))
                    for j in range(GRID):
                        if j in pools:
                            pe.wait_ge(sem("wpool"), i * len(pools) + pools.index(j) + 1)
                        else:
                            pe.wait_ge(sem("wdve"), i * len(dves) + dves.index(j) + 1)
                        after(pe, sem("out"), i * GRID + (j - NB + 1) if j >= NB else i * GRID)
                        w = wg[(par * GRID + j) % NW]
                        acc = pst[j % NB][:, 0:IMG]
                        top, low = blk[par % 4], blk[(par + 1) % 4]
                        for s, x in enumerate((pat[par % 2][:, j, :], low[:, j, :], low[:, j + 1, :],
                                               top[:, j, :], top[:, j + 1, :])):
                            nc.tensor.matmul(acc, w[:, s, :], x, start=s == 0, stop=False)
                        nc.tensor.matmul(acc, gbr[par % 2][:, j * E:(j + 1) * E], msT[:], start=False,
                                         stop=True).then_inc(sem("done"), 1)
                pe.wait_ge(sem("blk_first"), 16)
                row(0, 0, 0)
                with pe.Fori(0, 3) as it:
                    for par in range(4):
                        row(it * 4 + par + 1, par + 1, it * 2 + (par + 1) // 2)
        n.clear()


PARTS = 3
Q_OF = (0, 0, 1, 1, 0, 2)
K_OF = (0, 1, 0, 1, 2, 0)
KQ = len(Q_OF) * D
KB = KQ + D
UNITS = 8


def attention(nc, hT, ident, mats, weights, cols, scratch, lsh, tT_dram):
    stage = "lsh" if lsh else "att"
    scale = 1.0 / float(np.sqrt(E)) if lsh else 0.25
    NSIDE = 1 if lsh else 2
    NP = PARTS + 1 if lsh else 2 * PARTS
    LOADS = (2 * len(Q_OF) + 2) if lsh else 2 * len(Q_OF)
    with ExitStack() as ctx:
        n = Names(nc, ctx, stage)
        sem = n.sem
        wq = n.sb("wq", [128, E])
        wv = n.sb("wv", [128, E])
        wk = n.sb("wk", [128, E]) if not lsh else None
        wo = n.sb("wo", [128, E]) if not lsh else None
        hyp = n.sb("hyp", [128, E]) if lsh else None
        col = n.sb("col", [128, 8])
        sel_num = n.sb("sel_num", [128, 2, E])
        rest_ident = n.sb("rest_ident", [128, REM])
        rest_head = n.sb("rest_head", [128, 2 * E])
        mean_w = n.sb("mean_w", [128, 128])
        cent = n.sb("cent", [128, N2])
        sqr = n.sb("sqr", [128, N2])
        var, vneg, rstd, nwt, half3 = (n.sb(x, [128, 4]) for x in ("var", "vneg", "rstd", "nwt", "half3"))
        nbits = n.sb("nbits", [128, 4], I32)
        NXH = 2 if lsh else 4
        xh = [n.sb(f"xh{p}", [128, N2]) for p in range(NXH)]
        qf = n.sb("qf", [128, N2])
        kf = n.sb("kf", [128, N2]) if not lsh else None
        rst = n.sb("rst", [128, N2])
        att = n.sb("att", [128, N2])
        prj = n.sb("prj", [128, N2]) if lsh else None
        parts = n.sb("parts", [128, NP, 2 * TP], BF16)
        qs = [n.sb(f"qs{p}", [KB, H, 2 * TP], BF16) for p in range(2)]
        ks = [n.sb(f"ks{p}", [KB, H, 2 * TP], BF16) for p in range(2)]
        kb = [n.sb(f"kb{p}", [KB, H, 2 * TP], BF16) for p in range(2)] if lsh else None
        vm = [n.sb(f"vm{p}", [128, 2, H, 32]) for p in range(2)]
        vr = [n.sb(f"vr{p}", [128, 2, H, 32]) for p in range(2)]
        fac = [n.sb(f"fac{p}", [128, 3 * T], BF16) for p in range(2)] if lsh else None
        scr = [n.sb(f"scr{p}", [128, 3 * T]) for p in range(2)] if lsh else None
        mx = [n.sb(f"mx{p}", [128, 3]) for p in range(2)]
        nm = [n.sb(f"nm{p}", [128, 3]) for p in range(2)]
        prob = [n.sb(f"prob{p}", [128, 3 * T]) for p in range(2)]
        ptm = [n.sb(f"ptm{p}", [128, 2 * TP]) for p in range(2)]
        ptr = [n.sb(f"ptr{p}", [128, 2 * TP]) for p in range(2)]
        osb = n.sb("osb", [128, 2, N2])
        num = n.sb("num", [128, N2])
        sums = [n.sb(f"sums{p}", [128, 3 * UNITS]) for p in range(2)]
        rec = n.sb("rec", [128, 3 * UNITS])
        rec_wide = n.sb("rec_wide", [128, 2, 2, E])
        if not lsh:
            oh, yy, cent2, sqr2, nrm2, tt = (n.sb(x, [128, N2]) for x in ("oh", "yy", "cent2", "sqr2", "nrm2", "tt"))
            var2, vneg2, rstd2 = (n.sb(x, [128, 4]) for x in ("var2", "vneg2", "rstd2"))
        g0, g1 = n.ps("g0", [128, 512]), n.ps("g1", [128, 512])
        ps_s = [n.ps("s0", [128, 512])]
        ps_f = n.ps("f", [128, 512]) if lsh else None
        if not lsh:
            ps_s.append(n.ps("s1", [128, 512]))
        NS = len(ps_s)
        ps_tm, ps_tr = n.ps("tm", [128, 512]), n.ps("tr", [128, 512])
        ps_o = [n.ps(f"o{g}", [128, 512]) for g in range(2)]

        CONST = len(weights) + 5
        b_norm, b_den = (1, 0) if lsh else (0, 1)
        g_norm, g_den = (g0, g1)[b_norm], (g0, g1)[b_den]

        def consts(eng):
            eng.wait_ge(sem("const"), 16 * CONST)
            eng.wait_ge(sem("zero"), 1)

        def parts_made(eng, pairs_done):
            if lsh:
                after(eng, sem("parts"), pairs_done)
            else:
                after(eng, sem("split"), 4 * NSIDE * pairs_done)

        def both(ap):
            return ap.rearrange("p (i t) -> p i t", t=TP)[:, :, 0:T]

        def two(ap):
            return ap.rearrange("p (i t) -> p i t", t=T)

        def h_of(i):
            return hT[:, bass.ds(i * N2, N2)]

        UNROLL = 2 if lsh else 4

        def pairs(eng, head, step):
            head()
            step(0, 0, 0)
            step(1, 1, 0)
            with eng.Fori(0, (PAIRS - 4) // UNROLL) as it:
                for k in range(UNROLL):
                    step(it * UNROLL + (2 + k), (2 + k) % 4, it * (UNROLL // 2) + (2 + k) // 2)
            step(PAIRS - 2, (PAIRS - 2) % 4, (PAIRS - 2) // 2)
            step(PAIRS - 1, (PAIRS - 1) % 4, (PAIRS - 1) // 2)

        def is_last(i, k):
            return isinstance(i, int) and i + k >= PAIRS

        def first(i):
            return isinstance(i, int) and i == 0

        with nc.Block() as block:
            @block.sync
            def _(sp):
                for dst, src in zip((wq, wv, hyp) if lsh else (wq, wv, wk, wo), weights):
                    sp.dma_start(dst[:], src).then_inc(sem("const"), 16)
                sp.dma_start(col[:], cols).then_inc(sem("const"), 16)
                sp.dma_start(sel_num[:], mats[0]).then_inc(sem("const"), 16)
                sp.dma_start(rest_ident[:], mats[1]).then_inc(sem("const"), 16)
                sp.dma_start(rest_head[:], mats[2]).then_inc(sem("const"), 16)
                sp.dma_start(mean_w[:], mats[3]).then_inc(sem("const"), 16)
                sp.wait_ge(sem("zero"), 1)

                def stack(i, par):
                    parts_made(sp, i + 1)
                    sp.dma_start(scratch[par, 0:NP].rearrange("s p t -> p s t"), parts[:]).then_inc(sem("store"), 16)
                    sp.wait_ge(sem("store"), 16 * (i + 1))
                    after(sp, sem("s"), UNITS * (i - 1))
                    if lsh:
                        after(sp, sem("f"), UNITS * (i - 1))

                    def load(dst, row, part):
                        sp.dma_start(dst[row:row + D], scratch[par, part].rearrange(
                            "(h d) t -> d h t", d=D)).then_inc(sem(f"load{par}"), 16)
                    for j, (a, b) in enumerate(zip(Q_OF, K_OF)):
                        load(qs[par], j * D, a)
                        load(ks[par], j * D, b if lsh else b + PARTS)
                    if lsh:
                        load(qs[par], KQ, PARTS)
                        load(kb[par], KQ, PARTS)

                def head():
                    stack(0, 0)
                    stack(1, 1)

                def step(i, m, half):
                    if not is_last(i, 2):
                        stack(i + 2, m % 2)
                    if not lsh and not first(i) and not first(i - 1):
                        sp.wait_ge(sem("tt"), i - 1)
                        sp.dma_start(tT_dram[:, bass.ds((i - 2) * N2, N2)], tt[:]).then_inc(sem("out"), 16)
                pairs(sp, head, step)
                if not lsh:
                    for i in (PAIRS - 2, PAIRS - 1):
                        sp.wait_ge(sem("tt"), i + 1)
                        sp.dma_start(tT_dram[:, i * N2:(i + 1) * N2], tt[:]).then_inc(sem("out"), 16)
                    sp.wait_ge(sem("out"), 16 * PAIRS)

            @block.tensor
            def _(pe):
                mm = nc.tensor.matmul
                reader = [None, None]

                def bank(b, i, name, m, c):
                    if reader[b]:
                        pe.wait_ge(sem(reader[b][0]), i * reader[b][1] + reader[b][2])
                    reader[b] = (name, m, c)
                    return (g0, g1)[b]

                def next_step():
                    for b in range(2):
                        if reader[b]:
                            name, m, c = reader[b]
                            reader[b] = (name, m, c - m)

                def mean(i, b):
                    g = bank(b, i, "cent", 1, 3)
                    mm(g[:, 0:N2], mean_w[:], h_of(i + 2), start=True, stop=True).then_inc(sem("mean"), 1)

                def token_means(g, x):
                    for im in range(2):
                        for k, t0 in enumerate((im * T, im * T + REM)):
                            last = mm(g[:, 2 * im + k:2 * im + k + 1], x[:, t0:t0 + 128], mean_w[:, 0:1],
                                      start=True, stop=True)
                    return last

                def spread(g, column, rest):
                    for im in range(2):
                        mm(g[:, im * T:im * T + 128], column(im, 0), ident[:], start=True, stop=True)
                        last = mm(g[:, im * T + 128:(im + 1) * T], column(im, 1), rest, start=True, stop=True)
                    return last

                def spread_deviation(g, x):
                    return spread(g, lambda im, k: x[:, 2 * im + k:2 * im + k + 1].broadcast_to([128, 128]),
                                  ident[:, 128 - REM:128])

                def variance(i, b):
                    g = bank(b, i, "vcp", 1, 3)
                    pe.wait_ge(sem("sq"), i + 3)
                    token_means(g, sqr).then_inc(sem("var"), 1)

                def deviation(i, b):
                    g = bank(b, i, "xh", 1, 3)
                    pe.wait_ge(sem("rs"), NEWTON_OPS * (i + 3))
                    spread_deviation(g, rstd).then_inc(sem("rbc"), 1)

                def project(w, i, m, b, name, name_read):
                    g = bank(b, i, name_read, 1, 3)
                    pe.wait_ge(sem("xh"), i + 3)
                    mm(g[:, 0:N2], w[:], xh[(m + 2) % NXH][:], start=True, stop=True).then_inc(sem(name), 1)

                def hyperplanes(i, b):
                    g = bank(b, i, "prc", 1, 3)
                    pe.wait_ge(sem("qf"), i + 3)
                    mm(g[:, 0:N2], hyp[:], qf[:], start=True, stop=True).then_inc(sem("pr"), 1)

                def values(i, m, b):
                    g = bank(b, i, "v_copied", 1, 2)
                    pe.wait_ge(sem("xh"), i + 2)
                    for im in range(2):
                        x = xh[(m + 1) % NXH][:, im * T:(im + 1) * T]
                        mm(g[:, im * E:(im + 1) * E], x[:, 0:128], wv[:], start=True, stop=True)
                        last = mm(g[0:REM, (2 + im) * E:(3 + im) * E], x[:, 128:T], wv[:], start=True, stop=True)
                    last.then_inc(sem("v"), 1)

                def scores(i, par, half, u):
                    im, a = u // 4, 2 * (u % 4)
                    n_u = i * UNITS + u
                    if u == 0:
                        pe.wait_ge(sem(f"load{par}"), 16 * LOADS * (half + 1))
                    def products(dst, rows, k):
                        q0 = im * TP
                        for x in range(2):
                            mm(dst[:, x * T:(x + 1) * T], qs[par][0:rows, a + x, q0:q0 + 128],
                               k[par][0:rows, a + x, q0:q0 + T], start=True, stop=True)
                            last = mm(dst[64 * x:64 * x + 64, 2 * T:3 * T], qs[par][0:rows, a + x, q0 + 128:q0 + TP],
                                      k[par][0:rows, a + x, q0:q0 + T], start=True, stop=True)
                        return last
                    if lsh:
                        after(pe, sem("f_read"), n_u)
                        products(ps_f, KB, kb).then_inc(sem("f"), 1)
                    after(pe, sem("scr" if lsh else "exp"), n_u - (NS - 1))
                    products(ps_s[u % NS], KQ, ks).then_inc(sem("s"), 1)

                def transposes(i, u):
                    n_u = i * UNITS + u
                    pe.wait_ge(sem("exp"), n_u + 1)
                    after(pe, sem("tm_read"), n_u)
                    after(pe, sem("tr_read"), n_u)
                    p = prob[u % 2]
                    for x in range(2):
                        nc.tensor.transpose(ps_tm[:, x * TP:x * TP + 128], p[:, x * T:x * T + 128], ident[:])
                        nc.tensor.transpose(ps_tr[0:REM, x * TP:x * TP + 128], p[:, x * T + 128:(x + 1) * T], ident[:])
                    rest_m = ps_tm[:, 0:2 * TP].rearrange("p (x t) -> p x t", t=TP)[:, :, 128:TP]
                    rest_r = ps_tr[0:REM, 0:2 * TP].rearrange("p (x t) -> p x t", t=TP)[:, :, 128:TP]
                    nc.tensor.transpose(rest_m, p[:, 2 * T:2 * T + 128], ident[:])
                    nc.tensor.transpose(rest_r, p[:, 2 * T + 128:3 * T], ident[:]).then_inc(sem("t"), 1)

                def weighted(i, par, u):
                    im, a = u // 4, 2 * (u % 4)
                    n_u = i * UNITS + u
                    pe.wait_ge(sem("tm_read"), n_u + 1)
                    pe.wait_ge(sem("tr_read"), n_u + 1)
                    if u == 0:
                        pe.wait_ge(sem("v_copied"), i + 1)
                        after(pe, sem("o0"), i)
                        after(pe, sem("o1"), i)
                    for x in range(2):
                        hd = a + x
                        out = ps_o[hd // 4][32 * (hd % 4):32 * (hd % 4) + 32, im * T:(im + 1) * T]
                        mm(out, vm[par][:, im, hd, :], ptm[u % 2][:, x * TP:x * TP + T], start=True, stop=False)
                        last = mm(out, vr[par][:, im, hd, :], ptr[u % 2][:, x * TP:x * TP + T], start=False, stop=True)
                    last.then_inc(sem("pv"), 1)

                def finish(i):
                    pe.wait_ge(sem("o0"), i)
                    pe.wait_ge(sem("o1"), i)
                    g = bank(0, i, "num_copied", 1, 0)
                    mm(g[:, 0:N2], sel_num[:, 0, :], osb[:, 0, :], start=True, stop=False)
                    mm(g[:, 0:N2], sel_num[:, 1, :], osb[:, 1, :], start=False, stop=True).then_inc(sem("num"), 1)

                def spread_denominators(i, b):
                    g = bank(b, i, "tn", 1, 0)
                    pe.wait_ge(sem("rec_wide"), i)
                    spread(g, lambda im, k: rec_wide[:, k, im, :], rest_ident[:]).then_inc(sem("dbc"), 1)

                def output(i, k):
                    ready, done, read = (("oh", "wo", "yy"), ("yy", "mean2", "cent2"), ("sq2", "var2", "vcp2"))[k]
                    g = bank(1, i, read, 1, 0)
                    pe.wait_ge(sem(ready), i)
                    if k == 2:
                        last = token_means(g, sqr2)
                    else:
                        w, x = ((wo, oh), (mean_w, yy))[k]
                        last = mm(g[:, 0:N2], w[:], x[:], start=True, stop=True)
                    last.then_inc(sem(done), 1)

                def deviation2(i, back):
                    g = bank(1, i, "tn2", 1, 1 - back)
                    pe.wait_ge(sem("rs2"), (i + (1 - back)) * NEWTON_OPS)
                    spread_deviation(g, rstd2).then_inc(sem("rbc2"), 1)

                def head():
                    consts(pe)
                    for a in (-2, -1):
                        mean(a, 0)
                        variance(a, 1)
                        deviation(a, 0)
                        project(wq, a, a, 1, "q", "qf")
                        if lsh:
                            hyperplanes(a, 0)
                        else:
                            project(wk, a, a, 0, "k", "kf")
                        if a == -2:
                            next_step()
                    values(-1, -1, 1)
                    scores(0, 0, 0, 0)
                    scores(0, 0, 0, 1)

                def step(i, m, half):
                    par = m % 2
                    next_step()
                    have_a, have_v = not is_last(i, 2), not is_last(i, 1)
                    for u in range(UNITS):
                        if u < 6:
                            scores(i, par, half, u + 2)
                        elif have_v:
                            scores(i + 1, 1 - par, half + par, u - 6)
                        transposes(i, u)
                        if u > 0:
                            weighted(i, par, u - 1)
                        elif not first(i):
                            weighted(i - 1, 1 - par, UNITS - 1)
                        later = not lsh and not first(i)
                        if u == 0 and have_a:
                            mean(i, 1)
                        if u == 1 and not first(i):
                            finish(i)
                        if u == (3 if lsh else 1) and not first(i):
                            spread_denominators(i, b_den)
                        if u == 2 and have_a:
                            variance(i, b_norm)
                        if u == 3 and later and not first(i - 1):
                            deviation2(i, 2)
                        if u == 4 and later:
                            output(i, 0)
                        if u == 4 and have_a:
                            deviation(i, b_norm)
                        if u == 5 and later:
                            output(i, 1)
                        if u == 5 and have_a:
                            project(wq, i, m, b_norm, "q", "qf")
                        if u == 6 and have_a and not lsh:
                            project(wk, i, m, 0, "k", "kf")
                        if u == 6 and have_v:
                            values(i, m, b_den)
                        if u == 7 and have_a and lsh:
                            hyperplanes(i, 1)
                        if u == 7 and later:
                            output(i, 2)
                pairs(pe, head, step)
                weighted(PAIRS - 1, 1, UNITS - 1)
                next_step()
                finish(PAIRS)
                spread_denominators(PAIRS, b_den)
                if not lsh:
                    deviation2(PAIRS, 2)
                    for k in range(3):
                        output(PAIRS, k)
                    deviation2(PAIRS, 1)

            @block.scalar
            def _(act):
                fn = nc.scalar.activation

                def factors(i, u):
                    n_u = i * UNITS + u
                    act.wait_ge(sem("f"), n_u + 1)
                    after(act, sem("scr"), n_u - 1)
                    fn(fac[u % 2][:], ps_f[:, 0:3 * T], ACT.Copy, bias=-1.0, scale=8.0).then_inc(sem("f_read"), 1)

                def exponentials(i, par, u):
                    n_u = i * UNITS + u
                    act.wait_ge(sem("nm"), n_u + 1)
                    after(act, sem("t"), n_u - 1)
                    if u == 0:
                        after(act, sem("rec"), i - 1)
                    src = scr[u % 2] if lsh else ps_s[u % NS]
                    for x in range(3):
                        c = 2 * u + x if x < 2 else 2 * UNITS + u
                        last = fn(prob[u % 2][:, x * T:(x + 1) * T], src[:, x * T:(x + 1) * T], ACT.Exp,
                                  bias=nm[u % 2][:, x:x + 1], scale=scale, accum_out=sums[par][:, c:c + 1])
                    last.then_inc(sem("exp"), 1)

                def rest_keys(i, u):
                    n_u = i * UNITS + u
                    act.wait_ge(sem("t"), n_u + 1)
                    after(act, sem("pv"), n_u - 1)
                    fn(ptr[u % 2][0:REM, :], ps_tr[0:REM, 0:2 * TP], ACT.Copy).then_inc(sem("tr_read"), 1)

                def square(i):
                    act.wait_ge(sem("cent"), i + 3)
                    after(act, sem("var"), i + 2)
                    fn(sqr[:], cent[:], ACT.Square).then_inc(sem("sq"), 1)

                def with_bias(i, dst, g, bias, name, done):
                    act.wait_ge(sem(name), i + 3)
                    parts_made(act, i + 2)
                    fn(dst[:], g[:, 0:N2], ACT.Identity, bias=col[:, bias:bias + 1]).then_inc(sem(done), 1)

                def v_copy(i, par, g):
                    act.wait_ge(sem("v"), i + 2)
                    after(act, sem("pv"), UNITS * i)
                    fn(vm[par][:, :, :, 0:D], g[:, 0:2 * E].rearrange("p (i h d) -> p i h d", i=2, d=D), ACT.Copy)
                    fn(vr[par][0:REM, :, :, 0:D], g[0:REM, 2 * E:4 * E].rearrange("p (i h d) -> p i h d", i=2, d=D),
                       ACT.Copy).then_inc(sem("v_copied"), 1)

                def v_bias(i):
                    act.wait_ge(sem("tn"), i)
                    after(act, sem("wo"), i - 1)
                    fn(oh[:], att[:], ACT.Identity, bias=col[:, 2:3]).then_inc(sem("oh"), 1)

                def numerators(i):
                    act.wait_ge(sem("num"), i)
                    after(act, sem("tn"), i - 1)
                    fn(num[:], g0[:, 0:N2], ACT.Copy).then_inc(sem("num_copied"), 1)

                def head():
                    consts(act)
                    for a in (-2, -1):
                        square(a)
                        with_bias(a, qf, g1, 0, "q", "qf")
                        if lsh:
                            with_bias(a, prj, g0, 1, "pr", "prc")
                        else:
                            with_bias(a, kf, g0, 1, "k", "kf")
                    v_copy(-1, 0, g1)
                    if lsh:
                        factors(0, 0)
                        factors(0, 1)

                def step(i, m, half):
                    have_a, have_v = not is_last(i, 2), not is_last(i, 1)
                    for u in range(UNITS):
                        exponentials(i, m % 2, u)
                        if u > 0:
                            rest_keys(i, u - 1)
                        elif not first(i):
                            rest_keys(i - 1, UNITS - 1)
                        if lsh and u < 6:
                            factors(i, u + 2)
                        elif lsh and have_v:
                            factors(i + 1, u - 6)
                        if u == 0 and not first(i):
                            if lsh and not is_last(i, 1):
                                with_bias(i - 1, prj, g1, 1, "pr", "prc")
                            outputs(i)
                        if u == 2 and not first(i):
                            numerators(i)
                        if u == 2 and have_a:
                            square(i)
                        if u == 3 and not lsh and not first(i):
                            v_bias(i)
                        if u == 6 and have_a:
                            with_bias(i, qf, g_norm, 0, "q", "qf")
                        if u == 7 and have_a and not lsh:
                            with_bias(i, kf, g0, 1, "k", "kf")
                        if u == 7 and have_v:
                            v_copy(i, (m + 1) % 2, g_den)
                        if u == 7 and not lsh and not first(i):
                            square2(i)

                def outputs(i):
                    act.wait_ge(sem("pv"), UNITS * i)
                    after(act, sem("num"), i - 1)
                    fn(osb[:, 1, :], ps_o[1][:, 0:N2], ACT.Copy).then_inc(sem("o1"), 1)

                def square2(i):
                    act.wait_ge(sem("cent2"), i)
                    after(act, sem("var2"), i - 1)
                    fn(sqr2[:], cent2[:], ACT.Square).then_inc(sem("sq2"), 1)

                pairs(act, head, step)
                rest_keys(PAIRS - 1, UNITS - 1)
                outputs(PAIRS)
                numerators(PAIRS)
                if not lsh:
                    v_bias(PAIRS)
                if not lsh:
                    square2(PAIRS)

            @block.vector
            def _(dve):
                def row_max(i, u, between):
                    n_u = i * UNITS + u
                    dve.wait_ge(sem("s"), n_u + 1)
                    if lsh:
                        dve.wait_ge(sem("f_read"), n_u + 1)
                        after(dve, sem("exp"), n_u - 1)
                        nc.vector.scalar_tensor_tensor(scr[u % 2][:], fac[u % 2][:], 30.0, ps_s[0][:, 0:3 * T],
                                                       ALU.max, ALU.mult).then_inc(sem("scr"), 1)
                        between()
                        dve.wait_ge(sem("scr"), n_u + 1)
                    src = scr[u % 2] if lsh else ps_s[u % NS]
                    nc.vector.tensor_reduce(mx[u % 2][:], src[:, 0:3 * T].rearrange("p (x t) -> p x t", t=T),
                                            AX.X, ALU.max).then_inc(sem("mx"), 1)
                    if not lsh:
                        between()
                    dve.wait_ge(sem("mx"), n_u + 1)
                    after(dve, sem("exp"), n_u - 1)
                    nc.vector.tensor_scalar(nm[u % 2][:], mx[u % 2][:], -scale, None, ALU.mult).then_inc(sem("nm"), 1)

                def main_keys(i, u):
                    n_u = i * UNITS + u
                    dve.wait_ge(sem("t"), n_u + 1)
                    after(dve, sem("pv"), n_u - 1)
                    nc.vector.tensor_copy(ptm[u % 2][:], ps_tm[:, 0:2 * TP]).then_inc(sem("tm_read"), 1)

                def center(i, g):
                    dve.wait_ge(sem("mean"), i + 3)
                    after(dve, sem("sq"), i + 2)
                    after(dve, sem("xh"), i + 2)
                    nc.vector.tensor_tensor(cent[:], h_of(i + 2), g[:, 0:N2], ALU.subtract).then_inc(sem("cent"), 1)

                def guess(g, v, vn, y, ready, copied, spread_done, seeded, newton, nth):
                    dve.wait_ge(sem(ready), nth + 1)
                    after(dve, sem(newton), nth * NEWTON_OPS)
                    after(dve, sem(spread_done), nth)
                    nc.vector.tensor_scalar(v[:], g[:, 0:4], EPS_LN, None, ALU.add).then_inc(sem(copied), 1)
                    dve.wait_ge(sem(copied), nth + 1)
                    nc.vector.tensor_scalar(nbits[:], v[:].bitcast(I32), 1, None,
                                            ALU.arith_shift_right).then_inc(sem(seeded), 1)
                    dve.wait_ge(sem(seeded), 3 * nth + 1)
                    nc.vector.tensor_scalar(vn[:], v[:], -0.5, None, ALU.mult).then_inc(sem(seeded), 1)
                    nc.vector.tensor_scalar(y[:].bitcast(I32), nbits[:], -1.0, RSQRT_MAGIC, ALU.mult,
                                            ALU.add).then_inc(sem(seeded), 1)

                def normal(i, m, g):
                    dve.wait_ge(sem("rbc"), i + 3)
                    dve.wait_ge(sem("cent"), i + 3)
                    if not first(i + 2):
                        after(dve, sem("v"), i + 3 - NXH)
                        if not lsh:
                            after(dve, sem("yy"), i + 3 - NXH)
                            after(dve, sem("k"), i + 3 - NXH)
                        after(dve, sem("q"), i + 3 - NXH)
                    nc.vector.tensor_tensor(xh[(m + 2) % NXH][:], cent[:], g[:, 0:N2], ALU.mult).then_inc(sem("xh"), 1)

                def outputs(i):
                    dve.wait_ge(sem("pv"), UNITS * i)
                    after(dve, sem("num"), i - 1)
                    nc.vector.tensor_copy(osb[:, 0, :], ps_o[0][:, 0:N2]).then_inc(sem("o0"), 1)

                def denominators(i, par):
                    dve.wait_ge(sem("exp"), UNITS * i)
                    after(dve, sem("rec_wide"), i - 1)
                    nc.vector.reciprocal(rec[:], sums[par][:]).then_inc(sem("rec"), 1)
                    dve.wait_ge(sem("rec"), i)
                    after(dve, sem("dbc"), i - 1)
                    nc.vector.tensor_copy(
                        rec_wide[:, 0, :, :].rearrange("p i (h d) -> p (i h) d", d=D),
                        rec[:, 0:2 * UNITS].rearrange("p (h o) -> p h o", o=1).broadcast_to([128, 2 * UNITS, D]))
                    nc.vector.tensor_tensor(
                        rec_wide[:, 1, :, :].rearrange("p i (u f) -> p (i u) f", f=2 * D),
                        rec[:, 2 * UNITS:3 * UNITS].rearrange("p (h o) -> p h o", o=1).broadcast_to(
                            [128, UNITS, 2 * D]),
                        rest_head[:, :].rearrange("p (u f) -> p u f", f=2 * D), ALU.mult).then_inc(sem("rec_wide"), 1)

                def divide(i):
                    dve.wait_ge(sem("dbc"), i)
                    dve.wait_ge(sem("num_copied"), i)
                    if not lsh:
                        after(dve, sem("oh"), i - 1)
                    nc.vector.tensor_tensor(att[:], num[:], g_den[:, 0:N2], ALU.mult).then_inc(sem("tn"), 1)
                    if lsh:
                        dve.wait_ge(sem("tn"), i)
                        nc.vector.scalar_tensor_tensor(h_of(i - 1), att[:], col[:, 2:3], h_of(i - 1),
                                                       ALU.add, ALU.add).then_inc(sem("hnew"), 1)

                def residual(i, m):
                    dve.wait_ge(sem("wo"), i)
                    after(dve, sem("mean2"), i - 1)
                    after(dve, sem("cent2"), i - 1)
                    nc.vector.scalar_tensor_tensor(yy[:], g1[:, 0:N2], col[:, 3:4], xh[(m + 3) % 4][:],
                                                   ALU.add, ALU.add).then_inc(sem("yy"), 1)

                def center2(i):
                    dve.wait_ge(sem("mean2"), i)
                    dve.wait_ge(sem("yy"), i)
                    after(dve, sem("sq2"), i - 1)
                    after(dve, sem("tn2"), i - 1)
                    nc.vector.tensor_tensor(cent2[:], yy[:], g1[:, 0:N2], ALU.subtract).then_inc(sem("cent2"), 1)

                def normal2(i):
                    dve.wait_ge(sem("rbc2"), i)
                    dve.wait_ge(sem("cent2"), i)
                    after(dve, sem("tt"), i - 1)
                    nc.vector.tensor_tensor(nrm2[:], cent2[:], g1[:, 0:N2], ALU.mult).then_inc(sem("tn2"), 1)

                def guess2(nth):
                    guess(g1, var2, vneg2, rstd2, "var2", "vcp2", "rbc2", "seed2", "rs2", nth)

                def head():
                    for b in [parts, *vm, *vr, *ptr]:
                        nc.vector.memset(b[:], 0.0)
                    nc.vector.memset(ptm[0][:], 0.0)
                    if lsh:
                        for b in kb:
                            nc.vector.memset(b[:], 0.0)
                    nc.vector.memset(half3[:], 1.5)
                    nc.vector.memset(ptm[1][:], 0.0).then_inc(sem("zero"), 1)
                    consts(dve)
                    for a in (-2, -1):
                        center(a, g0)
                        guess(g1, var, vneg, rstd, "var", "vcp", "rbc", "seed", "rs", a + 2)
                        normal(a, a, g0)
                    row_max(0, 0, lambda: None)

                def step(i, m, half):
                    have_a, have_v = not is_last(i, 2), not is_last(i, 1)
                    for u in range(UNITS):
                        def last_keys():
                            if u > 0:
                                main_keys(i, u - 1)
                            elif not first(i):
                                main_keys(i - 1, UNITS - 1)
                        if u < 7:
                            row_max(i, u + 1, last_keys)
                        elif have_v:
                            row_max(i + 1, 0, last_keys)
                        else:
                            last_keys()
                        later = not lsh and not first(i)
                        if u == 0 and later and not first(i - 1):
                            guess2(i - 2)
                        if u == 0 and not first(i):
                            denominators(i, (m + 1) % 2)
                            outputs(i)
                        if u == 1 and have_a:
                            center(i, g1)
                        if u == 3 and have_a:
                            guess(g_norm, var, vneg, rstd, "var", "vcp", "rbc", "seed", "rs", i + 2)
                        if u == (4 if lsh else 2) and not first(i):
                            divide(i)
                        if u == 4 and later and not first(i - 1):
                            normal2(i - 1)
                        if u == 5 and later:
                            residual(i, m)
                        if u == 5 and have_a:
                            normal(i, m, g_norm)
                        if u == 6 and later:
                            center2(i)
                pairs(dve, head, step)
                main_keys(PAIRS - 1, UNITS - 1)
                outputs(PAIRS)
                if not lsh:
                    guess2(PAIRS - 2)
                denominators(PAIRS, 1)
                divide(PAIRS)
                if lsh:
                    dve.wait_ge(sem("hnew"), PAIRS)
                else:
                    normal2(PAIRS - 1)
                    residual(PAIRS, PAIRS % 4)
                    center2(PAIRS)
                    guess2(PAIRS - 1)
                    normal2(PAIRS)

            @block.gpsimd
            def _(pool):
                def newton(vn, y, seeded, done, nth):
                    pool.wait_ge(sem(seeded), 3 * nth + 3)
                    k = 0
                    for _ in range(3):
                        for dst, a, b, op in ((nwt, y, y, ALU.mult), (nwt, nwt, vn, ALU.mult),
                                              (nwt, nwt, half3, ALU.add), (y, y, nwt, ALU.mult)):
                            nc.gpsimd.tensor_tensor(dst[:], a[:], b[:], op).then_inc(sem(done), 1)
                            k += 1
                            pool.wait_ge(sem(done), nth * NEWTON_OPS + k)

                def split(i, src, ready, base, k):
                    pool.wait_ge(sem(ready), i + 3)
                    after(pool, sem("store"), 16 * (i + 2))
                    hold(pool, sem("pass"))
                    hi, mid, low = (both(parts[:, base + p, :]) for p in range(3))
                    n_s = (i + 2) * NSIDE * 4 + 4 * k
                    nc.gpsimd.tensor_copy(hi, two(src[:])).then_inc(sem("split"), 1)
                    pool.wait_ge(sem("split"), n_s + 1)
                    nc.gpsimd.tensor_tensor(two(rst[:]), two(src[:]), hi, ALU.subtract).then_inc(sem("split"), 1)
                    pool.wait_ge(sem("split"), n_s + 2)
                    hold(pool, sem("pass"))
                    nc.gpsimd.tensor_copy(mid, two(rst[:])).then_inc(sem("split"), 1)
                    pool.wait_ge(sem("split"), n_s + 3)
                    last = nc.gpsimd.tensor_tensor(low, two(rst[:]), mid, ALU.subtract)
                    last.then_inc(sem("split"), 1)
                    pool.wait_ge(sem("split"), n_s + 4)

                def make_parts(i):
                    split(i, qf, "qf", 0, 0)
                    if lsh:
                        pool.wait_ge(sem("prc"), i + 3)
                        hold(pool, sem("pass"))
                        nc.gpsimd.tensor_scalar(both(parts[:, PARTS, :]), two(prj[:]), 0.0, 0.5,
                                                ALU.is_ge, ALU.subtract).then_inc(sem("parts"), 1)
                    else:
                        split(i, kf, "kf", PARTS, 1)

                def head():
                    consts(pool)
                    for a in (-2, -1):
                        newton(vneg, rstd, "seed", "rs", a + 2)
                        make_parts(a)

                def step(i, m, half):
                    later = not lsh and not first(i)
                    if later and not first(i - 1):
                        newton(vneg2, rstd2, "seed2", "rs2", i - 2)
                    if not is_last(i, 2):
                        newton(vneg, rstd, "seed", "rs", i + 2)
                    if later and not first(i - 1):
                        affine(i - 1)
                    if not is_last(i, 2):
                        make_parts(i)

                def affine(i):
                    pool.wait_ge(sem("tn2"), i)
                    after(pool, sem("out"), 16 * (i - 1))
                    hold(pool, sem("pass"))
                    nc.gpsimd.tensor_scalar(tt[:], nrm2[:], col[:, 4:5], col[:, 5:6], ALU.mult,
                                            ALU.add).then_inc(sem("tt"), 1)

                pairs(pool, head, step)
                if not lsh:
                    newton(vneg2, rstd2, "seed2", "rs2", PAIRS - 2)
                    affine(PAIRS - 1)
                    newton(vneg2, rstd2, "seed2", "rs2", PAIRS - 1)
                    affine(PAIRS)
        n.clear()


def chunks(eng, step):
    for k in range(3):
        step(k, k % 2, k // 2)
    with eng.Fori(0, (NC - 3) // 2) as it:
        for p in range(2):
            step(it * 2 + (p + 3), 1 - p, it + (p + 1))


def route(nc, hT, ident, tT_dram, t_dram, sorted_dram, gate_w, gate_b, prefix_w, logit, dest, best, tile_expert,
          experts_sb, experts_in):
    with ExitStack() as ctx:
        n = Names(nc, ctx, "route")
        sem = n.sem
        gw = n.sb("gw", [128, NE])
        gb = n.sb("gb", [128, NE])
        upper = n.sb("upper", [128, 128])
        ones = n.sb("ones", [128, 128])
        tc = [n.sb(f"tc{p}", [128, CT * 128]) for p in range(2)]
        tok = [n.sb(f"tok{p}", [128, CT, ROW]) for p in range(2)]
        number = n.sb("number", [128, TILES])
        ps_l = [n.ps(f"l{p}", [128, 512]) for p in range(2)]
        ps_t = [n.ps(f"t{p}", [128, 512]) for p in range(2)]
        hot = n.sb("hot", [128, TILES, NE])
        rank = n.sb("rank", [128, TILES, NE])
        count = n.sb("count", [128, TILES, NE])
        cum = n.sb("cum", [128, NE, TILES])
        top = n.sb("top", [128, TILES])
        work = n.sb("work", [128, TILES, NE])
        pick = n.sb("pick", [128, TILES])
        idx_e = n.sb("idx_e", [128, NE])
        tot = n.sb("tot", [128, NE])
        tot_i = n.sb("tot_i", [128, NE], I32)
        tiles = n.sb("tiles", [128, NE])
        ends = n.sb("ends", [128, NE])
        starts = n.sb("starts", [128, NE])
        slot_no = n.sb("slot_no", [1, SLOTS])
        acc = [n.sb(f"acc{p}", [1, SLOTS]) for p in range(2)]

        with nc.Block() as block:
            @block.sync
            def _(sp):
                for dst, src in ((gw, gate_w), (gb, gate_b), (upper, prefix_w)):
                    sp.dma_start(dst[:], src).then_inc(sem("const"), 16)

                def load(k, p):
                    after(sp, sem("turned"), (k - 1) * CT)
                    sp.dma_start(tc[p][:], tT_dram[:, bass.ds(k * (CT * 128), CT * 128)]).then_inc(sem(f"load{p}"), 16)

                def store(k, p):
                    sp.wait_ge(sem("tok"), (k + 1) * CT)
                    sp.dma_start(t_dram[bass.ds(k * (CT * 128), CT * 128), :].rearrange("(c p) e -> p c e", p=128),
                                 tok[p][:, :, 0:E]).then_inc(sem(f"store{p}"), 16)

                load(0, 0)
                for k in range(2):
                    load(k + 1, 1 - k)
                    store(k, k)
                with sp.Fori(0, (NC - 3) // 2) as it:
                    for p in range(2):
                        load(it * 2 + (p + 3), 1 - p)
                        store(it * 2 + (p + 2), p)
                store(NC - 1, 0)
                sp.wait_ge(sem("store0"), 16 * ((NC + 1) // 2))
                sp.wait_ge(sem("store1"), 16 * (NC // 2))

            @block.tensor
            def _(pe):
                pe.wait_ge(sem("const"), 48)

                def chunk(k, p, half):
                    pe.wait_ge(sem(f"load{p}"), 16 * (half + 1))
                    after(pe, sem("logit"), k - 1)
                    for c in range(CT):
                        x = tc[p][:, c * 128:(c + 1) * 128]
                        nc.tensor.matmul(ps_l[p][:, c * NE:(c + 1) * NE], x, gw[:], start=True,
                                         stop=True).then_inc(sem("gate"), 1)
                        after(pe, sem("tok"), k * CT + (c - 1))
                        nc.tensor.transpose(ps_t[(p * CT + c) % 2][:, 0:128], x, ident[:]).then_inc(sem("turned"), 1)
                chunks(pe, chunk)

            @block.vector
            def _(dve):
                nc.vector.memset(ones[:], 1.0)
                dve.wait_ge(sem("const"), 48)

                def chunk(k, p, half):
                    after(dve, sem(f"store{p}"), 16 * half)
                    for c in range(CT):
                        dve.wait_ge(sem("turned"), k * CT + (c + 1))
                        nc.vector.tensor_copy(tok[p][:, c, 0:E], ps_t[(p * CT + c) % 2][:, 0:128]).then_inc(sem("tok"), 1)
                    dve.wait_ge(sem("gate"), (k + 1) * CT)
                    nc.vector.tensor_tensor(logit[:, bass.ds(k * CT, CT), :],
                                            ps_l[p][:, 0:CT * NE].rearrange("p (c e) -> p c e", e=NE),
                                            gb[:, :].rearrange("p (o e) -> p o e", o=1).broadcast_to([128, CT, NE]),
                                            ALU.add).then_inc(sem("logit"), 1)
                chunks(dve, chunk)

        def per_token(x):
            return x.rearrange("p (c o) -> p c o", o=1).broadcast_to([128, TILES, NE])

        def per_expert(x):
            return x.rearrange("p (o e) -> p o e", o=1).broadcast_to([128, TILES, NE])

        with nc.Block() as block:
            @block.gpsimd
            def _(pool):
                nc.gpsimd.iota(idx_e[:], pattern=[[1, NE]], base=-NE, channel_multiplier=0,
                               allow_small_or_imprecise_dtypes=True)
                nc.gpsimd.iota(number[:], pattern=[[128, TILES]], base=DUMP, channel_multiplier=1,
                               allow_small_or_imprecise_dtypes=True)
                nc.gpsimd.iota(slot_no[:], pattern=[[1, SLOTS]], base=0, channel_multiplier=0,
                               allow_small_or_imprecise_dtypes=True).then_inc(sem("iota"), 1)

            @block.scalar
            def _(act):
                act.wait_ge(sem("shifted"), 1)
                nc.scalar.activation(work[:], work[:], ACT.Exp).then_inc(sem("gate_exp"), 1)

            @block.tensor
            def _(pe):
                pe.wait_ge(sem("hot"), 1)
                flat = hot[:, :, :].rearrange("p c e -> p (c e)")
                W = TILES * NE
                for k in range(0, W, 512):
                    w = min(512, W - k)
                    b = k // 512
                    if b:
                        pe.wait_ge(sem("cnt"), b)
                    nc.tensor.matmul(ps_l[0][:, 0:w], upper[:], flat[:, k:k + w], start=True, stop=True)
                    nc.tensor.matmul(ps_l[1][:, 0:w], ones[:], flat[:, k:k + w], start=True,
                                     stop=True).then_inc(sem("ranked"), 1)

            @block.vector
            def _(dve):
                chain = [0]

                def link(ins):
                    chain[0] += 1
                    ins.then_inc(sem("chain"), 1)
                    dve.wait_ge(sem("chain"), chain[0])

                tt_, ts_ = nc.vector.tensor_tensor, nc.vector.tensor_scalar
                link(nc.vector.tensor_reduce(top[:], logit[:], AX.X, ALU.max))
                link(tt_(work[:], logit[:], per_token(top[:]), ALU.subtract))
                dve.wait_ge(sem("iota"), 1)
                link(ts_(hot[:], work[:], 0.0, None, ALU.is_equal))
                link(tt_(hot[:], hot[:], per_expert(idx_e[:]), ALU.mult))
                link(nc.vector.tensor_reduce(pick[:], hot[:], AX.X, ALU.min))
                nc.vector.tensor_copy(rank[:], per_expert(idx_e[:])).then_inc(sem("shifted"), 1)
                dve.wait_ge(sem("shifted"), 1)
                tt_(hot[:], rank[:], per_token(pick[:]), ALU.is_equal).then_inc(sem("hot"), 1)
                dve.wait_ge(sem("gate_exp"), 1)
                link(nc.vector.tensor_reduce(top[:], work[:], AX.X, ALU.add))
                link(nc.vector.reciprocal(best[:], top[:]))
                dve.wait_ge(sem("hot"), 1)
                W = TILES * NE
                rf, cf = (x[:, :, :].rearrange("p c e -> p (c e)") for x in (rank, count))
                for k in range(0, W, 512):
                    w = min(512, W - k)
                    dve.wait_ge(sem("ranked"), k // 512 + 1)
                    nc.vector.tensor_copy(rf[:, k:k + w], ps_l[0][:, 0:w])
                    last = nc.vector.tensor_copy(cf[:, k:k + w], ps_l[1][:, 0:w]).then_inc(sem("cnt"), 1)
                dve.wait_ge(sem("cnt"), (W + 511) // 512)
                for e in range(NE):
                    c = count[:, :, e]
                    last = nc.vector.tensor_tensor_scan(cum[:, e, :], c, c, 0.0, ALU.add, ALU.bypass)
                link(last)
                cv = cum[:, :, :].rearrange("p e c -> p c e")
                link(tt_(work[:], cv, count[:], ALU.subtract))
                link(tt_(rank[:], rank[:], work[:], ALU.add))
                link(ts_(tot_i[:], cum[:, :, TILES - 1], 127.0, None, ALU.add))
                link(ts_(tot_i[:], tot_i[:], 7, None, ALU.arith_shift_right))
                link(nc.vector.tensor_copy(tiles[:], tot_i[:]))
                link(nc.vector.tensor_tensor_scan(ends[:], tiles[:], tiles[:], 0.0, ALU.add, ALU.bypass))
                link(tt_(starts[:], ends[:], tiles[:], ALU.subtract))
                link(ts_(starts[:], starts[:], 128.0, None, ALU.mult))
                link(tt_(rank[:], rank[:], per_expert(starts[:]), ALU.add))
                link(tt_(rank[:], rank[:], hot[:], ALU.mult))
                link(nc.vector.tensor_reduce(pick[:], rank[:], AX.X, ALU.add))
                link(nc.vector.tensor_copy(dest[:], pick[:]))
                link(ts_(acc[0][:], slot_no[:], ends[0:1, 0:1], None, ALU.is_ge))
                for e in range(1, NE - 1):
                    link(nc.vector.scalar_tensor_tensor(acc[e % 2][:], slot_no[:], ends[0:1, e:e + 1],
                                                        acc[(e + 1) % 2][:], ALU.is_ge, ALU.add))
                link(nc.vector.tensor_copy(tile_expert[:], acc[(NE - 2) % 2][:]))

        with nc.Block() as block:
            @block.scalar
            def _(act):
                for dst, src in zip(experts_sb, experts_in):
                    act.dma_start(dst[:], src).then_inc(sem("weights"), 16)
                act.wait_ge(sem("weights"), 16 * len(experts_sb))

            @block.sync
            def _(sp):
                def load(k, p, half):
                    after(sp, sem(f"scattered{p}"), 16 * CT * half)
                    sp.dma_start(tok[p][:, :, 0:E], t_dram[bass.ds(k * (CT * 128), CT * 128), :].rearrange(
                        "(c p) e -> p c e", p=128)).then_inc(sem(f"back{p}"), 16)
                chunks(sp, load)

            @block.vector
            def _(dve):
                def numbers(k, p, half):
                    after(dve, sem(f"scattered{p}"), 16 * CT * half)
                    nc.vector.tensor_copy(tok[p][:, :, E], number[:, bass.ds(k * CT, CT)]).then_inc(sem("numbered"), 1)
                chunks(dve, numbers)

            @block.gpsimd
            def _(pool):
                ids = [n.sb(f"ids{p}", [128, CT], U32) for p in range(2)]

                def chunk(k, p, half):
                    after(pool, sem(f"scattered{p}"), 16 * CT * half)
                    hold(pool, sem("pass"))
                    nc.gpsimd.tensor_copy(ids[p][:], dest[:, bass.ds(k * CT, CT)]).then_inc(sem("ids"), 1)
                    pool.wait_ge(sem("ids"), k + 1)
                    pool.wait_ge(sem(f"back{p}"), 16 * (half + 1))
                    pool.wait_ge(sem("numbered"), k + 1)
                    hold(pool, sem("pass"))
                    for c in range(CT):
                        nc.gpsimd.indirect_dma_start(
                            sorted_dram[:, :], bass.IndirectOffsetOnAxis(ap=ids[p][:, c:c + 1], axis=0),
                            tok[p][:, c, :], None).then_inc(sem(f"scattered{p}"), 16)
                chunks(pool, chunk)
                pool.wait_ge(sem("scattered0"), 16 * CT * ((NC + 1) // 2))
                pool.wait_ge(sem("scattered1"), 16 * CT * (NC // 2))


def tiles(eng, step):
    for s in range(BODY):
        step(s, s, s // 4)
    with eng.Fori(0, SLOTS // BODY - 2) as it:
        for c in range(BODY):
            step(it * BODY + (c + BODY), c, it * (BODY // 4) + (c + BODY) // 4)
    for s in range(SLOTS - BODY, SLOTS):
        step(s, s % BODY, s // 4)


def experts(nc, ident, sorted_dram, expert_rows, weights, tile_expert):
    FC = FF // 128
    with ExitStack() as ctx:
        n = Names(nc, ctx, "moe")
        sem = n.sem
        w1_sb, b1_sb, w2_sb, b2_sb = weights
        xs = [n.sb(f"xs{p}", [128, ROW]) for p in range(4)]
        dump = n.sb("dump", [128, BODY])
        ids = [n.sb(f"ids{p}", [128, 1], U32) for p in range(BODY)]
        xt = [n.sb(f"xt{p}", [128, E]) for p in range(2)]
        pre = [n.sb(f"pre{p}", [128, FF]) for p in range(2)]
        hid = [n.sb(f"hid{p}", [128, FF]) for p in range(2)]
        hidT = [n.sb(f"hidT{p}", [128, FF]) for p in range(2)]
        ys = [n.sb(f"ys{p}", [128, E]) for p in range(4)]
        ps_x, ps_h, ps_t, ps_y = ([n.ps(f"{x}{p}", [128, 512]) for p in range(2)] for x in "xhty")

        def has(s):
            return not isinstance(s, int) or 0 <= s < SLOTS

        with nc.Block() as block:
            @block.sync
            def _(sp):
                def load(s, k):
                    after(sp, sem("ids"), s - 3)
                    sp.dma_start(xs[k][:], sorted_dram[bass.ds(s * 128, 128), :]).then_inc(sem(f"load{k}"), 16)

                def step(s, c, quarter):
                    k = c % 4
                    if has(s + 4):
                        load(s + 4, k)
                for s in range(4):
                    load(s, s)
                tiles(sp, step)

            @block.gpsimd
            def _(pool):
                nc.gpsimd.iota(dump[:], pattern=[[128, BODY]], base=0, channel_multiplier=1,
                               allow_small_or_imprecise_dtypes=True).then_inc(sem("dump"), 1)

                def step(s, c, quarter):
                    pool.wait_ge(sem("ys"), s + 1)
                    hold(pool, sem("pass"))
                    nc.gpsimd.indirect_dma_start(
                        expert_rows[:, :], bass.IndirectOffsetOnAxis(ap=ids[c][:], axis=0),
                        ys[c % 4][:], None).then_inc(sem(f"store{c % 4}"), 16)
                tiles(pool, step)
                for k in range(4):
                    pool.wait_ge(sem(f"store{k}"), 16 * (SLOTS // 4))

            def expert_of(eng, loaded, s, c):
                if c not in loaded:
                    loaded[c] = eng.value_load(tile_expert[0:1, bass.ds(s, 1)], min_val=0, max_val=NE - 1)
                return loaded[c]

            @block.tensor
            def _(pe):
                loaded = {}

                def turn_rows(s, k, quarter):
                    pe.wait_ge(sem(f"load{k}"), 16 * (quarter + 1))
                    after(pe, sem("xt"), s - 1)
                    nc.tensor.transpose(ps_x[k % 2][:, 0:128], xs[k][:, 0:E], ident[:]).then_inc(sem("xT"), 1)

                def first(s, p, c):
                    e = expert_of(pe, loaded, s, c)
                    pe.wait_ge(sem("xt"), s + 1)
                    after(pe, sem("pre"), s - 1)
                    nc.tensor.matmul(ps_h[p][:], xt[p][:], w1_sb[:, bass.ds(e * FF, FF)], start=True,
                                     stop=True).then_inc(sem("h"), 1)

                def turn_hidden(s, p):
                    pe.wait_ge(sem("gelu"), s + 1)
                    after(pe, sem("hT"), s - 1)
                    for f in range(FC):
                        last = nc.tensor.transpose(ps_t[p][:, f * 128:(f + 1) * 128], hid[p][:, f * 128:(f + 1) * 128],
                                                   ident[:])
                    last.then_inc(sem("ht"), 1)

                def second(s, p, c):
                    e = expert_of(pe, loaded, s, c)
                    pe.wait_ge(sem("hT"), s + 1)
                    after(pe, sem("ys"), s - 1)
                    for f in range(FC):
                        last = nc.tensor.matmul(ps_y[p][:, 0:E], hidT[p][:, f * 128:(f + 1) * 128],
                                                w2_sb[:, bass.ds(e * (FC * E) + f * E, E)], start=f == 0,
                                                stop=f == FC - 1)
                    last.then_inc(sem("y"), 1)

                def step(s, c, quarter):
                    k = c % 4
                    if c == 0:
                        loaded.clear()
                    if has(s + 2):
                        first(s + 2, k % 2, c + 2)
                    turn_hidden(s, k % 2)
                    if has(s + 3):
                        turn_rows(s + 3, (k + 3) % 4, quarter + (k + 3) // 4)
                    if has(s - 1):
                        second(s - 1, (k + 1) % 2, c - 1)
                turn_rows(0, 0, 0)
                turn_rows(1, 1, 0)
                first(0, 0, 0)
                turn_rows(2, 2, 0)
                first(1, 1, 1)
                tiles(pe, step)
                second(SLOTS - 1, 1, BODY - 1)

            @block.scalar
            def _(act):
                def gelu(s, p):
                    act.wait_ge(sem("pre"), s + 1)
                    after(act, sem("ht"), s - 1)
                    nc.scalar.activation(hid[p][:], pre[p][:], ACT.Gelu_apprx_tanh).then_inc(sem("gelu"), 1)

                def step(s, c, quarter):
                    k = c % 4
                    if has(s + 1):
                        gelu(s + 1, (k + 1) % 2)
                    act.wait_ge(sem("ht"), s + 1)
                    after(act, sem("y"), s - 1)
                    nc.scalar.activation(hidT[k % 2][:], ps_t[k % 2][:], ACT.Copy).then_inc(sem("hT"), 1)
                gelu(0, 0)
                tiles(act, step)

            @block.vector
            def _(dve):
                loaded = {}

                def rows(s, c, quarter):
                    p, k = c % 2, c % 4
                    dve.wait_ge(sem("xT"), s + 1)
                    after(dve, sem(f"store{k}"), 16 * (quarter - 1))
                    c %= BODY
                    nc.vector.tensor_tensor(ids[c][:], xs[k][:, E:ROW], dump[:, c:c + 1], ALU.max).then_inc(sem("ids"), 1)
                    after(dve, sem("h"), s - 1)
                    nc.vector.tensor_copy(xt[p][:], ps_x[p][:, 0:128]).then_inc(sem("xt"), 1)

                def hidden(s, p, c):
                    e = expert_of(dve, loaded, s, c)
                    dve.wait_ge(sem("h"), s + 1)
                    after(dve, sem("gelu"), s - 1)
                    nc.vector.tensor_tensor(pre[p][:], ps_h[p][:], b1_sb[:, bass.ds(e * FF, FF)],
                                            ALU.add).then_inc(sem("pre"), 1)

                def result(s, k, quarter, c):
                    e = expert_of(dve, loaded, s, c)
                    dve.wait_ge(sem("y"), s + 1)
                    after(dve, sem(f"store{k}"), 16 * quarter)
                    nc.vector.tensor_tensor(ys[k][:], ps_y[k % 2][:, 0:E], b2_sb[:, bass.ds(e * E, E)],
                                            ALU.add).then_inc(sem("ys"), 1)

                def step(s, c, quarter):
                    k = c % 4
                    if c == 0:
                        loaded.clear()
                    if has(s + 2):
                        hidden(s + 2, k % 2, c + 2)
                    if has(s + 3):
                        rows(s + 3, c + 3, quarter + (k + 3) // 4)
                    if has(s - 1):
                        result(s - 1, (k + 3) % 4, quarter + (k + 3) // 4 - 1, c - 1)
                dve.wait_ge(sem("dump"), 1)
                rows(0, 0, 0)
                rows(1, 1, 0)
                hidden(0, 0, 0)
                rows(2, 2, 0)
                hidden(1, 1, 1)
                tiles(dve, step)
                result(SLOTS - 1, 3, SLOTS // 4 - 1, BODY - 1)


def combine(nc, hT, ident, expert_rows, best, out):
    with ExitStack() as ctx:
        n = Names(nc, ctx, "comb")
        sem = n.sem
        rows = [n.sb(f"rows{p}", [128, CT, E]) for p in range(2)]
        hc = [n.sb(f"hc{p}", [128, CT * 128]) for p in range(2)]
        fin = [n.sb(f"fin{p}", [128, CT, E]) for p in range(2)]
        pr = [n.sb(f"pr{p}", [128, CT]) for p in range(2)]
        ps = [n.ps(f"ps{p}", [128, 512]) for p in range(2)]
        with nc.Block() as block:
            @block.sync
            def _(sp):
                def chunk(k, p, half):
                    after(sp, sem("fin"), CT * (k - 1))
                    sp.dma_start(rows[p][:], expert_rows[bass.ds(k * (CT * 128) + DUMP, CT * 128), :].rearrange(
                        "(c p) e -> p c e", p=128)).then_inc(sem(f"rows{p}"), 16)
                chunks(sp, chunk)

            @block.scalar
            def _(act):
                def chunk(k, p, half):
                    after(act, sem("turned"), CT * (k - 1))
                    nc.scalar.activation(hc[p][:], hT[:, bass.ds(k * (CT * 128), CT * 128)], ACT.Copy
                                         ).then_inc(sem("hc"), 1)
                chunks(act, chunk)

            @block.tensor
            def _(pe):
                def chunk(k, p, half):
                    pe.wait_ge(sem("hc"), k + 1)
                    for c in range(CT):
                        after(pe, sem("fin"), k * CT + (c - 1))
                        nc.tensor.transpose(ps[(p * CT + c) % 2][:, 0:128], hc[p][:, c * 128:(c + 1) * 128],
                                            ident[:]).then_inc(sem("turned"), 1)
                chunks(pe, chunk)

            @block.vector
            def _(dve):
                def chunk(k, p, half):
                    after(dve, sem(f"store{p}"), 16 * half)
                    dve.wait_ge(sem(f"rows{p}"), 16 * (half + 1))
                    nc.vector.tensor_copy(pr[p][:], best[:, bass.ds(k * CT, CT)]).then_inc(sem("pr"), 1)
                    dve.wait_ge(sem("pr"), k + 1)
                    for c in range(CT):
                        dve.wait_ge(sem("turned"), k * CT + (c + 1))
                        nc.vector.scalar_tensor_tensor(fin[p][:, c, :], rows[p][:, c, :], pr[p][:, c:c + 1],
                                                       ps[(p * CT + c) % 2][:, 0:128], ALU.mult,
                                                       ALU.add).then_inc(sem("fin"), 1)
                chunks(dve, chunk)

            @block.gpsimd
            def _(pool):
                def chunk(k, p, half):
                    pool.wait_ge(sem("fin"), CT * (k + 1))
                    hold(pool, sem("pass"))
                    pool.dma_start(out[bass.ds(k * (CT * 128), CT * 128), :].rearrange("(c p) e -> p c e", p=128),
                                   fin[p][:]).then_inc(sem(f"store{p}"), 16)
                chunks(pool, chunk)
                pool.wait_ge(sem("store0"), 16 * ((NC + 1) // 2))
                pool.wait_ge(sem("store1"), 16 * (NC // 2))


def tower(nc, a, out):
    scratch = nc.dram_tensor("qk_parts", [2, 2 * PARTS, 128, 2 * TP], BF16).ap()
    rows_dram = nc.dram_tensor("tok_rows", [2, T, E], F32).ap()
    tT_dram = nc.dram_tensor("t_features", [E, NT], F32).ap()
    t_dram = nc.dram_tensor("t_tokens", [NT, E], F32).ap()
    sorted_dram = nc.dram_tensor("t_sorted", [SLOTS * 128, ROW], F32).ap()
    expert_rows = nc.dram_tensor("expert_rows", [DUMP + NT, E], F32).ap()
    with ExitStack() as ctx:
        hT = ctx.enter_context(nc.sbuf_tensor("hT", [128, NT], F32))
        ident = ctx.enter_context(nc.sbuf_tensor("ident", [128, 128], F32))
        ld = ctx.enter_context(nc.semaphore("ident_loaded"))
        with nc.Block() as block:
            @block.sync
            def _(sp):
                sp.dma_start(ident[:], a["ident"]).then_inc(ld, 16)
                sp.wait_ge(ld, 16)
        patch_tokens(nc, hT, ident, a["ximg"], a["xblk"], a["xpatch"], a["gam"], a["bet"], a["wtok"], a["btok"],
                     rows_dram, sorted_dram)
        mats = (a["sel_num"], a["rest_ident"], a["rest_head"], a["mean_w"])
        attention(nc, hT, ident, mats, (a["lsh_wq"], a["lsh_wv"], a["lsh_hyp"]), a["lsh_cols"], scratch, True, None)
        attention(nc, hT, ident, mats, (a["att_wq"], a["att_wv"], a["att_wk"], a["att_wo"]), a["att_cols"], scratch,
                  False, tT_dram)
        with ExitStack() as tail:
            dest = tail.enter_context(nc.sbuf_tensor("dest", [128, TILES], U32))
            best = tail.enter_context(nc.sbuf_tensor("best", [128, TILES], F32))
            tile_expert = tail.enter_context(nc.sbuf_tensor("tile_expert", [1, SLOTS], I32))
            logit = tail.enter_context(nc.sbuf_tensor("logit", [128, TILES, NE], F32))
            experts_sb = [tail.enter_context(nc.sbuf_tensor(f"experts_{x}", [128, NE * w], F32))
                          for x, w in (("w1", FF), ("b1", FF), ("w2", FF), ("b2", E))]
            route(nc, hT, ident, tT_dram, t_dram, sorted_dram, a["gate_w"], a["gate_b"], a["prefix_w"], logit, dest,
                  best, tile_expert, experts_sb, (a["w1"], a["b1"], a["w2"], a["b2"]))
            experts(nc, ident, sorted_dram, expert_rows, experts_sb, tile_expert)
            combine(nc, hT, ident, expert_rows, best, out)


def constants():
    num = np.zeros((128, 2, E), np.float32)
    for h in range(H):
        g, s = h // 4, h % 4
        for d in range(D):
            num[32 * s + d, g, h * D + d] = 1.0
    rest_ident, rest_head = np.zeros((128, REM), np.float32), np.zeros((128, 2, H // 2, 2, D), np.float32)
    for x in range(2):
        rest_ident[64 * x:64 * x + REM] = np.eye(REM)
        rest_head[64 * x:64 * x + 64, :, :, x] = 1.0
    return {"sel_num": num, "rest_ident": rest_ident, "rest_head": rest_head.reshape(128, 2 * E), "mean_w": np.full((128, 128), 1.0 / E, np.float32),
            "ident": np.eye(128, dtype=np.float32), "prefix_w": np.triu(np.ones((128, 128), np.float32), 1)}


def layout(v):
    x = v["x"]
    wide = np.pad(x, ((0, 0), (0, 0), (HP, HP), (HP, HP)))

    def blocks(z, k):
        return z.reshape(IMG, CH, k, PATCH, k, PATCH).transpose(1, 3, 5, 2, 4, 0).reshape(E, k, k, IMG)

    def patches(z):
        return z.reshape(SRC, CH, GRID, PATCH, GRID, PATCH).transpose(1, 3, 5, 0, 2, 4).reshape(E, SRC, T)

    def columns(*arrays):
        c = np.zeros((E, 8), np.float32)
        for k, z in enumerate(arrays):
            c[:, k] = z
        return c
    hp = v["L0_attn_hyperplanes"]
    hyp, hyp_b = np.zeros((E, E), np.float32), np.zeros(E, np.float32)
    for h in range(H):
        hyp[h * D:(h + 1) * D, h * D:h * D + hp.shape[1]] = hp[:D]
        hyp_b[h * D:h * D + hp.shape[1]] = hp[D]
    W1, W2 = v["L0_ffn_W1"], v["L0_ffn_W2"]
    return {
        "ximg": x.reshape(IMG, 8, -1), "xblk": blocks(wide, NBLK), "xpatch": blocks(x, GRID),
        "gam": patches(v["L0_tok_gamma"]), "bet": patches(v["L0_tok_beta"]),
        "wtok": v["L0_tok_W"].reshape(E, SRC, CH, PATCH, PATCH).transpose(2, 3, 4, 1, 0).reshape(E, SRC, E),
        "btok": v["L0_tok_b"].reshape(1, E),
        "lsh_wq": v["L0_attn_Wq"], "lsh_wv": v["L0_attn_Wv"], "lsh_hyp": hyp,
        "lsh_cols": columns(v["L0_attn_bq"], hyp_b, v["L0_attn_bv"]),
        "att_wq": v["L0_ffn_Wq"], "att_wv": v["L0_ffn_Wv"], "att_wk": v["L0_ffn_Wk"], "att_wo": v["L0_ffn_Wo"],
        "att_cols": columns(*(v["L0_ffn_" + k] for k in ("bq", "bk", "bv", "bo", "ln1_g", "ln1_b"))),
        "gate_w": v["L0_ffn_gate_W"], "gate_b": np.broadcast_to(v["L0_ffn_gate_b"], (128, NE)),
        "w1": W1.transpose(1, 0, 2).reshape(E, NE * FF),
        "b1": np.broadcast_to(v["L0_ffn_b1"].reshape(1, -1), (128, NE * FF)),
        "w2": W2.reshape(NE, FF // 128, 128, E).transpose(2, 0, 1, 3).reshape(128, -1),
        "b2": np.broadcast_to(v["L0_ffn_b2"].reshape(1, -1), (128, NE * E)),
        **constants(),
    }


def kernel(**inputs):
    from concourse import bacc
    from concourse.bass_utils import run_bass_kernel_spmd

    nc = bacc.Bacc("TRN2", target_bir_lowering=False, num_devices=1)
    arrays = {k: np.ascontiguousarray(z) for k, z in layout({k: np.asarray(z) for k, z in inputs.items()}).items()}
    args = {k: nc.dram_tensor("in_" + k, z.shape, mybir.dt.from_np(z.dtype), kind="ExternalInput").ap()
            for k, z in arrays.items()}
    out = nc.dram_tensor("out", (NT, E), F32, kind="ExternalOutput").ap()
    tower(nc, args, out)
    result = run_bass_kernel_spmd(nc, [{"in_" + k: z for k, z in arrays.items()}], core_ids=[0])
    return result.results[0]["out"].reshape(IMG, T, E)
```
